# Optimizing a Trainium2 kernel written in Bass

```python
import numpy as np
import jax
import jax.numpy as jnp

def _softmax(x, axis=-1):
    return jax.nn.softmax(x, axis=axis)

def _gelu(x):
    return jax.nn.gelu(x, approximate=True)

def _silu(x):
    return jax.nn.silu(x)

def _sigmoid(x):
    return jax.nn.sigmoid(x)

def _layernorm(x, axis=-1, eps=1e-05):
    m = jnp.mean(x, axis=axis, keepdims=True)
    v = jnp.var(x, axis=axis, keepdims=True)
    return (x - m) / jnp.sqrt(v + eps)

def _scatter_add(tgt, idx, src, axis=0):
    return tgt.at[idx].add(src)

def _segment_sum(src, seg, n):
    return jax.ops.segment_sum(src, seg, n)
kernel_name = 'mk_lm_tower_d2_tok_ids768_r4_14fdee'

def setup_inputs(seed: int=0):
    np.random.seed(seed)
    _w = jnp.asarray

    def _rec_inputs():
        import jax
        import jax.numpy as jnp
        _rk = jax.random.key(seed)
        x = jax.random.randint(jax.random.fold_in(_rk, 1), (16, 128), 0, 30521, jnp.int32)
        itok_BS_2_399970 = jax.random.randint(jax.random.fold_in(_rk, 21), (16, 128), 2, 399971, jnp.int32)
        return (x, itok_BS_2_399970)
    x, itok_BS_2_399970 = _rec_inputs()

    def _L0_tok_setup():
        import jax, jax.numpy as jnp
        import numpy as np
        LN_EPS = 1e-12
        key = jax.random.key(seed)
        ks = jax.random.split(key, 8)
        B, S, H, D = (32, 128, 192, 75)
        V_BERT, V_W, P = (30522, 400001, 128)
        inp = {'sents': jax.random.randint(ks[0], (B, S), 0, V_BERT), 'wids': jax.random.randint(ks[1], (B, S), 0, V_W), 'word_emb': jax.random.normal(ks[2], (V_BERT, H), jnp.float32) * 0.02, 'pos_emb': jax.random.normal(ks[3], (P, H), jnp.float32) * 0.02, 'type_emb': jax.random.normal(ks[4], (2, H), jnp.float32) * 0.02, 'ln_gamma': jnp.ones((H,), jnp.float32), 'ln_beta': jnp.zeros((H,), jnp.float32), 'wvec': jax.random.normal(ks[5], (V_W, D), jnp.float32) * 0.1, 'g2b_w': jax.random.normal(ks[6], (H, D), jnp.float32) * 0.02, 'g2b_b': jnp.zeros((H,), jnp.float32), 'gate_w': jax.random.normal(ks[7], (1, H), jnp.float32) * 0.02, 'gate_b': jnp.zeros((1,), jnp.float32)}
        return inp
    _L0_tok_all = _L0_tok_setup()
    _L0_tok_in = {k: v for k, v in _L0_tok_all.items() if k in ('word_emb', 'pos_emb', 'type_emb', 'ln_gamma', 'ln_beta', 'wvec', 'g2b_w', 'g2b_b', 'gate_w', 'gate_b')}
    del _L0_tok_all

    def _L0_attn_setup():
        import jax, jax.numpy as jnp
        import numpy as np

        def _rotate_half(x):
            a, b = jnp.split(x, 2, axis=-1)
            return jnp.concatenate([-b, a], axis=-1)

        def _rope_tables(L, d, dtype):
            inv = 1.0 / 10000.0 ** (jnp.arange(0, d, 2, dtype=jnp.float32) / d)
            ang = jnp.arange(L, dtype=jnp.float32)[:, None] * inv[None, :]
            cos = jnp.repeat(jnp.cos(ang), 2, axis=-1)[None, :, None, :].astype(dtype)
            sin = jnp.repeat(jnp.sin(ang), 2, axis=-1)[None, :, None, :].astype(dtype)
            return (cos, sin)

        def _forward(X, Wq, Wk, Wv, Wu, Wg, Wo, prior_mu, prior_log_tau):
            B, L, D = X.shape
            h = prior_mu.shape[2]
            d = D // h
            eps = 1e-12
            q = (X @ Wq.T).reshape(B, L, h, d)
            k = (X @ Wk.T).reshape(B, L, h, d)
            v = (X @ Wv.T).reshape(B, L, h, d)
            u = (X @ Wu.T).reshape(B, L, h, d)
            gate = (X @ Wg.T).reshape(B, L, h, 3)
            t = jnp.arange(1, L + 1, dtype=X.dtype).reshape(1, L, 1, 1)
            log_tau = jnp.exp(jnp.clip(prior_log_tau, -50.0, 30.0))
            u_sum = jnp.cumsum(u, axis=1)
            bar_u = (log_tau * prior_mu + u_sum) / (log_tau + t)
            s_i = -jnp.sum(u * bar_u, axis=-1, keepdims=True) / np.float32(np.sqrt(d))
            cos, sin = _rope_tables(L, d, X.dtype)
            q = q * cos + _rotate_half(q) * sin
            k = k * cos + _rotate_half(k) * sin
            q = q / jnp.maximum(jnp.linalg.norm(q, axis=-1, keepdims=True), eps)
            k = k / jnp.maximum(jnp.linalg.norm(k, axis=-1, keepdims=True), eps)
            s_max = jax.lax.stop_gradient(jnp.max(s_i, axis=1, keepdims=True))
            exp_s = jnp.exp(s_i - s_max)
            E_t = jnp.cumsum(exp_s, axis=1)
            P_t = jnp.cumsum(s_i, axis=1)
            kv = jnp.einsum('blhd,blhe->blhde', k, v)
            F_t = jnp.cumsum(exp_s[..., None] * kv, axis=1)
            G_t = jnp.cumsum(s_i[..., None] * kv, axis=1)
            H_t = jnp.cumsum(kv, axis=1)
            sig1 = jax.nn.sigmoid(gate[..., 0:1])
            sigh = jax.nn.sigmoid(gate[..., 1:2])
            alpha = sigh / (E_t + eps)
            beta = (sig1 - sigh) / t
            gamma = -((beta * P_t + sigh) / t)
            M = alpha[..., None] * F_t + beta[..., None] * G_t + gamma[..., None] * H_t
            out = jnp.einsum('blhd,blhde->blhe', q, M)
            mu = jnp.mean(out, axis=-1, keepdims=True)
            var = jnp.mean(jnp.square(out - mu), axis=-1, keepdims=True)
            out = (out - mu) / jnp.sqrt(var + 1e-05)
            return out.reshape(B, L, D) @ Wo.T
        key = jax.random.key(seed)
        ks = jax.random.split(key, 7)
        B, L, D, h = (1, 256, 192, 12)
        d = D // h
        s = 0.02
        return {'X': jax.random.normal(ks[0], (B, L, D), jnp.float32), 'Wq': jax.random.normal(ks[1], (D, D), jnp.float32) * s, 'Wk': jax.random.normal(ks[2], (D, D), jnp.float32) * s, 'Wv': jax.random.normal(ks[3], (D, D), jnp.float32) * s, 'Wu': jax.random.normal(ks[4], (D, D), jnp.float32) * s, 'Wg': jax.random.normal(ks[5], (3 * h, D), jnp.float32) * s, 'Wo': jax.random.normal(ks[6], (D, D), jnp.float32) * s, 'prior_mu': jnp.zeros((1, 1, h, d), jnp.float32), 'prior_log_tau': jnp.zeros((1, 1, h, 1), jnp.float32)}
    _L0_attn_all = _L0_attn_setup()
    _L0_attn_in = {k: v for k, v in _L0_attn_all.items() if k in ('Wq', 'Wk', 'Wv', 'Wu', 'Wg', 'Wo', 'prior_mu', 'prior_log_tau')}
    del _L0_attn_all

    def _L0_ffn_setup():
        import jax, jax.numpy as jnp
        import numpy as np
        B, L, D, H, F = (4, 512, 192, 12, 768)
        ROUTE_FRAC = 0.15
        LN_EPS = 1e-05

        def _ln(x, g, b):
            m = jnp.mean(x, axis=-1, keepdims=True)
            v = jnp.mean((x - m) ** 2, axis=-1, keepdims=True)
            return (x - m) * jax.lax.rsqrt(v + LN_EPS) * g + b
        key = jax.random.key(seed)
        ks = jax.random.split(key, 20)
        s = 0.02
        return {'hidden_states': jax.random.normal(ks[0], (B, L, D), dtype=jnp.float32), 'g1': jnp.ones((D,), jnp.float32), 'b1': jnp.zeros((D,), jnp.float32), 'g2': jnp.ones((D,), jnp.float32), 'b2': jnp.zeros((D,), jnp.float32), 'Wr': jax.random.normal(ks[1], (D,), jnp.float32) * s, 'br': jnp.zeros((), jnp.float32), 'Wq': jax.random.normal(ks[2], (D, D), jnp.float32) * s, 'bq': jnp.zeros((D,), jnp.float32), 'Wk': jax.random.normal(ks[3], (D, D), jnp.float32) * s, 'bk': jnp.zeros((D,), jnp.float32), 'Wv': jax.random.normal(ks[4], (D, D), jnp.float32) * s, 'bv': jnp.zeros((D,), jnp.float32), 'Wo': jax.random.normal(ks[5], (D, D), jnp.float32) * s, 'bo': jnp.zeros((D,), jnp.float32), 'Wm': jax.random.normal(ks[6], (D, D), jnp.float32) * s, 'bm': jnp.zeros((D,), jnp.float32), 'W1': jax.random.normal(ks[7], (D, F), jnp.float32) * s, 'bf1': jnp.zeros((F,), jnp.float32), 'W2': jax.random.normal(ks[8], (F, D), jnp.float32) * s, 'bf2': jnp.zeros((D,), jnp.float32)}
    _L0_ffn_all = _L0_ffn_setup()
    _L0_ffn_in = {k: v for k, v in _L0_ffn_all.items() if k in ('g1', 'b1', 'g2', 'b2', 'Wr', 'br', 'Wq', 'bq', 'Wk', 'bk', 'Wv', 'bv', 'Wo', 'bo', 'Wm', 'bm', 'W1', 'bf1', 'W2', 'bf2')}
    del _L0_ffn_all

    def _L1_attn_setup():
        import jax, jax.numpy as jnp
        import numpy as np
        NUM_HEADS = 12

        def _split_heads(x, N, S):
            return x.reshape(N, S, NUM_HEADS, -1).transpose(0, 2, 1, 3)
        key = jax.random.key(seed)
        ks = jax.random.split(key, 12)
        N, S, E, R, RM = (8, 256, 192, 96, 64)
        hd = E // NUM_HEADS
        s = 0.02
        return {'hidden_states': jax.random.normal(ks[0], (N, S, E), dtype=jnp.float32), 'U_Q': jax.random.normal(ks[1], (R, E), dtype=jnp.float32) * s, 'V_Q': jax.random.normal(ks[2], (E, R), dtype=jnp.float32) * s, 'U_K': jax.random.normal(ks[3], (R, E), dtype=jnp.float32) * s, 'V_K': jax.random.normal(ks[4], (E, R), dtype=jnp.float32) * s, 'U_V': jax.random.normal(ks[5], (R, E), dtype=jnp.float32) * s, 'V_V': jax.random.normal(ks[6], (E, R), dtype=jnp.float32) * s, 'bias_q': jax.random.normal(ks[7], (E,), dtype=jnp.float32) * s, 'bias_k': jax.random.normal(ks[8], (E,), dtype=jnp.float32) * s, 'bias_v': jax.random.normal(ks[9], (E,), dtype=jnp.float32) * s, 'M_U': jax.random.normal(ks[10], (hd, RM), dtype=jnp.float32) * 0.1, 'M_V': jax.random.normal(ks[11], (RM, hd), dtype=jnp.float32) * 0.1}
    _L1_attn_all = _L1_attn_setup()
    _L1_attn_in = {k: v for k, v in _L1_attn_all.items() if k in ('U_Q', 'V_Q', 'U_K', 'V_K', 'U_V', 'V_V', 'bias_q', 'bias_k', 'bias_v', 'M_U', 'M_V')}
    del _L1_attn_all

    def _L1_ffn_setup():
        import jax, jax.numpy as jnp
        import numpy as np
        TOP_K = 2
        key = jax.random.key(seed)
        ks = jax.random.split(key, 5)
        B, S, D, H, E = (1, 512, 192, 768, 8)
        x = jax.random.normal(ks[0], (B, S, D), dtype=jnp.float32)
        gate_w = jax.random.normal(ks[1], (E, D), dtype=jnp.float32) * 0.02
        w1 = jax.random.normal(ks[2], (E, D, H), dtype=jnp.float32) * 0.02
        b1 = jnp.zeros((E, H), dtype=jnp.float32)
        w2 = jax.random.normal(ks[3], (E, H, D), dtype=jnp.float32) * 0.02
        b2 = jnp.zeros((E, D), dtype=jnp.float32)
        return {'x': x, 'gate_w': gate_w, 'w1': w1, 'b1': b1, 'w2': w2, 'b2': b2}
    _L1_ffn_all = _L1_ffn_setup()
    _L1_ffn_in = {k: v for k, v in _L1_ffn_all.items() if k in ('gate_w', 'w1', 'b1', 'w2', 'b2')}
    del _L1_ffn_all
    return {'x': x, 'itok_BS_2_399970': itok_BS_2_399970, 'L0_tok_word_emb': _L0_tok_in['word_emb'], 'L0_tok_pos_emb': _L0_tok_in['pos_emb'], 'L0_tok_type_emb': _L0_tok_in['type_emb'], 'L0_tok_ln_gamma': _L0_tok_in['ln_gamma'], 'L0_tok_ln_beta': _L0_tok_in['ln_beta'], 'L0_tok_wvec': _L0_tok_in['wvec'], 'L0_tok_g2b_w': _L0_tok_in['g2b_w'], 'L0_tok_g2b_b': _L0_tok_in['g2b_b'], 'L0_tok_gate_w': _L0_tok_in['gate_w'], 'L0_tok_gate_b': _L0_tok_in['gate_b'], 'L0_attn_Wq': _L0_attn_in['Wq'], 'L0_attn_Wk': _L0_attn_in['Wk'], 'L0_attn_Wv': _L0_attn_in['Wv'], 'L0_attn_Wu': _L0_attn_in['Wu'], 'L0_attn_Wg': _L0_attn_in['Wg'], 'L0_attn_Wo': _L0_attn_in['Wo'], 'L0_attn_prior_mu': _L0_attn_in['prior_mu'], 'L0_attn_prior_log_tau': _L0_attn_in['prior_log_tau'], 'L0_ffn_g1': _L0_ffn_in['g1'], 'L0_ffn_b1': _L0_ffn_in['b1'], 'L0_ffn_g2': _L0_ffn_in['g2'], 'L0_ffn_b2': _L0_ffn_in['b2'], 'L0_ffn_Wr': _L0_ffn_in['Wr'], 'L0_ffn_br': _L0_ffn_in['br'], 'L0_ffn_Wq': _L0_ffn_in['Wq'], 'L0_ffn_bq': _L0_ffn_in['bq'], 'L0_ffn_Wk': _L0_ffn_in['Wk'], 'L0_ffn_bk': _L0_ffn_in['bk'], 'L0_ffn_Wv': _L0_ffn_in['Wv'], 'L0_ffn_bv': _L0_ffn_in['bv'], 'L0_ffn_Wo': _L0_ffn_in['Wo'], 'L0_ffn_bo': _L0_ffn_in['bo'], 'L0_ffn_Wm': _L0_ffn_in['Wm'], 'L0_ffn_bm': _L0_ffn_in['bm'], 'L0_ffn_W1': _L0_ffn_in['W1'], 'L0_ffn_bf1': _L0_ffn_in['bf1'], 'L0_ffn_W2': _L0_ffn_in['W2'], 'L0_ffn_bf2': _L0_ffn_in['bf2'], 'L1_attn_U_Q': _L1_attn_in['U_Q'], 'L1_attn_V_Q': _L1_attn_in['V_Q'], 'L1_attn_U_K': _L1_attn_in['U_K'], 'L1_attn_V_K': _L1_attn_in['V_K'], 'L1_attn_U_V': _L1_attn_in['U_V'], 'L1_attn_V_V': _L1_attn_in['V_V'], 'L1_attn_bias_q': _L1_attn_in['bias_q'], 'L1_attn_bias_k': _L1_attn_in['bias_k'], 'L1_attn_bias_v': _L1_attn_in['bias_v'], 'L1_attn_M_U': _L1_attn_in['M_U'], 'L1_attn_M_V': _L1_attn_in['M_V'], 'L1_ffn_gate_w': _L1_ffn_in['gate_w'], 'L1_ffn_w1': _L1_ffn_in['w1'], 'L1_ffn_b1': _L1_ffn_in['b1'], 'L1_ffn_w2': _L1_ffn_in['w2'], 'L1_ffn_b2': _L1_ffn_in['b2']}

def reference(x, itok_BS_2_399970, L0_tok_word_emb, L0_tok_pos_emb, L0_tok_type_emb, L0_tok_ln_gamma, L0_tok_ln_beta, L0_tok_wvec, L0_tok_g2b_w, L0_tok_g2b_b, L0_tok_gate_w, L0_tok_gate_b, L0_attn_Wq, L0_attn_Wk, L0_attn_Wv, L0_attn_Wu, L0_attn_Wg, L0_attn_Wo, L0_attn_prior_mu, L0_attn_prior_log_tau, L0_ffn_g1, L0_ffn_b1, L0_ffn_g2, L0_ffn_b2, L0_ffn_Wr, L0_ffn_br, L0_ffn_Wq, L0_ffn_bq, L0_ffn_Wk, L0_ffn_bk, L0_ffn_Wv, L0_ffn_bv, L0_ffn_Wo, L0_ffn_bo, L0_ffn_Wm, L0_ffn_bm, L0_ffn_W1, L0_ffn_bf1, L0_ffn_W2, L0_ffn_bf2, L1_attn_U_Q, L1_attn_V_Q, L1_attn_U_K, L1_attn_V_K, L1_attn_U_V, L1_attn_V_V, L1_attn_bias_q, L1_attn_bias_k, L1_attn_bias_v, L1_attn_M_U, L1_attn_M_V, L1_ffn_gate_w, L1_ffn_w1, L1_ffn_b1, L1_ffn_w2, L1_ffn_b2):
    import jax
    import jax.numpy as jnp

    def _L0_tok_ref(sents, wids, word_emb, pos_emb, type_emb, ln_gamma, ln_beta, wvec, g2b_w, g2b_b, gate_w, gate_b):
        import jax, jax.numpy as jnp
        import numpy as np
        LN_EPS = 1e-12
        S = sents.shape[1]
        e = word_emb[sents] + pos_emb[:S][None, :, :] + type_emb[0][None, None, :]
        mu = jnp.mean(e, axis=-1, keepdims=True)
        var = jnp.mean(jnp.square(e - mu), axis=-1, keepdims=True)
        b = (e - mu) * jax.lax.rsqrt(var + LN_EPS) * ln_gamma + ln_beta
        a = jax.nn.sigmoid(jnp.einsum('bsh,oh->bso', b, gate_w) + gate_b)
        g = jnp.einsum('bsd,hd->bsh', wvec[wids], g2b_w) + g2b_b
        return (1.0 - a) * b + a * g

    def _L0_attn_ref(X, Wq, Wk, Wv, Wu, Wg, Wo, prior_mu, prior_log_tau):
        import jax, jax.numpy as jnp
        import numpy as np

        def _rotate_half(x):
            a, b = jnp.split(x, 2, axis=-1)
            return jnp.concatenate([-b, a], axis=-1)

        def _rope_tables(L, d, dtype):
            inv = 1.0 / 10000.0 ** (jnp.arange(0, d, 2, dtype=jnp.float32) / d)
            ang = jnp.arange(L, dtype=jnp.float32)[:, None] * inv[None, :]
            cos = jnp.repeat(jnp.cos(ang), 2, axis=-1)[None, :, None, :].astype(dtype)
            sin = jnp.repeat(jnp.sin(ang), 2, axis=-1)[None, :, None, :].astype(dtype)
            return (cos, sin)

        def _forward(X, Wq, Wk, Wv, Wu, Wg, Wo, prior_mu, prior_log_tau):
            B, L, D = X.shape
            h = prior_mu.shape[2]
            d = D // h
            eps = 1e-12
            q = (X @ Wq.T).reshape(B, L, h, d)
            k = (X @ Wk.T).reshape(B, L, h, d)
            v = (X @ Wv.T).reshape(B, L, h, d)
            u = (X @ Wu.T).reshape(B, L, h, d)
            gate = (X @ Wg.T).reshape(B, L, h, 3)
            t = jnp.arange(1, L + 1, dtype=X.dtype).reshape(1, L, 1, 1)
            log_tau = jnp.exp(jnp.clip(prior_log_tau, -50.0, 30.0))
            u_sum = jnp.cumsum(u, axis=1)
            bar_u = (log_tau * prior_mu + u_sum) / (log_tau + t)
            s_i = -jnp.sum(u * bar_u, axis=-1, keepdims=True) / np.float32(np.sqrt(d))
            cos, sin = _rope_tables(L, d, X.dtype)
            q = q * cos + _rotate_half(q) * sin
            k = k * cos + _rotate_half(k) * sin
            q = q / jnp.maximum(jnp.linalg.norm(q, axis=-1, keepdims=True), eps)
            k = k / jnp.maximum(jnp.linalg.norm(k, axis=-1, keepdims=True), eps)
            s_max = jax.lax.stop_gradient(jnp.max(s_i, axis=1, keepdims=True))
            exp_s = jnp.exp(s_i - s_max)
            E_t = jnp.cumsum(exp_s, axis=1)
            P_t = jnp.cumsum(s_i, axis=1)
            kv = jnp.einsum('blhd,blhe->blhde', k, v)
            F_t = jnp.cumsum(exp_s[..., None] * kv, axis=1)
            G_t = jnp.cumsum(s_i[..., None] * kv, axis=1)
            H_t = jnp.cumsum(kv, axis=1)
            sig1 = jax.nn.sigmoid(gate[..., 0:1])
            sigh = jax.nn.sigmoid(gate[..., 1:2])
            alpha = sigh / (E_t + eps)
            beta = (sig1 - sigh) / t
            gamma = -((beta * P_t + sigh) / t)
            M = alpha[..., None] * F_t + beta[..., None] * G_t + gamma[..., None] * H_t
            out = jnp.einsum('blhd,blhde->blhe', q, M)
            mu = jnp.mean(out, axis=-1, keepdims=True)
            var = jnp.mean(jnp.square(out - mu), axis=-1, keepdims=True)
            out = (out - mu) / jnp.sqrt(var + 1e-05)
            return out.reshape(B, L, D) @ Wo.T
        return _forward(X, Wq, Wk, Wv, Wu, Wg, Wo, prior_mu, prior_log_tau)

    def _L0_ffn_ref(hidden_states, g1, b1, g2, b2, Wr, br, Wq, bq, Wk, bk, Wv, bv, Wo, bo, Wm, bm, W1, bf1, W2, bf2):
        import jax, jax.numpy as jnp
        import numpy as np
        B, L, D, H, F = (4, 512, 192, 12, 768)
        ROUTE_FRAC = 0.15
        LN_EPS = 1e-05

        def _ln(x, g, b):
            m = jnp.mean(x, axis=-1, keepdims=True)
            v = jnp.mean((x - m) ** 2, axis=-1, keepdims=True)
            return (x - m) * jax.lax.rsqrt(v + LN_EPS) * g + b
        b, l, d = hidden_states.shape
        dh = d // H
        normed = _ln(hidden_states, g1, b1)
        scores = jax.nn.sigmoid(jnp.einsum('bld,d->bl', normed, Wr) + br)
        k = max(1, int(round(ROUTE_FRAC * l)))
        _, idx = jax.lax.top_k(-scores, k)
        attn_mask = jnp.zeros((b, l), bool).at[jnp.arange(b)[:, None], idx].set(True)
        q = (normed @ Wq + bq).reshape(b, l, H, dh)
        kk = (normed @ Wk + bk).reshape(b, l, H, dh)
        v = (normed @ Wv + bv).reshape(b, l, H, dh)
        logits = jnp.einsum('blhd,bmhd->bhlm', q, kk) / jnp.sqrt(jnp.float32(dh))
        probs = jax.nn.softmax(logits, axis=-1)
        ctx = jnp.einsum('bhlm,bmhd->blhd', probs, v).reshape(b, l, d)
        attn_out = ctx @ Wo + bo
        w = scores / (jnp.sum(scores, axis=1, keepdims=True) + 1e-06)
        pooled = jnp.einsum('bl,bld->bd', w, normed)
        mix_out = (normed + scores[..., None] * pooled[:, None, :]) @ Wm + bm
        merged = jnp.where(attn_mask[..., None], attn_out, mix_out)
        h = hidden_states + merged
        n2 = _ln(h, g2, b2)
        ffn = jax.nn.gelu(n2 @ W1 + bf1, approximate=False) @ W2 + bf2
        return h + ffn

    def _L1_attn_ref(hidden_states, U_Q, V_Q, U_K, V_K, U_V, V_V, bias_q, bias_k, bias_v, M_U, M_V):
        import jax, jax.numpy as jnp
        import numpy as np
        NUM_HEADS = 12

        def _split_heads(x, N, S):
            return x.reshape(N, S, NUM_HEADS, -1).transpose(0, 2, 1, 3)
        N, S, E = hidden_states.shape
        hd = E // NUM_HEADS
        scale = 1.0 / jnp.sqrt(jnp.asarray(hd, hidden_states.dtype))
        q = hidden_states @ V_Q @ U_Q + bias_q
        k = hidden_states @ V_K @ U_K + bias_k
        v = hidden_states @ V_V @ U_V + bias_v
        q = _split_heads(q, N, S)
        k = _split_heads(k, N, S)
        v = _split_heads(v, N, S)
        qm = jnp.einsum('bhsd,dr->bhsr', q, M_U)
        km = jnp.einsum('rd,bhtd->bhrt', M_V, k)
        attn = jnp.einsum('bhsr,bhrt->bhst', qm, km) * scale
        attn = jax.nn.softmax(attn, axis=-1)
        out = jnp.einsum('bhst,bhtd->bhsd', attn, v)
        out = out.transpose(0, 2, 1, 3).reshape(N, S, E)
        return out

    def _L1_ffn_ref(x, gate_w, w1, b1, w2, b2):
        import jax, jax.numpy as jnp
        import numpy as np
        TOP_K = 2
        B, S, D = x.shape
        E, _, H = w1.shape
        T = B * S
        K = TOP_K
        xf = x.reshape(T, D)
        logits = xf @ gate_w.T
        probs = jax.nn.softmax(logits, axis=-1)
        top_w, top_i = jax.lax.top_k(probs, K)
        top_w = top_w / (jnp.sum(top_w, axis=-1, keepdims=True) + 1e-09)
        flat_e = top_i.reshape(-1)
        flat_w = top_w.reshape(-1)
        tok_idx = jnp.repeat(jnp.arange(T), K)
        order = jnp.argsort(flat_e)
        se = flat_e[order]
        pt = tok_idx[order]
        pw = flat_w[order]
        counts = jax.ops.segment_sum(jnp.ones(T * K, jnp.int32), se, num_segments=E)
        starts = jnp.concatenate([jnp.zeros((1,), jnp.int32), jnp.cumsum(counts)[:-1]])
        pos = jnp.arange(T * K) - starts[se]
        cap = T * K
        padded = jnp.zeros((E, cap, D), x.dtype).at[se, pos].set(xf[pt])
        hidden = jax.nn.gelu(jnp.einsum('ecd,edh->ech', padded, w1) + b1[:, None, :], approximate=False)
        out = jnp.einsum('ech,ehd->ecd', hidden, w2) + b2[:, None, :]
        expert_out = out[se, pos] * pw[:, None]
        final = jnp.zeros((T, D), x.dtype).at[pt].add(expert_out)
        return final.reshape(B, S, D)
    h = _L0_tok_ref(x, itok_BS_2_399970, L0_tok_word_emb, L0_tok_pos_emb, L0_tok_type_emb, L0_tok_ln_gamma, L0_tok_ln_beta, L0_tok_wvec, L0_tok_g2b_w, L0_tok_g2b_b, L0_tok_gate_w, L0_tok_gate_b)
    h = h + _L0_attn_ref(_layernorm(h, axis=-1), L0_attn_Wq, L0_attn_Wk, L0_attn_Wv, L0_attn_Wu, L0_attn_Wg, L0_attn_Wo, L0_attn_prior_mu, L0_attn_prior_log_tau)
    h = h + _L0_ffn_ref(_layernorm(h, axis=-1), L0_ffn_g1, L0_ffn_b1, L0_ffn_g2, L0_ffn_b2, L0_ffn_Wr, L0_ffn_br, L0_ffn_Wq, L0_ffn_bq, L0_ffn_Wk, L0_ffn_bk, L0_ffn_Wv, L0_ffn_bv, L0_ffn_Wo, L0_ffn_bo, L0_ffn_Wm, L0_ffn_bm, L0_ffn_W1, L0_ffn_bf1, L0_ffn_W2, L0_ffn_bf2)
    h = h + _L1_attn_ref(_layernorm(h, axis=-1), L1_attn_U_Q, L1_attn_V_Q, L1_attn_U_K, L1_attn_V_K, L1_attn_U_V, L1_attn_V_V, L1_attn_bias_q, L1_attn_bias_k, L1_attn_bias_v, L1_attn_M_U, L1_attn_M_V)
    h = h + _L1_ffn_ref(_layernorm(h, axis=-1), L1_ffn_gate_w, L1_ffn_w1, L1_ffn_b1, L1_ffn_w2, L1_ffn_b2)
    return h

_drawn_inputs = setup_inputs


def setup_inputs(seed=0):
    import zlib

    import numpy as np

    out = dict(_drawn_inputs(seed))
    spreads = {'L0_tok_ln_gamma': (1.0, 0.2),
     'L0_tok_ln_beta': (0.0, 0.1),
     'L0_tok_g2b_b': (0.0, 0.1),
     'L0_attn_prior_mu': (0.0, 0.66),
     'L0_attn_prior_log_tau': (0.0, 0.8),
     'L0_ffn_g1': (1.0, 0.2),
     'L0_ffn_b1': (0.0, 0.308),
     'L0_ffn_g2': (1.0, 0.6),
     'L0_ffn_b2': (0.0, 0.8),
     'L0_ffn_bq': (0.0, 0.8),
     'L0_ffn_bk': (0.0, 2.0),
     'L0_ffn_bv': (0.0, 0.8),
     'L0_ffn_bo': (0.0, 0.306),
     'L0_ffn_bm': (0.0, 0.1),
     'L0_ffn_bf1': (0.0, 0.387),
     'L0_ffn_bf2': (0.0, 0.1),
     'L1_ffn_b1': (0.0, 0.588),
     'L1_ffn_b2': (0.0, 0.1)}
    factors = {'L0_tok_wvec': 2.819,
     'L0_attn_Wg': 3.901,
     'L0_ffn_Wq': 8.0,
     'L0_ffn_Wk': 8.0,
     'L0_ffn_Wv': 4.597,
     'L0_ffn_Wo': 3.997,
     'L1_attn_U_Q': 8.0,
     'L1_attn_V_Q': 8.0,
     'L1_attn_U_K': 8.0,
     'L1_attn_V_K': 8.0,
     'L1_attn_bias_q': 129.073,
     'L1_attn_bias_k': 200.0,
     'L1_attn_bias_v': 4.095,
     'L1_attn_M_U': 8.0,
     'L1_attn_M_V': 8.0}
    for name, (base, spread) in spreads.items():
        noise = np.random.default_rng([zlib.crc32(name.encode()), seed]).standard_normal(out[name].shape)
        drawn = base * np.exp(spread * noise) if base else spread * noise
        out[name] = jnp.asarray(drawn.astype(out[name].dtype))
    for name, factor in factors.items():
        out[name] = (out[name] * factor).astype(out[name].dtype)
    return out
```

```python
import numpy as np
import concourse.bass as bass
from concourse import mybir
from contextlib import ExitStack

F32 = mybir.dt.float32
I32 = mybir.dt.int32
U32 = mybir.dt.uint32
ALU = mybir.AluOpType
ACT = mybir.ActivationFunctionType
AX = mybir.AxisListType

B, S, D = 16, 128, 192
G = 4
NG = B // G
C, CW = 2, 96
H, HD = 12, 16
HC = H // C
WV = 75
F = 768
FJ = F // 128
KSEL = max(1, int(round(0.15 * S)))
NE = 8
XR = D + 2
MT = 39
LATE = 2
NOBODY = 1 << 20

_C = {}
_n = 0
for _name, _w in (("ident", 128), ("le", 128), ("lt", 128), ("gt", 128), ("ones", 128), ("iota", KSEL),
                  ("iota8", NE), ("hm", HC), ("cos", HD), ("sin", HD), ("rt", 1), ("t", 1), ("slot", 39)):
    _C[_name] = (_n, _n + _w)
    _n += _w
NC_COLS = _n

RSTD = ("ln0", "ln1", "norm2", "hln", "ln2", "ln3", "ln4", "ln5", "ln6")


def rstd_of(name):
    return RSTD.index(name) + 1


PER = dict(
    gathered=128, rstd=9, idx_cur=1, emb_sum=4, ln0=15, tok_scaled=4, tok_b=4, gate_dot=4, gate_exp=1, gate_a=2, wvT=4,
    gT=1, g_ready=4, g_diff=4, h_tok=4,
    ln1=15, x1T=4, xT=2, proj=4, rope=16, vug=4, qk_sq=4, norm2=5, qkT=4, q_evac=4, k_evac=4, usum=4, sdot=12,
    sT=1, smax=2, s_exp=1, eback=1, es_ready=1, cum=1, gexp=1, coef=16, vk=4, A0=8, A_masked=8, pv=4, o3=8,
    o_sum=8, hln=21, onT=4, oT=2, wo=4, h_attn=4,
    ln2=15, ln3=15, zdot=4, zexp=1, score=2, n3T=4, nT=2, dg=4, bc=4, ssum=1, wsel=4, rank=16, nmask=1,
    sel=4, selT=2, pool_fix=4, qT=1, q_bias=2, qbd=2, kT=1, kT_evac=2, v2p=4, v2=2, pselT_p=4, pselT=1, lg=4, nmax=8,
    pexp=8, pnorm=12, pT_p=4, pT=2, ctx=4, ctx_m=4, ctxT=4, asel_p=4, asel=2, attn=4, mixT=8, mix=4, hin=8, hb=8,
    ln4=15, n4T=4, n2T=2, mT_one=1, up=6, gelu=6, down=4, h_ffn=4,
    ln5=15, x5T=4, x5T_e=2, qk1=6, qk1_e=6, v1p=4, v1=2, lg1=8, nm1=12, e1=8, e1T=8, e1T_e=4, e1T_ev=4, pv1=4, h_l1=12,
    ln6=15, x6T=4, x6T_e=2, gate=1, smx=5, gexp2=1, topk=10, topw=10, keep=3, gatesT_p=4, gatesT=1, b2p=4, out_row=4, base_out=64,
)


def build(nc, a, out):
    with ExitStack() as ctx:
        def sb(name, shape, dt=F32):
            return ctx.enter_context(nc.sbuf_tensor(name, shape, dt))

        def sem(name):
            return ctx.enter_context(nc.semaphore(name))

        s = {name: sem(name) for name in PER}
        ld_const, ld_tok, ld_l0, ld_ffn, ld_l1, ld_w1, ld_w2 = (
            sem(n) for n in ("ld_const", "ld_tok", "ld_l0", "ld_ffn", "ld_l1", "ld_w1", "ld_w2"))
        fills, setup_v, setup_p, setup_a, slots_empty = (
            sem(n) for n in ("fills", "setup_v", "setup_p", "setup_a", "slots_empty"))
        route, route_p, scattered, second_w, carried = (
            sem(n) for n in ("route", "route_p", "scattered", "second_w", "carried"))
        slot_in = [sem(f"slot_in{u}") for u in range(2)]
        m_xT, m_xTe, m_up, m_gelu, m_hT, m_hTe, m_down, m_y, m_add = (
            sem(n) for n in ("m_xT", "m_xTe", "m_up", "m_gelu", "m_hT", "m_hTe", "m_down", "m_y", "m_add"))

        slots = nc.dram_tensor("slots", [MT * 128, XR], F32, kind="Internal").ap()

        cst = sb("cst", [128, NC_COLS])

        def con(name, p=128):
            lo, hi = _C[name]
            return cst[0:p, lo:hi]

        ident = con("ident")
        idx_all = sb("idx_all", [128, 2, B + G], I32)
        idx_cur = sb("idx_cur", [128, 2, G], I32)
        tok_no = sb("tok_no", [128, B], I32)
        pos_type = sb("pos_type", [128, D])
        rows = sb("rows", [128, 5, D])
        gammar, betar, gatewr, wrr, bf2r = (rows[:, k, :] for k in range(5))
        cols = sb("cols", [CW, 6, C])
        g1c, b1c, g2c, b2c, bqc, bkc = (cols[:, k, :] for k in range(6))
        bf1c = sb("bf1c", [128, FJ])
        sc = sb("sc", [128, 8])
        w_g2b = sb("w_g2b", [97, D])
        w_l0 = sb("w_l0", [CW, C, 4 * D + 3 * H])
        w_l0o = sb("w_l0o", [CW, C, D])
        rtau = sb("rtau", [128, H])
        taumu = sb("taumu", [1, D])
        w_fq = sb("w_fq", [CW, C, D])
        w_fk = sb("w_fk", [CW, C, D])
        w_fv = sb("w_fv", [97, C, D])
        w_fm = sb("w_fm", [97, C, D])
        w_1q = sb("w_1q", [97, C, H, 32])
        w_1k = sb("w_1k", [97, C, H, 32])
        w_1v = sb("w_1v", [97, C, H, HD + 1])
        w_gate = sb("w_gate", [CW, C, NE])
        w_b2 = sb("w_b2", [NE, D])
        arena_e = sb("arena_e", [128, NE * C * F])
        w_e1 = arena_e[0:97, :].rearrange("p (e c n) -> p e c n", e=NE, c=C)
        arena_e7 = arena_e[:, (NE - LATE) * C * F:]
        w_up = arena_e7[0:CW, 0:C * F].rearrange("p (c n) -> p c n", c=C)
        w_down = arena_e7[:, C * F:C * F + FJ * D].rearrange("p (j n) -> p j n", j=FJ)
        w_fo = arena_e7[0:97, C * F + FJ * D:2 * C * F].rearrange("p (c n) -> p c n", c=C)
        arena_w = sb("arena_w", [128, NE * FJ * D])
        w_e2 = arena_w[:, :].rearrange("p (e j n) -> p e j n", e=NE, j=FJ)

        at = [0]

        def part(buf, at, shape, p=128):
            n = int(np.prod(shape))
            lo = at[0]
            at[0] += n
            flat = buf[0:p, lo:lo + n]
            if len(shape) == 1:
                return flat
            names = "abcd"[:len(shape)]
            return flat.rearrange(f"p ({' '.join(names)}) -> p {' '.join(names)}",
                                  **{names[k]: shape[k] for k in range(1, len(shape))})

        emb = part(arena_w, at, [G, D])
        wvg = part(arena_w, at, [G, WV])
        btok = part(arena_w, at, [G, D])
        vug_at = at[0]
        vug = part(arena_w, at, [G, 420])
        sq = part(arena_w, at, [G, 24, HD])
        over = [vug_at]
        qbd = part(arena_w, over, [C, G, HC * KSEL], CW)
        ctxm = part(arena_w, over, [C, G, HC * KSEL], CW)
        aselb = part(arena_w, over, [G, D], KSEL)
        pselT = part(arena_w, over, [G, 128], KSEL)
        assert over[0] <= at[0]
        e1_at = [at[0]]
        rq = part(arena_w, at, [G, 24, 32])
        e1 = part(arena_w, e1_at, [2, H, 128])
        dg = part(arena_w, at, [G, 128])
        assert at[0] <= NE * FJ * D

        qk_T = sb("qk_T", [128, 2 * G * 3 * 128])
        qkT = qk_T[:, :].rearrange("p (w b j t) -> p w b j t", w=2, b=G, j=3)
        q1k1 = qk_T[:, :].rearrange("p (w j t) -> p w j t", w=2, j=3)
        big = sb("big", [128, 2 * H * 128])
        am = big[:, :].rearrange("p (u i j t) -> p u i j t", u=2, i=4, j=3)
        hid = big[:, :].rearrange("p (j t) -> p j t", j=FJ)
        eT = big[:, :].rearrange("p (u h t) -> p u h t", u=2, h=H)
        arena_b = sb("arena_b", [128, 5000])
        bt = [0]
        vk = part(arena_b, bt, [G, H, 48])
        o3 = part(arena_b, bt, [2, H, 48])
        osum = part(arena_b, bt, [G, D])
        onrm = part(arena_b, bt, [G, D])
        assert bt[0] <= 5000
        ct = [0]
        mT = part(arena_b, ct, [C, G * 128], 97)
        k2T = part(arena_b, ct, [C, G * 128], CW)
        v2 = part(arena_b, ct, [G, D])
        pr = part(arena_b, ct, [G, C, 128], HC * KSEL)
        pT = part(arena_b, ct, [C, G, HC * KSEL])
        assert ct[0] <= 5000
        dt_ = [0]
        v1 = part(arena_b, dt_, [G, H * (HD + 1)])
        att = part(arena_b, dt_, [G, D])

        h = sb("h", [128, G, D])
        x = sb("x", [128, G, D])
        xn = sb("xn", [128, G, D])
        hb = sb("hb", [128, G, D])
        xT = sb("xT", [97, C, G * 128])
        nT = sb("nT", [97, C, G * 128])
        gT = sb("gT", [97, G, 128])
        st = sb("st", [128, G, 6])
        mv = sb("mv", [128, 6, G])
        rs = sb("rs", [128, 2, G])
        minus_half = sb("minus_half", [128, G * 24])
        spare = sb("spare", [128, 1])
        ga = sb("ga", [128, 3, G])
        nrm = sb("nrm", [128, G, 24])
        es = sb("es", [128, 2, G, H])
        smx = sb("smx", [G * H, 1])
        eTs = sb("eTs", [G * H, 128])
        eg = sb("eg", [128, G, H, 2])
        cf = sb("cf", [128, 4, G, H])
        cq = sb("cq", [128, G, H, 3])
        ck = sb("ck", [128, G, H, 3])
        hl = sb("hl", [128, 4, G, H])
        zz = sb("zz", [128, 4, G])
        pw = sb("pw", [128, G, KSEL + 1])
        rk = sb("rk", [128, 3, G])
        nmask = sb("nmask", [128, G])
        junk = hb
        sT = sb("selT", [CW, C, G, KSEL + 1])
        poolT = sb("poolT", [CW, C, G])
        ptmp = sb("ptmp", [CW, C, G])
        nx = sb("nx", [HC * KSEL, 3, G, C])
        ctxT = sb("ctxT", [97, C, G, KSEL])
        nm1 = sb("nm1", [128, G, H])
        r1 = sb("r1", [128, G, H])
        gl = sb("gl", [128, 5, G, NE])
        g1s = sb("g1s", [128, 4, G])
        m8 = sb("m8", [128, G, 8])
        i8 = sb("i8", [128, G, 8], U32)
        i8f = sb("i8f", [128, G, 2])
        gatT = sb("gatT", [NE, G, 128])
        qTs = sb("qTs", [CW, C, G, KSEL])
        tw = sb("tw", [128, G, 2])
        ohg = sb("ohg", [128, 2, G, NE])
        x_all = sb("x_all", [128, B, XR])
        w12 = sb("w12", [128, B, 2])
        oh = sb("oh", [128, 2, B, NE])

        PS = [ctx.enter_context(nc.psum_tensor(f"ps{k}", [128, 2, 512], F32)) for k in range(4)]
        PA, PB, PC, PD = PS


        mu_mv = part(big, [0], [2, 64], 64)
        su = [0]
        u_fold = part(arena_b, su, [3, H, 97], HD)
        v_fold = qk_T[0:97, 0:3 * C * 97].rearrange("p (w c m) -> p w c m", w=3, c=C)
        um = part(qk_T, [3 * C * 97], [3, D], 97)
        mqk = part(qk_T, [3 * C * 97 + 3 * D], [HD], HD)
        rowtmp = part(qk_T, [3 * C * 97 + 3 * D + HD], [2, D])
        typer = part(qk_T, [3 * C * 97 + 5 * D + HD], [D])
        tau = sb("tau", [128, 3, H])
        mu_row = sb("mu_row", [1, D])
        empty = x_all[:, B - 1, :]

        rt_at = [0]
        ohs = part(arena_b, rt_at, [B, NE])
        tot = part(arena_b, rt_at, [B, NE])
        before = part(arena_b, rt_at, [B, NE])
        pos = part(arena_b, rt_at, [B, NE])
        posk = part(arena_b, rt_at, [2, B, NE])
        posf = part(arena_b, rt_at, [2, B])
        cnt = part(arena_b, rt_at, [4, NE])
        owner = part(arena_b, rt_at, [MT, NE])
        ownf = part(arena_b, rt_at, [MT])
        pos_i = sb("pos_i", [128, 2, B], I32)
        cnt_i = sb("cnt_i", [128, 2, NE], I32)
        own_i = sb("own_i", [128, MT], I32)

        m_at = [0]
        xs = part(qk_T, m_at, [2, XR])
        ym = part(qk_T, m_at, [2, D])
        b_at = [0]
        hm_ = part(big, b_at, [2, F])
        hTm = part(big, b_at, [2, FJ, 128])

        block = ctx.enter_context(nc.Block())

        def psl(pair, b, n):
            return pair[:, b // 2, (b % 2) * n:(b % 2) * n + n]

        def part_of(pair, p, b, c, n=128):
            lo = ((b % 2) * C + c) * n
            return pair[0:p, b // 2, lo:lo + n]

        def half_of(pair, p, hf, n=128):
            return pair[0:p, hf, 0:2 * C * n].rearrange("p (b c t) -> p b c t", b=2, c=C)

        def chunks(t, hf):
            return t[0:CW, :, hf * 256:hf * 256 + 256].rearrange("p c (b t) -> p b c t", b=2)

        def half(b):
            return b // 2 * 2 + 2

        def tok(b):
            return slice(b * 128, b * 128 + 128)

        def bc(ap, axis, n):
            ap = ap.unsqueeze(axis)
            shape = list(ap.shape)
            shape[axis] = n
            return ap.to_broadcast(shape)

        KC = (97, 96)

        V_G2B, V_EMPTY, V_TAU = 1, 3, 15
        V_MQK, V_UM, V_FOLDED = 21, 24, 30
        V_SETUP = 34
        R_OHS, R_DONE = 1, 44

        @block.sync
        def _(sp):
            def load(dst, src, sem):
                sp.dma_start(dst, src).then_inc(sem, 16)
            load(cst[:, :], a["consts"], ld_const)
            load(idx_all[:, :, 0:B], a["ids"], ld_const)
            load(tok_no[:, :], a["tok_no"], ld_const)
            load(pos_type[:, :], a["pos"][0:S, :], ld_tok)
            load(typer, a["type"][0:1, :].partition_broadcast(128), ld_tok)
            for k, n in enumerate(("gamma", "beta", "gate_w", "Wr", "bf2")):
                load(rows[:, k, :], a[n].partition_broadcast(128), ld_tok)
            load(rowtmp[:, 0, :], a["g1"].partition_broadcast(128), ld_tok)
            load(rowtmp[:, 1, :], a["b1"].partition_broadcast(128), ld_tok)
            load(sc[:, 0:1], a["gate_b"].partition_broadcast(128), ld_tok)
            load(sc[:, 1:2], a["br"].partition_broadcast(128), ld_tok)
            sp.wait_ge(setup_v, V_G2B)
            load(w_g2b[0:WV, :], a["g2b_w"], ld_tok)
            load(w_g2b[96:97, :], a["g2b_b"], ld_tok)
            lo = 0
            for n in ("Wq", "Wk", "Wv", "Wu", "Wg"):
                w = a[n].rearrange("(c p) n -> p c n", c=C)
                load(w_l0[:, :, lo:lo + w.shape[2]], w, ld_l0)
                lo += w.shape[2]
            load(w_l0o[:, :, :], a["Wo"].rearrange("(c p) n -> p c n", c=C), ld_l0)
            load(tau[:, 0, :], a["log_tau"].partition_broadcast(128), ld_l0)
            load(mu_row[:, :], a["mu"], ld_l0)
            load(mu_mv[0:64, 0, 0:HD], a["M_UT"], ld_l1)
            load(mu_mv[0:64, 1, 0:HD], a["M_V"], ld_l1)
            load(u_fold, a["U_fold"], ld_l1)
            load(v_fold, a["V_fold"], ld_l1)
            load(w_gate[:, :, :], a["gate"].rearrange("(c p) n -> p c n", c=C), ld_l1)
            load(w_b2[:, :], a["b2"], ld_l1)
            load(cols[:, :, :], a["cols"], ld_ffn)
            load(bf1c[:, :], a["bf1"], ld_ffn)
            for dst, n in ((w_fq, "fWq"), (w_fk, "fWk"), (w_fv, "fWv"), (w_fo, "fWo"), (w_fm, "fWm"), (w_up, "W1")):
                load(dst[0:CW, :, :], a[n].rearrange("(c p) n -> p c n", c=C), ld_ffn)
            for dst, n in ((w_fv, "bv"), (w_fo, "bo"), (w_fm, "bm")):
                load(dst[96:97, 0, :], a[n], ld_ffn)
            load(w_down[:, :, :], a["W2"].rearrange("(j p) n -> p j n", j=FJ), ld_ffn)
            sp.wait_ge(setup_v, V_EMPTY)
            sp.dma_start(slots.rearrange("(n p) c -> p n c", p=128), bc(empty, 1, MT)).then_inc(slots_empty, 16)
            def load_w1(lo, hi):
                for e in range(lo, hi):
                    load(w_e1[0:CW, e, :, :], a["w1"][e].rearrange("(c p) n -> p c n", c=C), ld_w1)
                load(w_e1[96:97, lo:hi, 0, :], a["eb1"][lo:hi].unsqueeze(0), ld_w1)

            load_w1(0, NE - LATE)
            with sp.Fori(0, NG) as g:
                for b in range(G):
                    sp.wait_ge(s["out_row"], g * PER["out_row"] + b + 1)
                    sp.dma_start(out[bass.ds(g * G + b, 1)].rearrange("a p n -> (a p) n"), xn[:, b, :])\
                        .then_inc(s["base_out"], 16)
            sp.wait_ge(s["keep"], NG * PER["keep"])
            load_w1(NE - LATE, NE)
            sp.wait_ge(s["gathered"], (NG + 1) * PER["gathered"])
            for e in range(NE):
                load(w_e2[:, e, :, :], a["w2"][e].rearrange("(j p) n -> p j n", j=FJ), ld_w2)
            sp.wait_ge(scattered, 16 * 2 * B)

            def slot_load(tile, u):
                sp.dma_start(xs[:, u, :], slots[bass.ds(tile * 128, 128), :]).then_inc(slot_in[u], 16)

            slot_load(0, 0)
            slot_load(1, 1)
            with sp.Fori(0, MT // 2 - 1) as r:
                for u in range(2):
                    sp.wait_ge(m_add, r * 32 + 16 * (u + 1))
                    slot_load(r * 2 + (u + 2), u)
            sp.wait_ge(m_add, 16 * (MT - 2))
            slot_load(MT - 1, 0)
            sp.wait_ge(m_add, 16 * MT)

        @block.gpsimd
        def _(pool):
            def gather():
                for b in range(G):
                    for k, (dst, table) in enumerate(((emb, "word_emb"), (wvg, "wvec"))):
                        pool.indirect_dma_start(
                            out=dst[:, b, :], out_offset=None, in_=a[table],
                            in_offset=bass.IndirectOffsetOnAxis(ap=idx_cur[:, k, b:b + 1], axis=0),
                        ).then_inc(s["gathered"], 16)

            pool.memset(idx_all[:, :, B:B + G], 0).then_inc(fills, 1)
            pool.memset(minus_half[:, :], -0.5).then_inc(fills, 1)
            pool.wait_ge(ld_const, 48)
            pool.tensor_copy(idx_cur[:, :, :], idx_all[:, :, 0:G]).then_inc(fills, 1)
            pool.wait_ge(fills, 3)
            gather()
            with pool.Fori(0, NG) as g:
                def w(name, n):
                    pool.wait_ge(s[name], g * PER[name] + n)
                def root(name, dst, src, n):
                    w(name, n)
                    half = minus_half[:, 0:src.free_size()]
                    if len(src.shape) == 3:
                        half = half.rearrange("p (b n) -> p b n", b=G)
                    pool.tensor_tensor(dst, src, half, ALU.pow).then_inc(s["rstd"], 1)

                def ln_root(name):
                    root(name, rs[:, 1, :], rs[:, 0, :], 11)

                def carry():
                    pool.tensor_tensor(spare[:, :], minus_half[:, 0:1], minus_half[:, 0:1], ALU.add)

                ln_root("ln0")
                for b in range(G):
                    w("ln0", 11 + b + 1)
                    pool.tensor_tensor(btok[:, b, :], btok[:, b, :], gammar, ALU.mult).then_inc(s["tok_scaled"], 1)
                for b in range(G):
                    w("tok_scaled", b + 1)
                    pool.tensor_tensor(btok[:, b, :], btok[:, b, :], betar, ALU.add).then_inc(s["tok_b"], 1)
                ln_root("ln1")
                root("norm2", nrm[:, :, :], nrm[:, :, :], 5)
                w("coef", 16)
                for b in range(G):
                    w("vug", b + 1)
                    pool.tensor_tensor(vk[:, b, :, :].rearrange("p h (k d) -> p h k d", k=3),
                                       bc(vug[:, b, 0:D].rearrange("p (h d) -> p h d", h=H), 2, 3),
                                       bc(ck[:, b, :, :], 3, HD), ALU.mult).then_inc(s["vk"], 1)
                for b in range(G):
                    o = osum[:, b, :].rearrange("p (h d) -> p h d", h=H)
                    w("o3", 2 * b + 2)
                    pool.tensor_tensor(o, o3[:, b % 2, :, 0:HD], o3[:, b % 2, :, HD:2 * HD], ALU.add)\
                        .then_inc(s["o_sum"], 1)
                    w("o_sum", 2 * b + 1)
                    pool.tensor_tensor(o, o, o3[:, b % 2, :, 2 * HD:3 * HD], ALU.add).then_inc(s["o_sum"], 1)
                root("hln", hl[:, 2, :, :], hl[:, 3, :, :], 17)
                ln_root("ln2")
                ln_root("ln3")
                w("gathered", 128)
                w("wvT", 4)
                pool.tensor_copy(idx_cur[:, :, :], idx_all[:, :, bass.ds(g * G + G, G)]).then_inc(s["idx_cur"], 1)
                w("idx_cur", 1)
                carry()
                gather()
                ln_root("ln4")
                for b in range(G):
                    w("hin", 2 * b + 2)
                    pool.tensor_tensor(hb[:, b, :], h[:, b, :], x[:, b, :], ALU.add).then_inc(s["hb"], 1)
                    w("hb", 2 * b + 1)
                    pool.tensor_tensor(hb[:, b, :], hb[:, b, :], bf2r, ALU.add).then_inc(s["hb"], 1)
                ln_root("ln5")
                ln_root("ln6")
                pool.wait_ge(slots_empty, 16)
                w("ln6", 15)
                pool.tensor_copy(x_all[:, bass.ds(g * G, G), 0:D], xn[:, :, :]).then_inc(s["keep"], 1)
                w("topw", 7)
                pool.tensor_copy(w12[:, bass.ds(g * G, G), :], tw[:, :, :]).then_inc(s["keep"], 1)
                pool.tensor_copy(oh[:, :, bass.ds(g * G, G), :], ohg[:, :, :, :]).then_inc(s["keep"], 1)
                w("out_row", 4)
            pool.wait_ge(s["gathered"], 128 * (NG + 1))
            pool.wait_ge(slots_empty, 16)
            for k in range(2):
                if k == 0:
                    pool.wait_ge(route, R_DONE)
                else:
                    pool.wait_ge(second_w, 1)
                for t in range(B):
                    pool.indirect_dma_start(
                        out=slots, out_offset=bass.IndirectOffsetOnAxis(ap=pos_i[:, k, t:t + 1], axis=0),
                        in_=x_all[:, t, :], in_offset=None).then_inc(scattered, 16)
            pool.wait_ge(s["base_out"], NG * PER["base_out"])
            rows_out = out.rearrange("b p n -> (b p) n")

            def add(tile, u):
                pool.wait_ge(m_y, tile + 1)
                pool.wait_ge(carried, tile)
                pool.wait_ge(m_add, tile * 16)
                pool.tensor_tensor(spare[:, :], minus_half[:, 0:1], minus_half[:, 0:1], ALU.add).then_inc(carried, 1)
                pool.indirect_dma_start(
                    out=rows_out, out_offset=bass.IndirectOffsetOnAxis(ap=xs[:, u, D + 1:D + 2].bitcast(I32), axis=0),
                    in_=ym[:, u, :], in_offset=None, bounds_check=B * S - 1, oob_is_err=False,
                    compute_op=ALU.add).then_inc(m_add, 16)

            with pool.Fori(0, MT // 2) as r:
                for u in range(2):
                    add(r * 2 + u, u)
            add(MT - 1, 0)
            pool.wait_ge(m_add, 16 * MT)

        @block.scalar
        def _(act):
            A = nc.scalar.activation
            act.wait_ge(setup_v, V_TAU)
            A(tau[:, 1, :], tau[:, 0, :], ACT.Exp).then_inc(setup_a, 1)
            with act.Fori(0, NG) as g:
                def w(name, n):
                    act.wait_ge(s[name], g * PER[name] + n)

                def done(name):
                    return s[name], 1

                act.wait_ge(s["out_row"], g * PER["out_row"])
                w("wvT", 4)
                A(gT[0:WV, :, :], PA[0:WV, 0, :].rearrange("p (b t) -> p b t", b=G), ACT.Copy).then_inc(*done("gT"))
                w("gate_dot", 4)
                A(ga[:, 0, :], zz[:, 0, :], ACT.Exp, bias=sc[:, 0:1], scale=-1.0).then_inc(*done("gate_exp"))
                for hf in range(2):
                    w("x1T", 2 * hf + 2)
                    A(chunks(xT, hf), half_of(PC, CW, hf), ACT.Copy).then_inc(*done("xT"))
                for b in range(G):
                    w("proj", b + 1)
                    A(vug[:, b, :], PS[b % 2][:, 1, 0:420], ACT.Copy).then_inc(*done("vug"))
                for b in range(G):
                    w("rope", 4 * b + 4)
                    A(sq[:, b, :, :], rq[:, b, :, 0:HD], ACT.Square).then_inc(*done("qk_sq"))
                w("vug", 4)
                A(eg[:, :, :, :], vug[:, :, 384:420].rearrange("p b (h k) -> p b h k", k=3)[:, :, :, 0:2],
                  ACT.Exp, scale=-1.0).then_inc(*done("gexp"))
                for b in range(G):
                    w("qkT", b + 1)
                    A(qkT[:, 0, b, :, :], PS[2 - b % 2][:, 0, 0:384].rearrange("p (j t) -> p j t", j=3), ACT.Copy)\
                        .then_inc(*done("q_evac"))
                w("smax", 2)
                A(eTs[:, :], PD[0:G * H, 0, 0:128], ACT.Exp, bias=smx[:, 0:1]).then_inc(*done("s_exp"))
                for hf in range(2):
                    w("onT", 2 * hf + 2)
                    A(chunks(nT, hf), half_of(PA, CW, hf), ACT.Copy).then_inc(*done("oT"))
                w("zdot", 4)
                A(zz[:, 1, :], zz[:, 0, :], ACT.Exp, bias=sc[:, 3:4], scale=-1.0).then_inc(*done("zexp"))
                for hf in range(2):
                    w("n3T", 2 * hf + 2)
                    for c in range(C):
                        i = A(chunks(nT, hf)[:, :, c, :], half_of(PC, CW, hf)[:, :, c, :], ACT.Identity,
                              bias=b1c[:, c:c + 1], scale=g1c[:, c:c + 1])
                    i.then_inc(*done("nT"))
                for c in range(C):
                    w("kT", 1)
                    A(k2T[:, c, :], PC[0:CW, c, :], ACT.Identity, bias=bkc[:, c:c + 1]).then_inc(*done("kT_evac"))
                for hf in range(2):
                    w("v2p", 2 * hf + 2)
                    A(v2[:, 2 * hf:2 * hf + 2, :].rearrange("p b n -> p (b n)"), PB[:, hf, 0:2 * D], ACT.Copy).then_inc(*done("v2"))
                w("sel", 4)
                for c in range(C):
                    A(sT[:, c, :, :], PA[0:CW, c, 0:G * (KSEL + 1)].rearrange("p (b k) -> p b k", b=G), ACT.Identity,
                      bias=b1c[:, c:c + 1], scale=g1c[:, c:c + 1]).then_inc(*done("selT"))
                w("qT", 1)
                for c in range(C):
                    A(qTs[:, c, :, :], PD[0:CW, 1, 64 + c * 80:64 + c * 80 + G * KSEL].rearrange("p (b k) -> p b k", b=G),
                      ACT.Identity, bias=bqc[:, c:c + 1]).then_inc(*done("q_bias"))
                w("pselT_p", 4)
                A(pselT[:, :, :].rearrange("p b t -> p (b t)"), PA[0:KSEL, 0, :], ACT.Copy).then_inc(*done("pselT"))
                for b in range(G):
                    w("nmax", 2 * half(b))
                    for c in range(C):
                        A(pr[:, b, c, :], part_of(PC, HC * KSEL, b, c), ACT.Exp, bias=nx[:, 1, b, c:c + 1], scale=0.25,
                          accum_out=nx[:, 2, b, c:c + 1]).then_inc(*done("pexp"))
                for hf in range(2):
                    w("pT_p", 2 * hf + 2)
                    A(pT[:, :, 2 * hf:2 * hf + 2, :].rearrange("p c b k -> p b c k"), half_of(PB, 128, hf, HC * KSEL),
                      ACT.Copy).then_inc(*done("pT"))
                for hf in range(2):
                    w("asel_p", 2 * hf + 2)
                    A(aselb[:, 2 * hf:2 * hf + 2, :].rearrange("p b n -> p (b n)"), PC[0:KSEL, hf, 0:2 * D], ACT.Copy).then_inc(*done("asel"))
                for hf in range(2):
                    w("n4T", 2 * hf + 2)
                    for c in range(C):
                        i = A(chunks(nT, hf)[:, :, c, :], half_of(PA, CW, hf)[:, :, c, :], ACT.Identity,
                              bias=b2c[:, c:c + 1], scale=g2c[:, c:c + 1])
                    i.then_inc(*done("n2T"))
                for j in range(FJ):
                    w("up", j + 1)
                    A(hid[:, j, :], PS[1 + j // 2][:, j % 2, :], ACT.Gelu, bias=bf1c[:, j:j + 1]).then_inc(*done("gelu"))
                for hf in range(2):
                    w("x5T", 2 * hf + 2)
                    A(chunks(xT, hf), half_of(PB, CW, hf), ACT.Copy).then_inc(*done("x5T_e"))
                for n in range(6):
                    w("qk1", n + 1)
                    A(q1k1[:, n % 2, n // 2, :], (PC, PD, PA)[n // 2][:, n % 2, :], ACT.Copy).then_inc(*done("qk1_e"))
                for hf in range(2):
                    w("v1p", 2 * hf + 2)
                    A(v1[:, 2 * hf:2 * hf + 2, :].rearrange("p b n -> p (b n)"), PB[:, hf, 0:2 * H * (HD + 1)], ACT.Copy).then_inc(*done("v1"))

                def exps(b):
                    w("nm1", 3 * b + 3)
                    if b >= 2:
                        w("e1T", 2 * (b - 2) + 2)
                    for k in range(H):
                        i, j = k // 3, k % 3
                        ins = A(e1[:, b % 2, k, :], (PC, PD)[i // 2][:, i % 2, j * 128:j * 128 + 128], ACT.Exp,
                                bias=nm1[:, b, k:k + 1], scale=0.25)
                        if k % 6 == 5:
                            ins.then_inc(*done("e1"))

                def eT_evac(b):
                    w("e1T", 2 * b + 2)
                    A(eT[:, b % 2, 8:12, :].rearrange("p h t -> p (h t)"), PB[:, 0, :], ACT.Copy).then_inc(*done("e1T_e"))

                for b in range(G):
                    exps(b)
                    if b:
                        eT_evac(b - 1)
                eT_evac(G - 1)
                for hf in range(2):
                    w("x6T", 2 * hf + 2)
                    A(chunks(xT, hf), half_of(PA, CW, hf), ACT.Copy).then_inc(*done("x6T_e"))
                w("smx", 2)
                A(gl[:, 1, :, :], gl[:, 0, :, :], ACT.Exp).then_inc(*done("gexp2"))
                w("gatesT_p", 4)
                A(gatT[:, :, :].rearrange("p b t -> p (b t)"), PB[0:NE, 1, :], ACT.Copy).then_inc(*done("gatesT"))

            def gelu(tile, u):
                act.wait_ge(m_up, tile + 1)
                A(hm_[:, u, :].rearrange("p (c n) -> p c n", c=2), PS[u][:, :, 0:384], ACT.Gelu).then_inc(m_gelu, 1)

            with act.Fori(0, MT // 2) as r:
                for u in range(2):
                    gelu(r * 2 + u, u)
            gelu(MT - 1, 0)

        @block.vector
        def _(dve):
            T, TS, STT = nc.vector.tensor_tensor, nc.vector.tensor_scalar, nc.vector.scalar_tensor_tensor
            steps = [0]

            def step(ins):
                ins.then_inc(setup_v, 1)
                steps[0] += 1
                return steps[0]

            fill = nc.vector.memset
            assert step(fill(w_g2b[64:96, :], 0.0)) == V_G2B
            n = step(fill(empty, 0.0))
            dve.wait_ge(setup_v, n)
            assert step(fill(empty[:, D + 1:D + 2].bitcast(I32), NOBODY)) == V_EMPTY
            n = step(fill(gT[64:96, :, :], 0.0))
            step(fill(gT[96:97, :, :], 1.0))
            step(fill(xT[96:97, :, :], 1.0))
            step(fill(nT[96:97, :, :], 1.0))
            step(fill(ctxT[96:97, :, :, :], 1.0))
            step(fill(rq[:, :, :, :], 0.0))
            step(fill(w_1q[:, :, :, :], 0.0))
            step(fill(w_1k[:, :, :, :], 0.0))
            n = step(fill(w_1v[:, :, :, :], 0.0))
            dve.wait_ge(setup_v, n)
            step(fill(w_1v[96:97, 0, :, HD:HD + 1], 1.0))
            dve.wait_ge(ld_l0, 128)
            n = step(TS(tau[:, 2, :], tau[:, 0, :], -50.0, 30.0, ALU.max, ALU.min))
            dve.wait_ge(setup_v, n)
            assert step(nc.vector.tensor_copy(tau[:, 0, :], tau[:, 2, :])) == V_TAU
            dve.wait_ge(ld_tok, 208)
            step(T(pos_type[:, :], pos_type[:, :], typer, ALU.add))
            step(nc.vector.tensor_tensor_reduce(out=junk[:, 0, :], in0=rowtmp[:, 1, :], in1=wrr, scale=1.0, scalar=0.0,
                                                op0=ALU.mult, op1=ALU.add, accum_out=sc[:, 2:3]))
            n = step(T(wrr, wrr, rowtmp[:, 0, :], ALU.mult))
            dve.wait_ge(setup_v, n)
            step(STT(sc[:, 3:4], sc[:, 2:3], -1.0, sc[:, 1:2], ALU.mult, ALU.subtract))
            step(TS(sc[:, 0:1], sc[:, 0:1], -1.0, None, ALU.mult))
            dve.wait_ge(setup_p, 1)
            assert step(nc.vector.tensor_copy(mqk, PA[0:HD, 0, 0:HD])) == V_MQK
            dve.wait_ge(setup_p, 2)
            step(nc.vector.tensor_copy(um[:, 0, :], PB[0:97, 0, 0:D]))
            step(nc.vector.tensor_copy(um[:, 1, :], PB[0:97, 0, D:2 * D]))
            assert step(nc.vector.tensor_copy(um[:, 2, :], PB[0:97, 1, 0:D])) == V_UM
            dve.wait_ge(setup_p, 3)
            for w_, (dst, src, lo) in enumerate(((w_1q, PC, 0), (w_1k, PC, D), (w_1v, PD, 0))):
                for c in range(C):
                    n = step(nc.vector.tensor_copy(dst[0:KC[c], c, :, 0:HD],
                                                   src[0:KC[c], c, lo:lo + D].rearrange("p (h d) -> p h d", h=H)))
            assert n == V_FOLDED
            dve.wait_ge(setup_a, 1)
            n = step(TS(tau[:, 2, :], tau[:, 1, :], con("t"), None, ALU.add))
            dve.wait_ge(setup_v, n)
            n = step(nc.vector.reciprocal(tau[:, 0, :], tau[:, 2, :]))
            dve.wait_ge(setup_v, n)
            step(TS(rtau[:, :], tau[:, 0, :], -float(HD) ** -0.5, None, ALU.mult))
            n = step(T(taumu[0:1, :].rearrange("p (h d) -> p h d", h=H), mu_row[0:1, :].rearrange("p (h d) -> p h d", h=H),
                       bc(tau[0:1, 1, :], 2, HD), ALU.mult))
            assert n == V_SETUP
            dve.wait_ge(setup_v, n)

            with dve.Fori(0, NG) as g:
                def w(name, n):
                    dve.wait_ge(s[name], g * PER[name] + n)

                def inc(ins, name):
                    ins.then_inc(s[name], 1)

                def norm(name, src, dst, ready, eps=1e-5):
                    for b in range(G):
                        w(ready[0], ready[1](b))
                        nc.vector.bn_stats(st[:, b, :], src[:, b, :]).then_inc(s[name], 1)
                    w(name, 4)
                    inc(T(mv[:, 0, :], st[:, :, 1], st[:, :, 4], ALU.add), name)
                    inc(T(mv[:, 1, :], st[:, :, 1], st[:, :, 4], ALU.subtract), name)
                    inc(T(mv[:, 2, :], st[:, :, 2], st[:, :, 5], ALU.add), name)
                    w(name, 5)
                    inc(TS(mv[:, 3, :], mv[:, 0, :], 0.5, None, ALU.mult), name)
                    w(name, 6)
                    inc(T(mv[:, 4, :], mv[:, 1, :], mv[:, 1, :], ALU.mult), name)
                    w(name, 9)
                    inc(STT(mv[:, 5, :], mv[:, 4, :], D / 4.0, mv[:, 2, :], ALU.mult, ALU.add), name)
                    w(name, 10)
                    inc(TS(rs[:, 0, :], mv[:, 5, :], 1.0 / D, eps, ALU.mult, ALU.add), name)
                    w("rstd", rstd_of(name))
                    for b in range(G):
                        TS(dst[:, b, :], src[:, b, :], mv[:, 3, b:b + 1], rs[:, 1, b:b + 1], ALU.subtract, ALU.mult)\
                            .then_inc(s[name], 1)

                w("gathered", 128)
                w("keep", 0)
                for b in range(G):
                    T(emb[:, b, :], emb[:, b, :], pos_type[:, :], ALU.add).then_inc(s["emb_sum"], 1)
                norm("ln0", emb, btok, ("emb_sum", lambda b: b + 1), 1e-12)
                for b in range(G):
                    w("tok_b", b + 1)
                    nc.vector.tensor_tensor_reduce(
                        out=junk[:, b, :], in0=btok[:, b, :], in1=gatewr, scale=1.0, scalar=0.0, op0=ALU.mult,
                        op1=ALU.add, accum_out=zz[:, 0, b:b + 1]).then_inc(s["gate_dot"], 1)
                w("gate_exp", 1)
                TS(ga[:, 1, :], ga[:, 0, :], 1.0, None, ALU.add).then_inc(s["gate_a"], 1)
                w("gate_a", 1)
                nc.vector.reciprocal(ga[:, 2, :], ga[:, 1, :]).then_inc(s["gate_a"], 1)
                for b in range(G):
                    w("g_ready", half(b))
                    T(hb[:, b, :], psl(PB, b, D), btok[:, b, :], ALU.subtract).then_inc(s["g_diff"], 1)
                w("gate_a", 2)
                for b in range(G):
                    w("g_diff", b + 1)
                    STT(h[:, b, :], hb[:, b, :], ga[:, 2, b:b + 1], btok[:, b, :], ALU.mult, ALU.add)\
                        .then_inc(s["h_tok"], 1)

                norm("ln1", h, x, ("h_tok", lambda b: b + 1))
                for b in range(G):
                    w("proj", b + 1)
                    qk = PS[b % 2][:, 0, 0:384].rearrange("p (h d) -> p h d", d=HD)
                    hh = HD // 2
                    T(rq[:, b, :, 0:HD], qk, bc(con("cos"), 1, 24), ALU.mult).then_inc(s["rope"], 1)
                    T(sq[:, b, :, 0:hh], qk[:, :, hh:HD], bc(con("sin")[:, 0:hh], 1, 24), ALU.mult)\
                        .then_inc(s["rope"], 1)
                    T(sq[:, b, :, hh:HD], qk[:, :, 0:hh], bc(con("sin")[:, hh:HD], 1, 24), ALU.mult)\
                        .then_inc(s["rope"], 1)
                    w("rope", 4 * b + 3)
                    T(rq[:, b, :, 0:HD], rq[:, b, :, 0:HD], sq[:, b, :, :], ALU.add).then_inc(s["rope"], 1)
                for b in range(G):
                    w("usum", half(b))
                    T(osum[:, b, :], psl(PD, b, D), vug[:, b, D:2 * D], ALU.mult).then_inc(s["sdot"], 1)
                    w("sdot", 3 * b + 1)
                    nc.vector.reduce_sum(hl[:, 0, b, :], osum[:, b, :].rearrange("p (h d) -> p h d", h=H), AX.X)\
                        .then_inc(s["sdot"], 1)
                    w("sdot", 3 * b + 2)
                    T(es[:, 1, b, :], hl[:, 0, b, :], rtau[:, :], ALU.mult).then_inc(s["sdot"], 1)
                for b in range(G):
                    w("qk_sq", b + 1)
                    nc.vector.reduce_sum(nrm[:, b, :], sq[:, b, :, :], AX.X).then_inc(s["norm2"], 1)
                w("norm2", 4)
                TS(nrm[:, :, :], nrm[:, :, :], 1e-24, None, ALU.max).then_inc(s["norm2"], 1)
                w("sT", 1)
                nc.vector.reduce_max(smx[:, :], PD[0:G * H, 0, 0:128], AX.X).then_inc(s["smax"], 1)
                w("smax", 1)
                TS(smx[:, :], smx[:, :], -1.0, None, ALU.mult).then_inc(s["smax"], 1)
                for b in range(G):
                    w("qkT", b + 1)
                    nc.vector.tensor_copy(qkT[:, 1, b, :, :], PS[2 - b % 2][:, 1, 0:384].rearrange("p (j t) -> p j t", j=3))\
                        .then_inc(s["k_evac"], 1)
                w("eback", 1)
                nc.vector.tensor_copy(es[:, 0, :, :], PD[:, 0, 128:128 + G * H].rearrange("p (b h) -> p b h", b=G))\
                    .then_inc(s["es_ready"], 1)
                sig1, sigh = eg[:, :, :, 0], eg[:, :, :, 1]
                et = PD[:, 0, 192:240].rearrange("p (b h) -> p b h", b=G)
                pt = PD[:, 0, 240:288].rearrange("p (b h) -> p b h", b=G)
                al, be, gm = cf[:, 0, :, :], cf[:, 1, :, :], cf[:, 2, :, :]
                w("gexp", 1)
                inc(TS(eg[:, :, :, :], eg[:, :, :, :], 1.0, None, ALU.add), "coef")
                w("coef", 1)
                inc(nc.vector.reciprocal(eg[:, :, :, :], eg[:, :, :, :]), "coef")
                w("rstd", rstd_of("norm2"))
                inc(nc.vector.tensor_copy(ck[:, :, :, 2], nrm[:, :, H:24]), "coef")
                w("es_ready", 1)
                inc(T(ck[:, :, :, 0], es[:, 0, :, :], nrm[:, :, H:24], ALU.mult), "coef")
                inc(T(ck[:, :, :, 1], es[:, 1, :, :], nrm[:, :, H:24], ALU.mult), "coef")
                w("coef", 2)
                inc(T(be, sig1, sigh, ALU.subtract), "coef")
                w("coef", 6)
                inc(TS(be, be, con("rt"), None, ALU.mult), "coef")
                w("cum", 1)
                inc(TS(al, et, 1e-12, None, ALU.add), "coef")
                w("coef", 8)
                inc(nc.vector.reciprocal(al, al), "coef")
                inc(T(gm, be, pt, ALU.mult), "coef")
                w("coef", 10)
                inc(T(al, al, sigh, ALU.mult), "coef")
                inc(T(gm, gm, sigh, ALU.add), "coef")
                w("coef", 12)
                inc(TS(gm, gm, con("rt"), -1.0, ALU.mult, ALU.mult), "coef")
                inc(T(cq[:, :, :, 0], al, nrm[:, :, 0:H], ALU.mult), "coef")
                inc(T(cq[:, :, :, 1], be, nrm[:, :, 0:H], ALU.mult), "coef")
                w("coef", 13)
                inc(T(cq[:, :, :, 2], gm, nrm[:, :, 0:H], ALU.mult), "coef")

                def mask(b):
                    if b >= 2:
                        w("pv", b - 1)
                    for hf in range(2):
                        w("A0", 2 * b + hf + 1)
                        T(am[:, b % 2, 2 * hf:2 * hf + 2, :, :],
                          PS[hf][:, :, 0:384].rearrange("p i (j t) -> p i j t", j=3),
                          bc(bc(con("le"), 1, 3), 1, 2), ALU.mult).then_inc(s["A_masked"], 1)

                def weigh(b):
                    w("pv", b + 1)
                    if b >= 2:
                        w("o_sum", 2 * (b - 2) + 2)
                    for c in range(C):
                        T(o3[:, b % 2, c * HC:(c + 1) * HC, :].rearrange("p h (k d) -> p (h k) d", k=3),
                          PS[2 + b % 2][:, c, 0:288].rearrange("p (x d) -> p x d", d=HD),
                          bc(cq[:, b, c * HC:(c + 1) * HC, :].rearrange("p h k -> p (h k)"), 2, HD), ALU.mult)\
                            .then_inc(s["o3"], 1)

                for b in range(G):
                    mask(b)
                    if b:
                        weigh(b - 1)
                weigh(G - 1)
                oh3 = [osum[:, b, :].rearrange("p (h d) -> p h d", h=H) for b in range(G)]
                on3 = [onrm[:, b, :].rearrange("p (h d) -> p h d", h=H) for b in range(G)]
                jk3 = [junk[:, b, :].rearrange("p (h d) -> p h d", h=H) for b in range(G)]
                for b in range(G):
                    w("o_sum", 2 * b + 2)
                    nc.vector.reduce_sum(hl[:, 0, b, :], oh3[b], AX.X).then_inc(s["hln"], 1)
                for b in range(G):
                    w("hln", b + 1)
                    STT(on3[b], bc(hl[:, 0, b, :], 2, HD), -1.0 / HD, oh3[b], ALU.mult, ALU.add).then_inc(s["hln"], 1)
                for b in range(G):
                    w("hln", 4 + b + 1)
                    T(jk3[b], on3[b], on3[b], ALU.mult).then_inc(s["hln"], 1)
                for b in range(G):
                    w("hln", 8 + b + 1)
                    nc.vector.reduce_sum(hl[:, 1, b, :], jk3[b], AX.X).then_inc(s["hln"], 1)
                w("hln", 16)
                TS(hl[:, 3, :, :], hl[:, 1, :, :], HD * 1e-5, None, ALU.add).then_inc(s["hln"], 1)
                w("rstd", rstd_of("hln"))
                for b in range(G):
                    STT(on3[b], on3[b], float(HD) ** 0.5, bc(hl[:, 2, b, :], 2, HD), ALU.mult, ALU.mult)\
                        .then_inc(s["hln"], 1)
                for b in range(G):
                    w("wo", half(b))
                    T(h[:, b, :], h[:, b, :], psl(PB, b, D), ALU.add).then_inc(s["h_attn"], 1)

                norm("ln2", h, x, ("h_attn", lambda b: b + 1))
                dve.wait_ge(s["base_out"], g * PER["base_out"])
                norm("ln3", x, xn, ("ln2", lambda b: 11 + b + 1))
                for b in range(G):
                    w("ln3", 11 + b + 1)
                    nc.vector.tensor_tensor_reduce(
                        out=junk[:, b, :], in0=xn[:, b, :], in1=wrr, scale=1.0, scalar=0.0, op0=ALU.mult,
                        op1=ALU.add, accum_out=zz[:, 0, b:b + 1]).then_inc(s["zdot"], 1)
                w("zexp", 1)
                TS(zz[:, 2, :], zz[:, 1, :], 1.0, None, ALU.add).then_inc(s["score"], 1)
                w("score", 1)
                nc.vector.reciprocal(zz[:, 3, :], zz[:, 2, :]).then_inc(s["score"], 1)
                w("score", 2)
                for b in range(G):
                    TS(dg[:, b, :], ident, zz[:, 3, b:b + 1], None, ALU.mult).then_inc(s["dg"], 1)
                w("ssum", 1)
                TS(ga[:, 0, :], PD[:, 1, 0:G], 1e-6, None, ALU.add).then_inc(s["wsel"], 1)
                w("wsel", 1)
                nc.vector.reciprocal(ga[:, 1, :], ga[:, 0, :]).then_inc(s["wsel"], 1)
                w("wsel", 2)
                T(pw[:, :, KSEL], zz[:, 3, :], ga[:, 1, :], ALU.mult).then_inc(s["wsel"], 1)
                T(ga[:, 2, :], PD[:, 1, 0:G], ga[:, 1, :], ALU.mult).then_inc(s["wsel"], 1)
                for b in range(G):
                    w("bc", 4)
                    STT(junk[:, b, 0:128], PD[:, 0, tok(b)], zz[:, 3, b:b + 1], con("gt"), ALU.is_lt, ALU.mult,
                        accum_out=rk[:, 0, b:b + 1]).then_inc(s["rank"], 1)
                for b in range(G):
                    STT(btok[:, b, 0:128], PD[:, 0, tok(b)], zz[:, 3, b:b + 1], con("lt"), ALU.is_le, ALU.mult,
                        accum_out=rk[:, 1, b:b + 1]).then_inc(s["rank"], 1)
                for b in range(G):
                    w("rank", 4 + b + 1)
                    T(rk[:, 2, b:b + 1], rk[:, 0, b:b + 1], rk[:, 1, b:b + 1], ALU.add).then_inc(s["rank"], 1)
                for b in range(G):
                    w("rank", 8 + b + 1)
                    TS(pw[:, b, 0:KSEL], con("iota"), rk[:, 2, b:b + 1], None, ALU.is_equal).then_inc(s["rank"], 1)
                TS(nmask[:, :], rk[:, 2, :], KSEL - 0.5, None, ALU.is_ge).then_inc(s["nmask"], 1)
                w("selT", 2)
                for c in range(C):
                    TS(ptmp[:, c, :], ga[0:CW, 2, :], b1c[:, c:c + 1], None, ALU.mult).then_inc(s["pool_fix"], 1)
                    w("pool_fix", 2 * c + 1)
                    STT(poolT[:, c, :], PA[0:CW, c, 0:G * (KSEL + 1)].rearrange("p (b k) -> p b k", b=G)[:, :, KSEL],
                        g1c[:, c:c + 1], ptmp[:, c, :], ALU.mult, ALU.add).then_inc(s["pool_fix"], 1)
                hmb = con("hm", CW)
                for c in range(C):
                    w("q_bias", c + 1)
                    T(qbd[:, c, :, :].rearrange("p b (h k) -> p b h k", h=HC), bc(qTs[:, c, :, :], 2, HC),
                      bc(bc(hmb, 2, KSEL), 1, G), ALU.mult).then_inc(s["qbd"], 1)
                fill(mT[96:97, :, :], 1.0).then_inc(s["mT_one"], 1)
                w("pool_fix", 4)
                for b in range(G):
                    w("nT", b // 2 + 1)
                    for c in range(C):
                        STT(mT[0:CW, c, tok(b)], PD[0:CW, 0, tok(b)], poolT[:, c, b:b + 1], nT[0:CW, c, tok(b)],
                            ALU.mult, ALU.add).then_inc(s["mixT"], 1)
                for b in range(G):
                    w("lg", half(b))
                    nc.vector.reduce_max(nx[:, 0, b, :], half_of(PC, HC * KSEL, b // 2)[:, b % 2, :, :], AX.X).then_inc(s["nmax"], 1)
                    w("nmax", 2 * b + 1)
                    TS(nx[:, 1, b, :], nx[:, 0, b, :], -0.25, None, ALU.mult).then_inc(s["nmax"], 1)
                for b in range(G):
                    w("pexp", 2 * b + 2)
                    nc.vector.reciprocal(nx[:, 0, b, :], nx[:, 2, b, :]).then_inc(s["pnorm"], 1)
                    w("pnorm", 3 * b + 1)
                    for c in range(C):
                        TS(pr[:, b, c, :], pr[:, b, c, :], nx[:, 0, b, c:c + 1], None, ALU.mult)\
                            .then_inc(s["pnorm"], 1)
                for b in range(G):
                    w("ctx", half(b))
                    T(ctxm[:, :, b, :].rearrange("p c (h k) -> p c h k", h=HC),
                      half_of(PA, CW, b // 2, HC * KSEL)[:, b % 2, :, :].rearrange("p c (h k) -> p c h k", h=HC),
                      bc(bc(hmb, 2, KSEL), 1, C), ALU.mult).then_inc(s["ctx_m"], 1)
                    w("ctx_m", b + 1)
                    nc.vector.reduce_sum(ctxT[0:CW, :, b, :], ctxm[:, :, b, :].rearrange("p c (h k) -> p c k h", h=HC),
                                         AX.X).then_inc(s["ctxT"], 1)
                for b in range(G):
                    w("mix", half(b))
                    STT(x[:, b, :], psl(PC, b, D), nmask[:, b:b + 1], x[:, b, :], ALU.mult, ALU.add)\
                        .then_inc(s["hin"], 1)
                    w("attn", half(b))
                    w("hin", 2 * b + 1)
                    T(x[:, b, :], x[:, b, :], psl(PB, b, D), ALU.add).then_inc(s["hin"], 1)
                norm("ln4", x, xn, ("hin", lambda b: 2 * b + 2))
                for b in range(G):
                    w("down", half(b))
                    w("hb", 2 * b + 2)
                    T(h[:, b, :], hb[:, b, :], psl(PA, b, D), ALU.add).then_inc(s["h_ffn"], 1)

                norm("ln5", h, x, ("h_ffn", lambda b: b + 1))

                def maxima(b):
                    for hf in range(2):
                        w("lg1", 2 * b + hf + 1)
                        nc.vector.reduce_max(nm1[:, b, 6 * hf:6 * hf + 6],
                                             PS[2 + hf][:, :, 0:384].rearrange("p i (j t) -> p i j t", j=3), AX.X)\
                            .then_inc(s["nm1"], 1)
                    w("nm1", 3 * b + 2)
                    TS(nm1[:, b, :], nm1[:, b, :], -0.25, None, ALU.mult).then_inc(s["nm1"], 1)

                def eT_evac(b):
                    w("e1T", 2 * b + 1)
                    if b >= 2:
                        w("pv1", b - 1)
                    nc.vector.tensor_copy(eT[:, b % 2, 0:8, :].rearrange("p (i j) t -> p i (j t)", i=2), PA[:, :, :])\
                        .then_inc(s["e1T_ev"], 1)

                def attend(b):
                    w("pv1", b + 1)
                    pv = PB[:, 1, 0:H * (HD + 1)].rearrange("p (h d) -> p h d", h=H)
                    r = r1[:, b, :]
                    at_ = att[:, b, :].rearrange("p (h d) -> p h d", h=H)
                    nc.vector.reciprocal(r, pv[:, :, HD]).then_inc(s["h_l1"], 1)
                    w("h_l1", 3 * b + 1)
                    T(at_, pv[:, :, 0:HD], bc(r, 2, HD), ALU.mult).then_inc(s["h_l1"], 1)
                    w("h_l1", 3 * b + 2)
                    T(h[:, b, :], h[:, b, :], att[:, b, :], ALU.add).then_inc(s["h_l1"], 1)

                maxima(0)
                for b in range(G):
                    if b + 1 < G:
                        maxima(b + 1)
                    eT_evac(b)
                    if b:
                        attend(b - 1)
                attend(G - 1)

                norm("ln6", h, xn, ("h_l1", lambda b: 3 * b + 3))
                w("gate", 1)
                lg = PB[:, 0, 0:G * NE].rearrange("p (b e) -> p b e", b=G)
                nc.vector.reduce_max(g1s[:, 0, :], lg, AX.X).then_inc(s["smx"], 1)
                w("smx", 1)
                T(gl[:, 0, :, :], lg, bc(g1s[:, 0, :], 2, NE), ALU.subtract).then_inc(s["smx"], 1)
                w("gexp2", 1)
                nc.vector.reduce_sum(g1s[:, 1, :], gl[:, 1, :, :], AX.X).then_inc(s["smx"], 1)
                w("smx", 3)
                nc.vector.reciprocal(g1s[:, 2, :], g1s[:, 1, :]).then_inc(s["smx"], 1)
                w("smx", 4)
                T(gl[:, 2, :, :], gl[:, 1, :, :], bc(g1s[:, 2, :], 2, NE), ALU.mult).then_inc(s["smx"], 1)
                w("smx", 5)
                inc(nc.vector.tensor_copy(g1s[:, 3, :], g1s[:, 2, :]), "topk")
                for b in range(G):
                    nc.vector.max(m8[:, b, :], gl[:, 2, b, :]).then_inc(s["topk"], 1)
                w("topk", 5)
                inc(nc.vector.tensor_copy(g1s[:, 3, :], g1s[:, 2, :]), "topk")
                for b in range(G):
                    nc.vector.max_index(i8[:, b, :], m8[:, b, :], gl[:, 2, b, :]).then_inc(s["topk"], 1)
                inc(T(g1s[:, 0, :], m8[:, :, 0], m8[:, :, 1], ALU.add), "topw")
                w("topk", 10)
                inc(nc.vector.tensor_copy(i8f[:, :, :], i8[:, :, 0:2]), "topw")
                w("topw", 1)
                inc(TS(g1s[:, 1, :], g1s[:, 0, :], 1e-9, None, ALU.add), "topw")
                w("topw", 2)
                io8 = bc(con("iota8"), 1, G)
                inc(T(ohg[:, 0, :, :], io8, bc(i8f[:, :, 0], 2, NE), ALU.is_equal), "topw")
                inc(T(ohg[:, 1, :, :], io8, bc(i8f[:, :, 1], 2, NE), ALU.is_equal), "topw")
                w("topw", 3)
                inc(nc.vector.reciprocal(g1s[:, 3, :], g1s[:, 1, :]), "topw")
                w("topw", 6)
                inc(T(tw[:, :, :], m8[:, :, 0:2], bc(g1s[:, 3, :], 2, 2), ALU.mult), "topw")
                w("topw", 7)
                inc(T(gl[:, 3, :, :], ohg[:, 0, :, :], bc(tw[:, :, 0], 2, NE), ALU.mult), "topw")
                inc(T(gl[:, 4, :, :], ohg[:, 1, :, :], bc(tw[:, :, 1], 2, NE), ALU.mult), "topw")
                w("topw", 9)
                inc(T(gl[:, 0, :, :], gl[:, 3, :, :], gl[:, 4, :, :], ALU.add), "topw")
                w("keep", 1)
                for b in range(G):
                    w("b2p", half(b))
                    T(xn[:, b, :], h[:, b, :], psl(PC, b, D), ALU.add).then_inc(s["out_row"], 1)

            done = [0]

            def r_step(ins):
                ins.then_inc(route, 1)
                done[0] += 1
                return done[0]

            def r_wait(n):
                dve.wait_ge(route, n)

            flat = "p b e -> p (b e)"
            dve.wait_ge(s["keep"], NG * PER["keep"])
            n = r_step(T(ohs, oh[:, 0, :, :], oh[:, 1, :, :], ALU.add))
            assert n == R_OHS
            r_step(nc.vector.tensor_copy(x_all[:, :, D], w12[:, :, 0]))
            r_step(nc.vector.tensor_copy(x_all[:, :, D + 1].bitcast(I32), tok_no[:, :]))
            r_step(fill(before[:, 0, :], 0.0))
            dve.wait_ge(route_p, 1)
            n = r_step(nc.vector.tensor_copy(tot.rearrange(flat), PA[:, 0, 128:256]))
            for t in range(1, B):
                r_wait(n)
                n = r_step(T(before[:, t, :], before[:, t - 1, :], tot[:, t - 1, :], ALU.add))
            r_wait(n)
            n = r_step(T(cnt[:, 0, :], before[:, B - 1, :], tot[:, B - 1, :], ALU.add))
            r_wait(n)
            n = r_step(TS(cnt_i[:, 0, :], cnt[:, 0, :], 127.0, None, ALU.add))
            r_wait(n)
            n = r_step(TS(cnt_i[:, 1, :], cnt_i[:, 0, :], 7, None, ALU.logical_shift_right))
            r_wait(n)
            n = r_step(nc.vector.tensor_copy(cnt[:, 1, :], cnt_i[:, 1, :]))
            r_wait(n)
            n = r_step(nc.vector.tensor_copy(cnt[:, 2, 0:1], cnt[:, 1, 0:1]))
            for e in range(1, NE):
                r_wait(n)
                n = r_step(T(cnt[:, 2, e:e + 1], cnt[:, 2, e - 1:e], cnt[:, 1, e:e + 1], ALU.add))
            r_wait(n)
            n = r_step(T(cnt[:, 3, :], cnt[:, 2, :], cnt[:, 1, :], ALU.subtract))
            k = r_step(T(owner, bc(con("slot"), 2, NE), bc(cnt[:, 2, :], 1, MT), ALU.is_ge))
            r_wait(n)
            n = r_step(TS(cnt[:, 3, :], cnt[:, 3, :], 128.0, None, ALU.mult))
            r_wait(k)
            k = r_step(nc.vector.reduce_sum(ownf, owner, AX.X))
            r_step(T(pos.rearrange(flat), before.rearrange(flat), PA[:, 0, 0:128], ALU.add))
            r_wait(k)
            r_step(TS(own_i[:, :], ownf, float(NE - 1), None, ALU.min))
            r_wait(n + 2)
            n = r_step(T(pos, pos, bc(cnt[:, 3, :], 1, B), ALU.add))
            r_wait(n)
            for k in range(2):
                n = r_step(T(posk[:, k, :, :], oh[:, k, :, :], pos, ALU.mult))
            r_wait(n)
            for k in range(2):
                n = r_step(nc.vector.reduce_sum(posf[:, k, :], posk[:, k, :, :], AX.X))
            r_wait(n)
            n = r_step(nc.vector.tensor_copy(pos_i[:, :, :], posf))
            assert n == R_DONE, n
            dve.wait_ge(scattered, 16 * B)
            nc.vector.tensor_copy(x_all[:, :, D], w12[:, :, 1]).then_inc(second_w, 1)

            def xT_evac(tile, u):
                dve.wait_ge(m_xT, tile + 1)
                nc.vector.tensor_copy(xT[0:CW, :, tok(u)], PD[0:CW, 0, 0:256].rearrange("p (c t) -> p c t", c=C))\
                    .then_inc(m_xTe, 1)

            def hT_evac(tile, u):
                dve.wait_ge(m_hT, tile + 1)
                nc.vector.tensor_copy(hTm[:, u, :, :].rearrange("p (c j) t -> p c j t", c=2),
                                      PC[:, :, 0:384].rearrange("p c (j t) -> p c j t", j=3)).then_inc(m_hTe, 1)

            def weight(tile, u):
                dve.wait_ge(m_down, tile + 1)
                dve.wait_ge(m_add, tile * 16)
                TS(ym[:, u, :], PD[:, 1, 0:D], xs[:, u, D:D + 1], None, ALU.mult).then_inc(m_y, 1)

            xT_evac(0, 0)
            with dve.Fori(0, MT // 2) as r:
                for u in range(2):
                    tile = r * 2 + u
                    xT_evac(r * 2 + (u + 1), 1 - u)
                    hT_evac(tile, u)
                    weight(tile, u)
            hT_evac(MT - 1, 0)
            weight(MT - 1, 0)

        @block.tensor
        def _(pe):
            def mm(o, l, r, start=True, stop=True):
                return nc.tensor.matmul(o, l, r, start=start, stop=stop)

            def tr(o, i, k):
                return nc.tensor.transpose(o, i, ident[0:k, 0:k])

            pe.wait_ge(ld_const, 48)
            pe.wait_ge(ld_l1, 96)
            mm(PA[0:HD, 0, 0:HD], mu_mv[:, 0, 0:HD], mu_mv[:, 1, 0:HD]).then_inc(setup_p, 1)
            pe.wait_ge(setup_v, V_MQK)
            for w_ in range(3):
                for hh in range(H):
                    lo = (w_ % 2) * D + hh * HD
                    i = mm(PB[0:97, w_ // 2, lo:lo + HD], u_fold[:, w_, hh, :], mqk if w_ == 0 else ident[0:HD, 0:HD])
            i.then_inc(setup_p, 1)
            pe.wait_ge(setup_v, V_UM)
            for w_, (dst, lo) in enumerate(((PC, 0), (PC, D), (PD, 0))):
                for c in range(C):
                    i = mm(dst[0:KC[c], c, lo:lo + D], v_fold[:, w_, c, 0:KC[c]], um[:, w_, :])
            i.then_inc(setup_p, 1)
            pe.wait_ge(setup_v, V_SETUP)
            pe.wait_ge(ld_l0, 128)
            pe.wait_ge(ld_tok, 208)
            pe.wait_ge(ld_ffn, 192)

            with pe.Fori(0, NG) as g:
                def w(name, n):
                    pe.wait_ge(s[name], g * PER[name] + n)

                def inc(ins, name):
                    ins.then_inc(s[name], 1)

                def both(o, l, r, rows=(CW, CW), extra=None):
                    mm(o, l(0)[0:rows[0]], r(0)[0:rows[0]], True, False)
                    return mm(o, l(1)[0:rows[1]], r(1)[0:rows[1]], False, True)

                w("gathered", 128)
                pe.wait_ge(s["out_row"], g * PER["out_row"])
                for b in range(G):
                    inc(tr(PA[0:WV, 0, tok(b)], wvg[:, b, :], 128), "wvT")
                for b in range(G):
                    w("gT", 1)
                    inc(mm(psl(PB, b, D), gT[:, b, :], w_g2b[:, :]), "g_ready")
                for b in range(G):
                    w("ln1", 11 + b + 1)
                    for c in range(C):
                        i = tr(part_of(PC, CW, b, c), x[:, b, c * CW:(c + 1) * CW], 128)
                    inc(i, "x1T")
                w("h_tok", 4)
                for b in range(G):
                    w("xT", b // 2 + 1)
                    if b >= 2:
                        w("vug", b - 1)
                        w("rope", 4 * (b - 2) + 3)
                    for k, (lo, hi) in enumerate(((0, 384), (384, 804))):
                        i = both(PS[b % 2][:, k, 0:hi - lo], lambda c: xT[:, c, tok(b)], lambda c: w_l0[:, c, lo:hi])
                    inc(i, "proj")
                for b in range(G):
                    w("vug", b + 1)
                    mm(psl(PD, b, D), con("le"), vug[:, b, D:2 * D], True, False)
                    inc(mm(psl(PD, b, D), con("ones")[0:1, :], taumu[:, :], False, True), "usum")
                w("sdot", 12)
                inc(mm(PD[0:G * H, 0, 0:128], es[:, 1, :, :].rearrange("p b h -> p (b h)"), ident), "sT")
                for b in range(G):
                    w("rope", 4 * b + 4)
                    if b == 0:
                        w("xT", 2)
                    elif b == 1:
                        w("rope", 16)
                        w("vug", 4)
                    else:
                        w("q_evac", b - 1)
                        w("k_evac", b - 1)
                    for k in range(2):
                        for j in range(3):
                            i = tr(PS[2 - b % 2][:, k, j * 128:(j + 1) * 128],
                                   rq[:, b, 12 * k + 4 * j:12 * k + 4 * j + 4, :].rearrange("p h d -> p (h d)"), 128)
                    inc(i, "qkT")
                w("s_exp", 1)
                inc(mm(PD[:, 0, 128:128 + G * H], eTs[:, :], ident[0:G * H, 0:G * H]), "eback")
                w("es_ready", 1)
                inc(mm(PD[:, 0, 192:288], con("le"), es[:, :, :, :].rearrange("p k b h -> p (k b h)")), "cum")

                def kq(b):
                    for hf in range(2):
                        if b:
                            w("A_masked", 2 * (b - 1) + hf + 1)
                        elif hf == 0:
                            w("q_evac", 4)
                            w("k_evac", 4)
                        for j in range(3):
                            for i_ in (2 * hf, 2 * hf + 1):
                                r = slice(32 * i_, 32 * i_ + HD)
                                i = mm(PS[hf][:, i_ % 2, j * 128:(j + 1) * 128], qkT[r, 1, b, j, :], qkT[r, 0, b, j, :])
                        inc(i, "A0")

                def av(b):
                    w("A_masked", 2 * b + 2)
                    w("vk", b + 1)
                    if b >= 2:
                        w("o3", 2 * (b - 2) + 2)
                    elif b == 1:
                        w("coef", 16)
                    for hh in range(H):
                        i = mm(PS[2 + b % 2][:, hh // HC, (hh % HC) * 48:(hh % HC) * 48 + 48],
                               am[:, b % 2, hh % 4, hh // 4, :], vk[:, b, hh, :])
                    inc(i, "pv")

                for b in range(G):
                    kq(b)
                    if b:
                        av(b - 1)
                av(G - 1)
                for b in range(G):
                    w("hln", 17 + b + 1)
                    for c in range(C):
                        i = tr(part_of(PA, CW, b, c), onrm[:, b, c * CW:(c + 1) * CW], 128)
                    inc(i, "onT")
                for b in range(G):
                    w("oT", b // 2 + 1)
                    inc(both(psl(PB, b, D), lambda c: nT[:, c, tok(b)], lambda c: w_l0o[:, c, :]), "wo")

                for b in range(G):
                    w("ln3", 11 + b + 1)
                    for c in range(C):
                        i = tr(part_of(PC, CW, b, c), xn[:, b, c * CW:(c + 1) * CW], 128)
                    inc(i, "n3T")
                w("score", 2)
                inc(mm(PD[:, 1, 0:G], con("ones"), zz[:, 3, :]), "ssum")
                for b in range(G):
                    w("dg", b + 1)
                    inc(mm(PD[:, 0, tok(b)], con("ones"), dg[:, b, :]), "bc")
                w("nT", 2)
                for c in range(C):
                    i = both(PC[0:CW, c, :], lambda k: w_fk[:, k, c * CW:(c + 1) * CW], lambda k: nT[:, k, :])
                inc(i, "kT")
                w("h_attn", 4)
                for b in range(G):
                    inc(both(psl(PB, b, D), lambda c: nT[:, c, tok(b)], lambda c: w_fv[:, c, :], KC), "v2p")
                w("wsel", 4)
                for b in range(G):
                    w("rank", 12 + b + 1)
                    lo = b * (KSEL + 1)
                    for c in range(C):
                        i = mm(PA[0:CW, c, lo:lo + KSEL + 1], xn[:, b, c * CW:(c + 1) * CW], pw[:, b, :])
                    inc(i, "sel")
                w("selT", 2)
                for c in range(C):
                    i = both(PD[0:CW, 1, 64 + c * 80:64 + c * 80 + G * KSEL], lambda k: w_fq[:, k, c * CW:(c + 1) * CW],
                             lambda k: sT[:, k, :, 0:KSEL])
                inc(i, "qT")
                w("pool_fix", 4)
                for b in range(G):
                    inc(tr(PA[0:KSEL, 0, tok(b)], pw[:, b, 0:KSEL], 128), "pselT_p")
                w("kT_evac", 2)
                w("qbd", 2)
                for b in range(G):
                    for c in range(C):
                        i = mm(part_of(PC, HC * KSEL, b, c), qbd[:, c, b, :], k2T[:, c, tok(b)])
                    inc(i, "lg")
                w("v2", 2)
                for b in range(G):
                    w("pnorm", 3 * b + 3)
                    for c in range(C):
                        i = tr(part_of(PB, 128, b, c, HC * KSEL), pr[:, b, c, :], HC * KSEL)
                    inc(i, "pT_p")
                w("pselT", 1)
                for b in range(G):
                    w("pT", b // 2 + 1)
                    for c in range(C):
                        i = mm(part_of(PA, CW, b, c, HC * KSEL), v2[:, b, c * CW:(c + 1) * CW], pT[:, c, b, :])
                    inc(i, "ctx")
                for b in range(G):
                    w("ctxT", b + 1)
                    inc(both(psl(PC, b, D)[0:KSEL, :], lambda c: ctxT[:, c, b, :], lambda c: w_fo[:, c, :], KC), "asel_p")
                for b in range(G):
                    w("asel", b // 2 + 1)
                    inc(mm(psl(PB, b, D), pselT[:, b, :], aselb[:, b, :]), "attn")
                w("mT_one", 1)
                for b in range(G):
                    w("mixT", 2 * b + 2)
                    inc(both(psl(PC, b, D), lambda c: mT[:, c, tok(b)], lambda c: w_fm[:, c, :], KC), "mix")
                for b in range(G):
                    w("ln4", 11 + b + 1)
                    for c in range(C):
                        i = tr(part_of(PA, CW, b, c), xn[:, b, c * CW:(c + 1) * CW], 128)
                    inc(i, "n4T")
                w("n2T", 2)
                for j in range(FJ):
                    inc(both(PS[1 + j // 2][:, j % 2, :], lambda k: w_up[:, k, j * 128:(j + 1) * 128], lambda k: nT[:, k, :]),
                        "up")
                for b in range(G):
                    w("gelu", FJ)
                    for j in range(FJ):
                        i = mm(psl(PA, b, D), hid[:, j, tok(b)], w_down[:, j, :], j == 0, j == FJ - 1)
                    inc(i, "down")

                for b in range(G):
                    w("ln5", 11 + b + 1)
                    for c in range(C):
                        i = tr(part_of(PB, CW, b, c), x[:, b, c * CW:(c + 1) * CW], 128)
                    inc(i, "x5T")
                w("x5T_e", 2)
                for n in range(6):
                    j, wt = n // 2, (w_1q, w_1k)[n % 2]
                    inc(both((PC, PD, PA)[j][:, n % 2, :],
                             lambda k: wt[:, k, 4 * j:4 * j + 4, :].rearrange("p h d -> p (h d)"),
                             lambda k: xT[:, k, :], KC), "qk1")
                for b in range(G):
                    inc(both(psl(PB, b, H * (HD + 1)), lambda c: xT[:, c, tok(b)],
                             lambda c: w_1v[:, c, :, :].rearrange("p h d -> p (h d)"), KC), "v1p")

                def logits(b):
                    for hf in range(2):
                        if b:
                            w("e1", 2 * (b - 1) + hf + 1)
                        elif hf == 0:
                            w("qk1_e", 6)
                        for j in range(3):
                            for i_ in (2 * hf, 2 * hf + 1):
                                r = slice(32 * i_, 32 * i_ + HD)
                                i = mm(PS[2 + hf][:, i_ % 2, j * 128:(j + 1) * 128], q1k1[r, 0, j, tok(b)],
                                       q1k1[r, 1, j, tok(b)])
                        inc(i, "lg1")

                def eT_(b):
                    w("e1", 2 * b + 1)
                    if b:
                        w("e1T_ev", b)
                    for k in range(H):
                        if k == 6:
                            w("e1", 2 * b + 2)
                        if k == 8:
                            if b:
                                w("e1T_e", b)
                            else:
                                w("v1", 2)
                        i = tr((PA, PB)[k // 8][:, (k % 8) // 4, (k % 4) * 128:(k % 4) * 128 + 128], e1[:, b % 2, k, :], 128)
                        if k in (7, 11):
                            inc(i, "e1T")

                def av1(b):
                    w("e1T_e", b + 1)
                    w("e1T_ev", b + 1)
                    if b:
                        w("h_l1", 3 * (b - 1) + 2)
                    for hh in range(H):
                        i = mm(PB[:, 1, hh * (HD + 1):(hh + 1) * (HD + 1)], eT[:, b % 2, (hh % 4) * 3 + hh // 4, :],
                               v1[:, b, hh * (HD + 1):(hh + 1) * (HD + 1)])
                    inc(i, "pv1")

                logits(0)
                for b in range(G):
                    if b + 1 < G:
                        logits(b + 1)
                    eT_(b)
                    if b:
                        av1(b - 1)
                av1(G - 1)

                for b in range(G):
                    w("ln6", 11 + b + 1)
                    for c in range(C):
                        i = tr(part_of(PA, CW, b, c), xn[:, b, c * CW:(c + 1) * CW], 128)
                    inc(i, "x6T")
                for b in range(G):
                    w("x6T_e", b // 2 + 1)
                    i = both(PB[:, 0, b * NE:(b + 1) * NE], lambda c: xT[:, c, tok(b)], lambda c: w_gate[:, c, :])
                inc(i, "gate")
                w("topw", 10)
                for b in range(G):
                    inc(tr(PB[0:NE, 1, tok(b)], gl[:, 0, b, :], 128), "gatesT_p")
                for b in range(G):
                    w("gatesT", 1)
                    inc(mm(psl(PC, b, D), gatT[:, b, :], w_b2[:, :]), "b2p")

            pe.wait_ge(route, R_OHS)
            pe.wait_ge(s["out_row"], NG * PER["out_row"])
            mm(PA[:, 0, 0:128], con("gt"), ohs.rearrange("p b e -> p (b e)"))
            mm(PA[:, 0, 128:256], con("ones"), ohs.rearrange("p b e -> p (b e)")).then_inc(route_p, 1)
            pe.wait_ge(route, R_DONE)
            pe.wait_ge(ld_w1, 16 * (NE + 2))

            def x_T(tile, u, slot_count):
                pe.wait_ge(slot_in[u], slot_count)
                pe.wait_ge(m_xTe, tile)
                for c in range(C):
                    i = tr(PD[0:CW, 0, c * 128:(c + 1) * 128], xs[:, u, c * CW:(c + 1) * CW], 128)
                i.then_inc(m_xT, 1)

            def up(tile, u, first=False):
                expert = pe.value_load(own_i[0:1, bass.ds(tile, 1)], min_val=0, max_val=NE - 1)
                pe.wait_ge(m_xTe, tile + 1)
                if not first:
                    pe.wait_ge(m_gelu, tile - 1)
                for hf in range(2):
                    for c in range(C):
                        i = mm(PS[u][:, hf, 0:384], xT[0:KC[c], c, tok(u)],
                               w_e1[0:KC[c], bass.ds(expert, 1), c, hf * 384:(hf + 1) * 384].rearrange("p a n -> p (a n)"),
                               c == 0, c == C - 1)
                i.then_inc(m_up, 1)

            def down(tile, u):
                pe.wait_ge(m_gelu, tile + 1)
                pe.wait_ge(m_hTe, tile)
                for j in range(FJ):
                    i = tr(PC[:, j // 3, (j % 3) * 128:(j % 3) * 128 + 128], hm_[:, u, j * 128:(j + 1) * 128], 128)
                i.then_inc(m_hT, 1)
                expert = pe.value_load(own_i[0:1, bass.ds(tile, 1)], min_val=0, max_val=NE - 1)
                pe.wait_ge(m_hTe, tile + 1)
                pe.wait_ge(m_y, tile)
                for j in range(FJ):
                    i = mm(PD[:, 1, 0:D], hTm[:, u, j, :],
                           w_e2[:, bass.ds(expert, 1), j, :].rearrange("p a n -> p (a n)"), j == 0, j == FJ - 1)
                i.then_inc(m_down, 1)

            x_T(0, 0, 16)
            up(0, 0, first=True)
            pe.wait_ge(ld_w2, 16 * NE)
            with pe.Fori(0, MT // 2) as r:
                for u in range(2):
                    x_T(r * 2 + (u + 1), 1 - u, r * 16 + 16 * (u + 1))
                    up(r * 2 + (u + 1), 1 - u)
                    down(r * 2 + u, u)
            down(MT - 1, 0)


def _constants():
    p = np.arange(128)[:, None]
    f = np.arange(128)[None, :]
    inv = (1.0 / 10000.0 ** (np.arange(0, HD, 2, dtype=np.float32) / np.float32(HD))).astype(np.float32)
    ang = np.arange(S, dtype=np.float32)[:, None] * inv[None, :]
    sin = np.repeat(np.sin(ang), 2, axis=-1)
    sin[:, 0:HD // 2] *= -1
    parts = dict(
        ident=p == f, le=p <= f, lt=f < p, gt=f > p, ones=np.ones((128, 128)), iota=np.tile(np.arange(KSEL), (128, 1)),
        iota8=np.tile(np.arange(NE), (128, 1)), hm=(p // HD == np.arange(HC)[None, :]),
        cos=np.repeat(np.cos(ang), 2, axis=-1), sin=sin, rt=np.float32(1) / (p + 1).astype(np.float32), t=p + 1,
        slot=np.tile(np.arange(MT), (128, 1)))
    return np.concatenate([np.asarray(parts[n], np.float32) for n in _C], axis=1)


def _layout(i):
    n = {k: np.asarray(v) for k, v in i.items()}

    def col(name, c=C):
        return n[name].reshape(c, -1).T

    d = {"consts": _constants()}
    d["ids"] = np.stack([n["x"].T, n["itok_BS_2_399970"].T], axis=1)
    d["tok_no"] = (np.arange(B)[None, :] * S + np.arange(S)[:, None]).astype(np.int32)
    t = "L0_tok_"
    d["word_emb"], d["wvec"], d["pos"], d["type"] = (n[t + k] for k in ("word_emb", "wvec", "pos_emb", "type_emb"))
    d["gamma"], d["beta"], d["gate_w"] = (n[t + k].reshape(D) for k in ("ln_gamma", "ln_beta", "gate_w"))
    d["gate_b"] = n[t + "gate_b"].reshape(1)
    d["g2b_w"] = n[t + "g2b_w"].T
    d["g2b_b"] = n[t + "g2b_b"].reshape(1, D)
    for k in ("Wq", "Wk", "Wv", "Wu", "Wg", "Wo"):
        d[k] = n["L0_attn_" + k].T
    d["log_tau"] = n["L0_attn_prior_log_tau"].reshape(H)
    d["mu"] = n["L0_attn_prior_mu"].reshape(1, D)
    f = "L0_ffn_"
    d["Wr"], d["bf2"], d["g1"], d["b1"] = (n[f + k] for k in ("Wr", "bf2", "g1", "b1"))
    d["br"] = n[f + "br"].reshape(1)
    d["cols"] = np.stack([col(f + k) for k in ("g1", "b1", "g2", "b2", "bq", "bk")], axis=1)
    d["bf1"] = col(f + "bf1", FJ)
    for k in ("Wq", "Wk", "Wv", "Wo", "Wm"):
        d["f" + k] = n[f + k]
    d["W1"], d["W2"] = n[f + "W1"], n[f + "W2"]
    for k in ("bv", "bo", "bm"):
        d[k] = n[f + k].reshape(1, D)
    l = "L1_attn_"
    d["M_UT"], d["M_V"] = n[l + "M_U"].T, n[l + "M_V"]
    u_fold = np.zeros((HD, 3, H, 97), np.float32)
    v_fold = np.zeros((97, 3, C, 97), np.float32)
    v_fold[96, :, 0, 96] = 1
    for w, k in enumerate("QKV"):
        u_fold[:, w, :, 0:96] = n[l + "U_" + k].reshape(96, H, HD).transpose(2, 1, 0)
        u_fold[:, w, :, 96] = n[l + "bias_" + k.lower()].reshape(H, HD).T
        v_fold[0:96, w, :, 0:96] = n[l + "V_" + k].reshape(C, CW, 96).transpose(2, 0, 1)
    d["U_fold"], d["V_fold"] = u_fold, v_fold
    e = "L1_ffn_"
    d["gate"] = n[e + "gate_w"].T
    d["w1"], d["eb1"], d["w2"], d["b2"] = (n[e + k] for k in ("w1", "b1", "w2", "b2"))
    return {k: np.ascontiguousarray(v) for k, v in d.items()}


def kernel(**inputs):
    import concourse.bacc as bacc
    from concourse.bass_utils import run_bass_kernel_spmd

    nc = bacc.Bacc("TRN2", target_bir_lowering=False, num_devices=1)
    arrays, aps = {}, {}
    for name, v in _layout(inputs).items():
        arrays[f"in_{name}"] = v
        aps[name] = nc.dram_tensor(f"in_{name}", v.shape, mybir.dt.from_np(v.dtype), kind="ExternalInput").ap()
    out = nc.dram_tensor("out_0", (B, S, D), F32, kind="ExternalOutput").ap()
    build(nc, aps, out)
    r = run_bass_kernel_spmd(nc, [arrays], core_ids=[0])
    return r.results[0]["out_0"]
```

```python
import numpy as np
import concourse.bass as bass
from concourse import mybir
from contextlib import ExitStack

F32 = mybir.dt.float32
I32 = mybir.dt.int32
U32 = mybir.dt.uint32
ALU = mybir.AluOpType
ACT = mybir.ActivationFunctionType
AX = mybir.AxisListType

B, S, D = 16, 128, 192
G = 4
NG = B // G
C, CW = 2, 96
H, HD = 12, 16
HC = H // C
WV = 75
F = 768
FJ = F // 128
KSEL = max(1, int(round(0.15 * S)))
NE = 8
XR = D + 2
MT = 2 * B * S // 128 + NE - 1
RING = 6
LATE = 2
NOBODY = 1 << 20

_C = {}
_n = 0
for _name, _w in (("ident", 128), ("le", 128), ("lt", 128), ("gt", 128), ("ones", 128), ("iota", KSEL),
                  ("iota8", NE), ("hm", HC), ("cos", HD), ("sin", HD), ("rt", 1), ("t", 1), ("slot", MT)):
    _C[_name] = (_n, _n + _w)
    _n += _w
NC_COLS = _n

RSTD = ("ln2", "ln3", "ln4", "ln5", "ln1", "ln6")


def rstd_of(name):
    return 1 + RSTD.index(name) + 1


AHEAD = 1
PER = dict(
    gathered=128, rstd=6, root0=1, roots=2, idx_cur=1, emb_sum=4, ln0=15, tok_scaled=4, tok_b=4, gate_dot=4,
    gate_exp=1, gate_a=2, wvT=4, gT=1, g_ready=4, g_diff=4, h_tok=4,
    ln1=15, x1T=4, xT=2, proj=4, rope=16, vug=4, qk_sq=4, norm2=6, qkT=4, q_evac=4, k_evac=4, usum=5, sdot=12,
    smax=2, s_exp=1, eback=1, es_ready=1, cum=1, gexp=1, coef=16, vk=4, A0=8, A_masked=8, pv=4, o3=8,
    o_sum=8, hln=22, onT=4, oT=2, wo=4, h_attn=4,
    ln2=15, ln3=7, zdot=4, zexp=1, score=2, n3T=4, nT=2, dg=4, bc=4, ssum=1, wsel=4, rank=16, nmask=1,
    sel=4, selT=2, pool_fix=4, qT=1, q_bias=2, qbd=2, kT=1, kT_evac=2, v2p=4, v2=2, pselT_p=4, pselT=1, lg=4, nmax=8,
    pexp=8, pnorm=12, pT_p=4, pT=2, ctx=4, ctx_m=4, ctxT=4, asel_p=4, asel=2, attn=4, mixT=8, mix=4, hin=8, hb=8,
    ln4=15, n4T=4, n2T=2, mT_one=1, up=6, gelu=6, down=4, h_ffn=4,
    ln5=15, x5T=4, x5T_e=2, qk1=6, qk1_e=6, v1p=4, v1=2, lg1=8, nm1=12, e1=8, e1T=8, e1T_e=4, e1T_ev=4, pv1=4, h_l1=12,
    ln6=15, x6T=4, x6T_e=2, gate=1, smx=5, gexp2=1, topk=10, topw=10, keep=3, gatesT_p=4, gatesT=1, b2p=4, out_row=4, base_out=64,
)


def build(nc, a, out):
    with ExitStack() as ctx:
        def sb(name, shape, dt=F32):
            return ctx.enter_context(nc.sbuf_tensor(name, shape, dt))

        def sem(name):
            return ctx.enter_context(nc.semaphore(name))

        s = {name: sem(name) for name in PER}
        ld_const, ld_tok, ld_l0, ld_ffn, ld_l1, ld_w1, ld_w2 = (
            sem(n) for n in ("ld_const", "ld_tok", "ld_l0", "ld_ffn", "ld_l1", "ld_w1", "ld_w2"))
        fills, setup_v, setup_p, setup_a, slots_empty = (
            sem(n) for n in ("fills", "setup_v", "setup_p", "setup_a", "slots_empty"))
        route, route_p, scattered, carried = (
            sem(n) for n in ("route", "route_p", "scattered", "carried"))
        slot_in = [sem(f"slot_in{u}") for u in range(RING)]
        m_xT, m_xTe, m_up, m_gelu, m_hT, m_hTe, m_down, m_y, m_add = (
            sem(n) for n in ("m_xT", "m_xTe", "m_up", "m_gelu", "m_hT", "m_hTe", "m_down", "m_y", "m_add"))

        slots = nc.dram_tensor("slots", [MT * 128, XR], F32, kind="Internal").ap()

        cst = sb("cst", [128, NC_COLS])

        def con(name, p=128):
            lo, hi = _C[name]
            return cst[0:p, lo:hi]

        ident = con("ident")
        idx_all = sb("idx_all", [128, 2, B + G], I32)
        idx_cur = sb("idx_cur", [128, 2, G], I32)
        tok_no = sb("tok_no", [128, B], I32)
        pos_type = sb("pos_type", [128, D])
        rows = sb("rows", [128, 5, D])
        gammar, betar, gatewr, wrr, bf2r = (rows[:, k, :] for k in range(5))
        cols = sb("cols", [CW, 6, C])
        g1c, b1c, g2c, b2c, bqc, bkc = (cols[:, k, :] for k in range(6))
        bf1c = sb("bf1c", [128, FJ])
        sc = sb("sc", [128, 8])
        w_g2b = sb("w_g2b", [97, D])
        w_l0 = sb("w_l0", [CW, C, 4 * D + 3 * H])
        w_l0o = sb("w_l0o", [CW, C, D])
        rtau = sb("rtau", [128, H])
        taumu = sb("taumu", [1, D])
        w_fq = sb("w_fq", [CW, C, D])
        w_fk = sb("w_fk", [CW, C, D])
        w_fv = sb("w_fv", [97, C, D])
        w_fm = sb("w_fm", [97, C, D])
        w_1q = sb("w_1q", [97, C, H, 32])
        w_1k = sb("w_1k", [97, C, H, 32])
        w_1v = sb("w_1v", [97, C, H, HD + 1])
        w_gate = sb("w_gate", [CW, C, NE])
        w_b2 = sb("w_b2", [NE, D])
        arena_e = sb("arena_e", [128, NE * C * F])
        w_e1 = arena_e[0:97, :].rearrange("p (e c n) -> p e c n", e=NE, c=C)
        arena_e7 = arena_e[:, (NE - LATE) * C * F:]
        w_up = arena_e7[0:CW, 0:C * F].rearrange("p (c n) -> p c n", c=C)
        w_down = arena_e7[:, C * F:C * F + FJ * D].rearrange("p (j n) -> p j n", j=FJ)
        w_fo = arena_e7[0:97, C * F + FJ * D:2 * C * F].rearrange("p (c n) -> p c n", c=C)
        arena_w = sb("arena_w", [128, NE * FJ * D])
        w_e2 = arena_w[:, :].rearrange("p (e j n) -> p e j n", e=NE, j=FJ)

        at = [0]

        def part(buf, at, shape, p=128):
            n = int(np.prod(shape))
            lo = at[0]
            at[0] += n
            flat = buf[0:p, lo:lo + n]
            if len(shape) == 1:
                return flat
            names = "abcd"[:len(shape)]
            return flat.rearrange(f"p ({' '.join(names)}) -> p {' '.join(names)}",
                                  **{names[k]: shape[k] for k in range(1, len(shape))})

        emb = part(arena_w, at, [G, D])
        wvg = part(arena_w, at, [G, WV])
        btok = part(arena_w, at, [G, D])
        vug_at = at[0]
        vug = part(arena_w, at, [G, 420])
        sq = part(arena_w, at, [G, 24, HD])
        over = [vug_at]
        qbd = part(arena_w, over, [C, G, HC * KSEL], CW)
        ctxm = part(arena_w, over, [C, G, HC * KSEL], CW)
        aselb = part(arena_w, over, [G, D], KSEL)
        pselT = part(arena_w, over, [G, 128], KSEL)
        assert over[0] <= at[0]
        e1_at = [at[0]]
        rq = part(arena_w, at, [G, 24, 32])
        e1 = part(arena_w, e1_at, [2, H, 128])
        dg = part(arena_w, at, [G, 128])
        assert at[0] <= NE * FJ * D

        qk_T = sb("qk_T", [128, 2 * G * 3 * 128])
        qkT = qk_T[:, :].rearrange("p (w b j t) -> p w b j t", w=2, b=G, j=3)
        q1k1 = qk_T[:, :].rearrange("p (w j t) -> p w j t", w=2, j=3)
        big = sb("big", [128, 2 * H * 128])
        am = big[:, :].rearrange("p (u i j t) -> p u i j t", u=2, i=4, j=3)
        hid = big[:, :].rearrange("p (j t) -> p j t", j=FJ)
        eT = big[:, :].rearrange("p (u h t) -> p u h t", u=2, h=H)
        arena_b = sb("arena_b", [128, 5000])
        bt = [0]
        vk = part(arena_b, bt, [G, H, 48])
        o3 = part(arena_b, bt, [2, H, 48])
        osum = part(arena_b, bt, [G, D])
        onrm = part(arena_b, bt, [G, D])
        assert bt[0] <= 5000
        ct = [0]
        mT = part(arena_b, ct, [C, G * 128], 97)
        k2T = part(arena_b, ct, [C, G * 128], CW)
        v2 = part(arena_b, ct, [G, D])
        pr = part(arena_b, ct, [G, C, 128], HC * KSEL)
        pT = part(arena_b, ct, [C, G, HC * KSEL])
        assert ct[0] <= 5000
        dt_ = [0]
        v1 = part(arena_b, dt_, [G, H * (HD + 1)])
        att = part(arena_b, dt_, [G, D])

        h = sb("h", [128, G, D])
        x = sb("x", [128, G, D])
        xn = sb("xn", [128, G, D])
        hb = sb("hb", [128, G, D])
        xT = sb("xT", [97, C, G * 128])
        nT = sb("nT", [97, C, G * 128])
        gT = sb("gT", [97, G, 128])
        st = sb("st", [128, G, 6])
        mv = sb("mv", [128, 6, G])
        rs = sb("rs", [128, 2, G])
        r0 = sb("r0", [128, 2, G])
        minus_half = sb("minus_half", [128, G])
        spare = sb("spare", [128, 1])
        first = sb("first", [128, 3])
        ga = sb("ga", [128, 3, G])
        nrm = sb("nrm", [128, G, 24])
        es = sb("es", [128, 2, G, H])
        smx = sb("smx", [G * H, 1])
        eTs = sb("eTs", [G * H, 128])
        eg = sb("eg", [128, G, H, 2])
        cf = sb("cf", [128, 4, G, H])
        cq = sb("cq", [128, G, H, 3])
        ck = sb("ck", [128, G, H, 3])
        hl = sb("hl", [128, 4, G, H])
        zz = sb("zz", [128, 4, G])
        pw = sb("pw", [128, G, KSEL + 1])
        rk = sb("rk", [128, 3, G])
        nmask = sb("nmask", [128, G])
        junk = hb
        sT = sb("selT", [CW, C, G, KSEL + 1])
        poolT = sb("poolT", [CW, C, G])
        ptmp = sb("ptmp", [CW, C, G])
        nx = sb("nx", [HC * KSEL, 3, G, C])
        ctxT = sb("ctxT", [97, C, G, KSEL])
        nm1 = sb("nm1", [128, G, H])
        r1 = sb("r1", [128, G, H])
        gl = sb("gl", [128, 5, G, NE])
        g1s = sb("g1s", [128, 4, G])
        m8 = sb("m8", [128, G, 8])
        i8 = sb("i8", [128, G, 8], U32)
        i8f = sb("i8f", [128, G, 2])
        gatT = sb("gatT", [NE, G, 128])
        qTs = sb("qTs", [CW, C, G, KSEL])
        tw = sb("tw", [128, G, 2])
        ohg = sb("ohg", [128, 2, G, NE])
        x_all = sb("x_all", [128, B, XR])
        w12 = sb("w12", [128, B, 2])
        oh = sb("oh", [128, 2, B, NE])

        PS = [ctx.enter_context(nc.psum_tensor(f"ps{k}", [128, 2, 512], F32)) for k in range(4)]
        PA, PB, PC, PD = PS


        mu_mv = part(big, [0], [2, 64], 64)
        su = [0]
        u_fold = part(arena_b, su, [H, 97], HD)
        v_fold = qk_T[0:97, 0:3 * C * 97].rearrange("p (w c m) -> p w c m", w=3, c=C)
        um = part(qk_T, [3 * C * 97], [3, D], 97)
        mqk = part(qk_T, [3 * C * 97 + 3 * D], [HD], HD)
        rowtmp = part(qk_T, [3 * C * 97 + 3 * D + HD], [2, D])
        typer = part(qk_T, [3 * C * 97 + 5 * D + HD], [D])
        tau = sb("tau", [128, 3, H])
        mu_row = sb("mu_row", [1, D])
        empty = x_all[:, B - 1, :]

        rt_at = [0]
        ohs = part(arena_b, rt_at, [B, NE])
        tot = part(arena_b, rt_at, [B, NE])
        before = part(arena_b, rt_at, [B, NE])
        pos = part(arena_b, rt_at, [B, NE])
        posk = part(arena_b, rt_at, [2, B, NE])
        posf = part(arena_b, rt_at, [2, B])
        cnt = part(arena_b, rt_at, [4, NE])
        owner = part(arena_b, rt_at, [MT, NE])
        ownf = part(arena_b, rt_at, [MT])
        pos_i = sb("pos_i", [128, 2, B], I32)
        cnt_i = sb("cnt_i", [128, 2, NE], I32)
        own_i = sb("own_i", [128, MT], I32)

        m_at = [0]
        xs = part(qk_T, m_at, [RING, XR])
        ym = part(qk_T, m_at, [RING, D])
        b_at = [0]
        hm_ = part(big, b_at, [2, F])
        hTm = part(big, b_at, [2, FJ, 128])

        block = ctx.enter_context(nc.Block())

        def psl(pair, b, n):
            return pair[:, b // 2, (b % 2) * n:(b % 2) * n + n]

        def part_of(pair, p, b, c, n=128):
            lo = ((b % 2) * C + c) * n
            return pair[0:p, b // 2, lo:lo + n]

        def half_of(pair, p, hf, n=128):
            return pair[0:p, hf, 0:2 * C * n].rearrange("p (b c t) -> p b c t", b=2, c=C)

        def chunks(t, hf):
            return t[0:CW, :, hf * 256:hf * 256 + 256].rearrange("p c (b t) -> p b c t", b=2)

        def half(b):
            return b // 2 * 2 + 2

        def tok(b):
            return slice(b * 128, b * 128 + 128)

        def bc(ap, axis, n):
            ap = ap.unsqueeze(axis)
            shape = list(ap.shape)
            shape[axis] = n
            return ap.to_broadcast(shape)

        KC = (97, 96)

        V_G2B, V_EMPTY, V_TAU = 1, 3, 15
        V_MQK, V_UM, V_FOLDED = 21, 22, 28
        V_SETUP = 32
        R_OHS, R_DONE = 1, 44

        def tiles(engine, do):
            for u in range(RING):
                do(u, u, 0)
            with engine.Fori(0, MT // RING - 1) as r:
                for u in range(RING):
                    do(r * RING + (u + RING), u, r + 1)
            for u in range(MT % RING):
                do(MT // RING * RING + u, u, MT // RING)

        def since(engine, semaphore, n):
            if not isinstance(n, int) or n > 0:
                engine.wait_ge(semaphore, n)

        def more(tile, k):
            return not isinstance(tile, int) or 0 <= tile + k < MT

        @block.sync
        def _(sp):
            def load(dst, src, sem):
                sp.dma_start(dst, src).then_inc(sem, 16)
            load(cst[:, :], a["consts"], ld_const)
            load(idx_all[:, :, 0:B], a["ids"], ld_const)
            load(tok_no[:, :], a["tok_no"], ld_const)
            load(pos_type[:, :], a["pos"][0:S, :], ld_tok)
            load(typer, a["type"][0:1, :].partition_broadcast(128), ld_tok)
            for k, n in enumerate(("gamma", "beta", "gate_w", "Wr", "bf2")):
                load(rows[:, k, :], a[n].partition_broadcast(128), ld_tok)
            load(rowtmp[:, 0, :], a["g1"].partition_broadcast(128), ld_tok)
            load(rowtmp[:, 1, :], a["b1"].partition_broadcast(128), ld_tok)
            load(sc[:, 0:1], a["gate_b"].partition_broadcast(128), ld_tok)
            load(sc[:, 1:2], a["br"].partition_broadcast(128), ld_tok)
            sp.wait_ge(setup_v, V_G2B)
            load(w_g2b[0:WV, :], a["g2b_w"], ld_tok)
            load(w_g2b[96:97, :], a["g2b_b"], ld_tok)
            lo = 0
            for n in ("Wq", "Wk", "Wv", "Wu", "Wg"):
                w = a[n].rearrange("(c p) n -> p c n", c=C)
                load(w_l0[:, :, lo:lo + w.shape[2]], w, ld_l0)
                lo += w.shape[2]
            load(w_l0o[:, :, :], a["Wo"].rearrange("(c p) n -> p c n", c=C), ld_l0)
            load(tau[:, 0, :], a["log_tau"].partition_broadcast(128), ld_l0)
            load(mu_row[:, :], a["mu"], ld_l0)
            load(mu_mv[0:64, 0, 0:HD], a["M_UT"], ld_l1)
            load(mu_mv[0:64, 1, 0:HD], a["M_V"], ld_l1)
            load(u_fold, a["U_fold"], ld_l1)
            load(um[:, 1:3, :], a["U_rows"], ld_l1)
            load(v_fold, a["V_fold"], ld_l1)
            load(w_gate[:, :, :], a["gate"].rearrange("(c p) n -> p c n", c=C), ld_l1)
            load(w_b2[:, :], a["b2"], ld_l1)
            load(cols[:, :, :], a["cols"], ld_ffn)
            load(bf1c[:, :], a["bf1"], ld_ffn)
            for dst, n in ((w_fq, "fWq"), (w_fk, "fWk"), (w_fv, "fWv"), (w_fo, "fWo"), (w_fm, "fWm"), (w_up, "W1")):
                load(dst[0:CW, :, :], a[n].rearrange("(c p) n -> p c n", c=C), ld_ffn)
            for dst, n in ((w_fv, "bv"), (w_fo, "bo"), (w_fm, "bm")):
                load(dst[96:97, 0, :], a[n], ld_ffn)
            load(w_down[:, :, :], a["W2"].rearrange("(j p) n -> p j n", j=FJ), ld_ffn)
            sp.wait_ge(setup_v, V_EMPTY)
            sp.dma_start(slots.rearrange("(n p) c -> p n c", p=128), bc(empty, 1, MT)).then_inc(slots_empty, 16)
            def load_w1(lo, hi):
                for e in range(lo, hi):
                    load(w_e1[0:CW, e, :, :], a["w1"][e].rearrange("(c p) n -> p c n", c=C), ld_w1)
                load(w_e1[96:97, lo:hi, 0, :], a["eb1"][lo:hi].unsqueeze(0), ld_w1)

            load_w1(0, NE - LATE)
            with sp.Fori(0, NG) as g:
                for b in range(G):
                    sp.wait_ge(s["out_row"], AHEAD + g * PER["out_row"] + b + 1)
                    sp.dma_start(out[bass.ds(g * G + b, 1)].rearrange("a p n -> (a p) n"), xn[:, b, :])\
                        .then_inc(s["base_out"], 16)
            sp.wait_ge(s["keep"], AHEAD + NG * PER["keep"])
            load_w1(NE - LATE, NE)
            sp.wait_ge(s["gathered"], (NG + 1) * PER["gathered"])
            for e in range(NE):
                load(w_e2[:, e, :, :], a["w2"][e].rearrange("(j p) n -> p j n", j=FJ), ld_w2)
            sp.wait_ge(scattered, 16 * 2 * B)

            def slot_load(tile, u):
                sp.dma_start(xs[:, u, :], slots[bass.ds(tile * 128, 128), :]).then_inc(slot_in[u], 16)

            for u in range(RING):
                slot_load(u, u)
            with sp.Fori(0, MT // RING - 1) as r:
                for u in range(RING):
                    sp.wait_ge(m_add, r * (16 * RING) + 16 * (u + 1))
                    slot_load(r * RING + (u + RING), u)
            for u in range(MT % RING):
                sp.wait_ge(m_add, 16 * (MT // RING * RING - RING + u + 1))
                slot_load(MT // RING * RING + u, u)
            sp.wait_ge(m_add, 16 * MT)

        @block.gpsimd
        def _(pool):
            def gather():
                for b in range(G):
                    for k, (dst, table) in enumerate(((emb, "word_emb"), (wvg, "wvec"))):
                        pool.indirect_dma_start(
                            out=dst[:, b, :], out_offset=None, in_=a[table],
                            in_offset=bass.IndirectOffsetOnAxis(ap=idx_cur[:, k, b:b + 1], axis=0),
                        ).then_inc(s["gathered"], 16)

            pool.memset(idx_all[:, :, B:B + G], 0).then_inc(fills, 1)
            pool.memset(minus_half[:, :], -0.5).then_inc(fills, 1)
            pool.wait_ge(ld_const, 48)
            pool.tensor_copy(idx_cur[:, :, :], idx_all[:, :, 0:G]).then_inc(fills, 1)
            pool.wait_ge(fills, 3)
            gather()

            def scale_token(base, tok_base):
                pool.wait_ge(s["ln0"], base + 11)
                pool.tensor_tensor(r0[:, 1, :], r0[:, 0, :], minus_half[:, :], ALU.pow).then_inc(s["root0"], 1)
                for b in range(G):
                    pool.wait_ge(s["ln0"], base + 11 + b + 1)
                    pool.tensor_tensor(btok[:, b, :], btok[:, b, :], gammar, ALU.mult).then_inc(s["tok_scaled"], 1)
                for b in range(G):
                    pool.wait_ge(s["tok_scaled"], tok_base + b + 1)
                    pool.tensor_tensor(btok[:, b, :], btok[:, b, :], betar, ALU.add).then_inc(s["tok_b"], 1)

            pool.wait_ge(ld_tok, 208)
            scale_token(0, 0)
            pool.wait_ge(s["ln1"], 11)
            pool.tensor_tensor(rs[:, 1, :], rs[:, 0, :], minus_half[:, :], ALU.pow).then_inc(s["rstd"], 1)
            with pool.Fori(0, NG) as g:
                def w(name, n):
                    pool.wait_ge(s[name], g * PER[name] + n)
                def ln_root(name, n=11):
                    w(name, n)
                    pool.tensor_tensor(rs[:, 1, :], rs[:, 0, :], minus_half[:, :], ALU.pow).then_inc(s["rstd"], 1)

                def carry():
                    pool.tensor_tensor(spare[:, :], minus_half[:, 0:1], minus_half[:, 0:1], ALU.add)

                pool.wait_ge(s["gathered"], g * PER["gathered"] + PER["gathered"])
                w("g_ready", 4)
                w("h_tok", 4)
                pool.tensor_copy(idx_cur[:, :, :], idx_all[:, :, bass.ds(g * G + G, G)]).then_inc(s["idx_cur"], 1)
                w("idx_cur", 1)
                carry()
                gather()
                w("coef", 16)
                for b in range(G):
                    w("vug", b + 1)
                    pool.tensor_tensor(vk[:, b, :, :].rearrange("p h (k d) -> p h k d", k=3),
                                       bc(vug[:, b, 0:D].rearrange("p (h d) -> p h d", h=H), 2, 3),
                                       bc(ck[:, b, :, :], 3, HD), ALU.mult).then_inc(s["vk"], 1)
                for b in range(G):
                    o = osum[:, b, :].rearrange("p (h d) -> p h d", h=H)
                    w("o3", 2 * b + 2)
                    pool.tensor_tensor(o, o3[:, b % 2, :, 0:HD], o3[:, b % 2, :, HD:2 * HD], ALU.add)\
                        .then_inc(s["o_sum"], 1)
                    w("o_sum", 2 * b + 1)
                    pool.tensor_tensor(o, o, o3[:, b % 2, :, 2 * HD:3 * HD], ALU.add).then_inc(s["o_sum"], 1)
                ln_root("ln2")
                ln_root("ln3", 3)
                scale_token(g * PER["ln0"] + PER["ln0"], g * G + G)
                ln_root("ln4")
                for b in range(G):
                    w("hin", 2 * b + 2)
                    pool.tensor_tensor(hb[:, b, :], h[:, b, :], x[:, b, :], ALU.add).then_inc(s["hb"], 1)
                    w("hb", 2 * b + 1)
                    pool.tensor_tensor(hb[:, b, :], hb[:, b, :], bf2r, ALU.add).then_inc(s["hb"], 1)
                ln_root("ln5")
                ln_root("ln1", PER["ln1"] + 11)
                ln_root("ln6")
                pool.wait_ge(slots_empty, 16)
                w("ln6", 15)
                pool.tensor_copy(x_all[:, bass.ds(g * G, G), 0:D], xn[:, :, :]).then_inc(s["keep"], 1)
                w("topw", 7)
                pool.tensor_copy(w12[:, bass.ds(g * G, G), :], tw[:, :, :]).then_inc(s["keep"], 1)
                pool.tensor_copy(oh[:, :, bass.ds(g * G, G), :], ohg[:, :, :, :]).then_inc(s["keep"], 1)
                w("out_row", AHEAD + 4)
            pool.wait_ge(s["gathered"], 128 * (NG + 1))
            pool.wait_ge(slots_empty, 16)
            for k in range(2):
                if k == 0:
                    pool.wait_ge(route, R_DONE)
                else:
                    pool.wait_ge(route, R_DONE + 1)
                for t in range(B):
                    pool.indirect_dma_start(
                        out=slots, out_offset=bass.IndirectOffsetOnAxis(ap=pos_i[:, k, t:t + 1], axis=0),
                        in_=x_all[:, t, :], in_offset=None).then_inc(scattered, 16)
            pool.wait_ge(s["base_out"], AHEAD + NG * PER["base_out"])
            rows_out = out.rearrange("b p n -> (b p) n")

            def add(tile, u, turn):
                pool.wait_ge(m_y, tile + 1)
                since(pool, carried, tile)
                since(pool, m_add, tile * 16)
                pool.tensor_tensor(spare[:, :], minus_half[:, 0:1], minus_half[:, 0:1], ALU.add).then_inc(carried, 1)
                pool.indirect_dma_start(
                    out=rows_out, out_offset=bass.IndirectOffsetOnAxis(ap=xs[:, u, D + 1:D + 2].bitcast(I32), axis=0),
                    in_=ym[:, u, :], in_offset=None, bounds_check=B * S - 1, oob_is_err=False,
                    compute_op=ALU.add).then_inc(m_add, 16)

            tiles(pool, add)
            pool.wait_ge(m_add, 16 * MT)

        @block.scalar
        def _(act):
            A = nc.scalar.activation
            act.wait_ge(setup_v, V_TAU)
            A(tau[:, 1, :], tau[:, 0, :], ACT.Exp).then_inc(setup_a, 1)

            def word_vectors(base):
                act.wait_ge(s["wvT"], base + 4)
                A(gT[0:WV, :, :], PA[0:WV, 0, :].rearrange("p (b t) -> p b t", b=G), ACT.Copy).then_inc(s["gT"], 1)

            def token_gate(base):
                act.wait_ge(s["gate_dot"], base + 4)
                A(ga[:, 0, :], zz[:, 0, :], ACT.Exp, bias=sc[:, 0:1], scale=-1.0).then_inc(s["gate_exp"], 1)

            word_vectors(0)
            act.wait_ge(setup_v, V_SETUP)
            token_gate(0)
            with act.Fori(0, NG) as g:
                def w(name, n):
                    act.wait_ge(s[name], g * PER[name] + n)

                def done(name):
                    return s[name], 1

                for hf in range(2):
                    w("x1T", 2 * hf + 2)
                    A(chunks(xT, hf), half_of(PD, CW, hf), ACT.Copy).then_inc(*done("xT"))
                for b in range(G):
                    w("proj", b + 1)
                    A(vug[:, b, :], PS[b % 2][:, 1, 0:420], ACT.Copy).then_inc(*done("vug"))
                for b in range(G):
                    w("rope", 4 * b + 4)
                    A(sq[:, b, :, :], rq[:, b, :, 0:HD], ACT.Square).then_inc(*done("qk_sq"))
                w("vug", 4)
                A(eg[:, :, :, :], vug[:, :, 384:420].rearrange("p b (h k) -> p b h k", k=3)[:, :, :, 0:2],
                  ACT.Exp, scale=-1.0).then_inc(*done("gexp"))
                w("norm2", 5)
                A(nrm[:, :, :], nrm[:, :, :], ACT.Sqrt).then_inc(*done("roots"))
                for b in range(G):
                    w("qkT", b + 1)
                    A(qkT[:, 0, b, :, :], PS[2 - b % 2][:, 0, 0:384].rearrange("p (j t) -> p j t", j=3), ACT.Copy)\
                        .then_inc(*done("q_evac"))
                    if b == 1:
                        w("smax", 2)
                        A(eTs[:, :], PD[0:G * H, 0, 0:128], ACT.Exp, bias=smx[:, 0:1]).then_inc(*done("s_exp"))
                w("hln", 17)
                A(hl[:, 2, :, :], hl[:, 3, :, :], ACT.Sqrt).then_inc(*done("roots"))
                for hf in range(2):
                    w("onT", 2 * hf + 2)
                    A(chunks(nT, hf), half_of(PA, CW, hf), ACT.Copy).then_inc(*done("oT"))
                w("zdot", 4)
                A(zz[:, 1, :], zz[:, 0, :], ACT.Exp, bias=sc[:, 3:4], scale=-1.0).then_inc(*done("zexp"))
                for hf in range(2):
                    w("n3T", 2 * hf + 2)
                    for c in range(C):
                        i = A(chunks(nT, hf)[:, :, c, :], half_of(PC, CW, hf)[:, :, c, :], ACT.Identity,
                              bias=b1c[:, c:c + 1], scale=g1c[:, c:c + 1])
                    i.then_inc(*done("nT"))
                for c in range(C):
                    w("kT", 1)
                    A(k2T[:, c, :], PC[0:CW, c, :], ACT.Identity, bias=bkc[:, c:c + 1]).then_inc(*done("kT_evac"))
                for hf in range(2):
                    w("v2p", 2 * hf + 2)
                    A(v2[:, 2 * hf:2 * hf + 2, :].rearrange("p b n -> p (b n)"), PB[:, hf, 0:2 * D], ACT.Copy).then_inc(*done("v2"))
                w("sel", 4)
                for c in range(C):
                    A(sT[:, c, :, :], PA[0:CW, c, 0:G * (KSEL + 1)].rearrange("p (b k) -> p b k", b=G), ACT.Identity,
                      bias=b1c[:, c:c + 1], scale=g1c[:, c:c + 1]).then_inc(*done("selT"))
                w("qT", 1)
                for c in range(C):
                    A(qTs[:, c, :, :], PD[0:CW, 1, 64 + c * 80:64 + c * 80 + G * KSEL].rearrange("p (b k) -> p b k", b=G),
                      ACT.Identity, bias=bqc[:, c:c + 1]).then_inc(*done("q_bias"))
                w("pselT_p", 4)
                A(pselT[:, :, :].rearrange("p b t -> p (b t)"), PA[0:KSEL, 0, :], ACT.Copy).then_inc(*done("pselT"))
                for b in range(G):
                    w("nmax", 2 * half(b))
                    for c in range(C):
                        A(pr[:, b, c, :], part_of(PC, HC * KSEL, b, c), ACT.Exp, bias=nx[:, 1, b, c:c + 1], scale=0.25,
                          accum_out=nx[:, 2, b, c:c + 1]).then_inc(*done("pexp"))
                for hf in range(2):
                    w("pT_p", 2 * hf + 2)
                    A(pT[:, :, 2 * hf:2 * hf + 2, :].rearrange("p c b k -> p b c k"), half_of(PB, 128, hf, HC * KSEL),
                      ACT.Copy).then_inc(*done("pT"))
                for hf in range(2):
                    w("asel_p", 2 * hf + 2)
                    A(aselb[:, 2 * hf:2 * hf + 2, :].rearrange("p b n -> p (b n)"), PC[0:KSEL, hf, 0:2 * D], ACT.Copy).then_inc(*done("asel"))
                word_vectors(g * G + G)
                for hf in range(2):
                    w("n4T", 2 * hf + 2)
                    for c in range(C):
                        i = A(chunks(nT, hf)[:, :, c, :], half_of(PA, CW, hf)[:, :, c, :], ACT.Identity,
                              bias=b2c[:, c:c + 1], scale=g2c[:, c:c + 1])
                    i.then_inc(*done("n2T"))
                for j in range(FJ):
                    w("up", j + 1)
                    A(hid[:, j, :], PS[1 + j // 2][:, j % 2, :], ACT.Gelu, bias=bf1c[:, j:j + 1]).then_inc(*done("gelu"))
                for hf in range(2):
                    w("x5T", 2 * hf + 2)
                    A(chunks(xT, hf), half_of(PB, CW, hf), ACT.Copy).then_inc(*done("x5T_e"))
                token_gate(g * G + G)
                for n in range(6):
                    w("qk1", n + 1)
                    A(q1k1[:, n % 2, n // 2, :], (PC, PD, PA)[n // 2][:, n % 2, :], ACT.Copy).then_inc(*done("qk1_e"))
                def exps(b):
                    w("nm1", 3 * b + 3)
                    if b >= 2:
                        w("e1T", 2 * (b - 2) + 2)
                    for k in range(H):
                        i, j = k // 3, k % 3
                        ins = A(e1[:, b % 2, k, :], (PC, PD)[i // 2][:, i % 2, j * 128:j * 128 + 128], ACT.Exp,
                                bias=nm1[:, b, k:k + 1], scale=0.25)
                        if k % 6 == 5:
                            ins.then_inc(*done("e1"))

                def eT_evac(b):
                    w("e1T", 2 * b + 2)
                    A(eT[:, b % 2, 8:12, :].rearrange("p h t -> p (h t)"), PB[:, 0, :], ACT.Copy).then_inc(*done("e1T_e"))

                for b in range(G):
                    exps(b)
                    if b == 0:
                        for hf in range(2):
                            w("v1p", 2 * hf + 2)
                            A(v1[:, 2 * hf:2 * hf + 2, :].rearrange("p b n -> p (b n)"), PB[:, hf, 0:2 * H * (HD + 1)], ACT.Copy).then_inc(*done("v1"))
                    if b:
                        eT_evac(b - 1)
                eT_evac(G - 1)
                for hf in range(2):
                    w("x6T", 2 * hf + 2)
                    A(chunks(xT, hf), half_of(PA, CW, hf), ACT.Copy).then_inc(*done("x6T_e"))
                w("smx", 2)
                A(gl[:, 1, :, :], gl[:, 0, :, :], ACT.Exp).then_inc(*done("gexp2"))
                w("gatesT_p", 4)
                A(gatT[:, :, :].rearrange("p b t -> p (b t)"), PB[0:NE, 1, :], ACT.Copy).then_inc(*done("gatesT"))

            def gelu(tile, u, turn):
                act.wait_ge(m_up, tile + 1)
                since(act, m_hT, tile - 1)
                A(hm_[:, u % 2, :].rearrange("p (c n) -> p c n", c=2), PS[u % 2][:, :, 0:384], ACT.Gelu).then_inc(m_gelu, 1)

            tiles(act, gelu)

        @block.vector
        def _(dve):
            T, TS, STT = nc.vector.tensor_tensor, nc.vector.tensor_scalar, nc.vector.scalar_tensor_tensor
            steps = [0]

            def step(ins):
                ins.then_inc(setup_v, 1)
                steps[0] += 1
                return steps[0]

            fill = nc.vector.memset

            def norm(name, src, dst, ready, eps, base, root, r_):
                def own(n):
                    dve.wait_ge(s[name], base + n)

                def inc(ins):
                    ins.then_inc(s[name], 1)

                for b in range(G):
                    dve.wait_ge(*ready(b))
                    nc.vector.bn_stats(st[:, b, :], src[:, b, :]).then_inc(s[name], 1)
                own(4)
                inc(T(mv[:, 0, :], st[:, :, 1], st[:, :, 4], ALU.add))
                inc(T(mv[:, 1, :], st[:, :, 1], st[:, :, 4], ALU.subtract))
                inc(T(mv[:, 2, :], st[:, :, 2], st[:, :, 5], ALU.add))
                own(5)
                inc(TS(mv[:, 3, :], mv[:, 0, :], 0.5, None, ALU.mult))
                own(6)
                inc(T(mv[:, 4, :], mv[:, 1, :], mv[:, 1, :], ALU.mult))
                own(9)
                inc(STT(mv[:, 5, :], mv[:, 4, :], D / 4.0, mv[:, 2, :], ALU.mult, ALU.add))
                own(10)
                inc(TS(r_[:, 0, :], mv[:, 5, :], 1.0 / D, eps, ALU.mult, ALU.add))
                dve.wait_ge(*root)
                for b in range(G):
                    TS(dst[:, b, :], src[:, b, :], mv[:, 3, b:b + 1], r_[:, 1, b:b + 1], ALU.subtract, ALU.mult)\
                        .then_inc(s[name], 1)

            def token_rows(turn):
                dve.wait_ge(s["gathered"], turn * 128 + 128)
                for b in range(G):
                    T(emb[:, b, :], emb[:, b, :], pos_type[:, :], ALU.add).then_inc(s["emb_sum"], 1)
                norm("ln0", emb, btok, lambda b: (s["emb_sum"], turn * G + b + 1), 1e-12, turn * PER["ln0"],
                     (s["root0"], turn + 1), r0)

            def token_dot(turn):
                for b in range(G):
                    dve.wait_ge(s["tok_b"], turn * G + b + 1)
                    nc.vector.tensor_tensor_reduce(
                        out=emb[:, b, :], in0=btok[:, b, :], in1=gatewr, scale=1.0, scalar=0.0, op0=ALU.mult,
                        op1=ALU.add, accum_out=zz[:, 0, b:b + 1]).then_inc(s["gate_dot"], 1)
                for b in range(G):
                    dve.wait_ge(s["g_ready"], turn * G + half(b))
                    dve.wait_ge(s["gate_dot"], turn * G + b + 1)
                    T(emb[:, b, :], psl(PD, b, D), btok[:, b, :], ALU.subtract).then_inc(s["g_diff"], 1)

            def token_mix(turn):
                dve.wait_ge(s["gate_exp"], turn + 1)
                TS(ga[:, 1, :], ga[:, 0, :], 1.0, None, ALU.add).then_inc(s["gate_a"], 1)
                dve.wait_ge(s["gate_a"], turn * 2 + 1)
                nc.vector.reciprocal(ga[:, 2, :], ga[:, 1, :]).then_inc(s["gate_a"], 1)
                dve.wait_ge(s["gate_a"], turn * 2 + 2)
                for b in range(G):
                    dve.wait_ge(s["g_diff"], turn * G + b + 1)
                    STT(btok[:, b, :], emb[:, b, :], ga[:, 2, b:b + 1], btok[:, b, :], ALU.mult, ALU.add)\
                        .then_inc(s["h_tok"], 1)

            for k, ahead in enumerate((s["out_row"], s["keep"], s["base_out"])):
                fill(first[:, k:k + 1], 0.0).then_inc(ahead, AHEAD)
            assert step(fill(w_g2b[64:96, :], 0.0)) == V_G2B
            n = step(fill(empty, 0.0))
            dve.wait_ge(setup_v, n)
            assert step(fill(empty[:, D + 1:D + 2].bitcast(I32), NOBODY)) == V_EMPTY
            n = step(fill(gT[64:96, :, :], 0.0))
            step(fill(gT[96:97, :, :], 1.0))
            step(fill(xT[96:97, :, :], 1.0))
            step(fill(nT[96:97, :, :], 1.0))
            step(fill(ctxT[96:97, :, :, :], 1.0))
            step(fill(rq[:, :, :, :], 0.0))
            step(fill(w_1q[:, :, :, :], 0.0))
            step(fill(w_1k[:, :, :, :], 0.0))
            n = step(fill(w_1v[:, :, :, :], 0.0))
            dve.wait_ge(setup_v, n)
            step(fill(w_1v[96:97, 0, :, HD:HD + 1], 1.0))
            dve.wait_ge(ld_l0, 128)
            n = step(TS(tau[:, 2, :], tau[:, 0, :], -50.0, 30.0, ALU.max, ALU.min))
            dve.wait_ge(setup_v, n)
            assert step(nc.vector.tensor_copy(tau[:, 0, :], tau[:, 2, :])) == V_TAU
            dve.wait_ge(ld_tok, 208)
            step(T(pos_type[:, :], pos_type[:, :], typer, ALU.add))
            step(nc.vector.tensor_tensor_reduce(out=junk[:, 0, :], in0=rowtmp[:, 1, :], in1=wrr, scale=1.0, scalar=0.0,
                                                op0=ALU.mult, op1=ALU.add, accum_out=sc[:, 2:3]))
            n = step(T(wrr, wrr, rowtmp[:, 0, :], ALU.mult))
            dve.wait_ge(setup_v, n)
            step(STT(sc[:, 3:4], sc[:, 2:3], -1.0, sc[:, 1:2], ALU.mult, ALU.subtract))
            step(TS(sc[:, 0:1], sc[:, 0:1], -1.0, None, ALU.mult))
            token_rows(0)
            dve.wait_ge(setup_p, 1)
            assert step(nc.vector.tensor_copy(mqk, PA[0:HD, 0, 0:HD])) == V_MQK
            dve.wait_ge(setup_p, 2)
            assert step(nc.vector.tensor_copy(um[:, 0, :], PB[0:97, 0, 0:D])) == V_UM
            dve.wait_ge(setup_p, 3)
            for w_, (dst, src, lo) in enumerate(((w_1q, PC, 0), (w_1k, PC, D), (w_1v, PD, 0))):
                for c in range(C):
                    n = step(nc.vector.tensor_copy(dst[0:KC[c], c, :, 0:HD],
                                                   src[0:KC[c], c, lo:lo + D].rearrange("p (h d) -> p h d", h=H)))
            assert n == V_FOLDED
            dve.wait_ge(setup_a, 1)
            n = step(TS(tau[:, 2, :], tau[:, 1, :], con("t"), None, ALU.add))
            dve.wait_ge(setup_v, n)
            n = step(nc.vector.reciprocal(tau[:, 0, :], tau[:, 2, :]))
            dve.wait_ge(setup_v, n)
            step(TS(rtau[:, :], tau[:, 0, :], -float(HD) ** -0.5, None, ALU.mult))
            n = step(T(taumu[0:1, :].rearrange("p (h d) -> p h d", h=H), mu_row[0:1, :].rearrange("p (h d) -> p h d", h=H),
                       bc(tau[0:1, 1, :], 2, HD), ALU.mult))
            assert n == V_SETUP
            dve.wait_ge(setup_v, n)


            def ln_1(turn, roots):
                norm("ln1", btok, x, lambda b: (s["h_tok"], turn * G + b + 1), 1e-5, turn * PER["ln1"],
                     (s["rstd"], roots), rs)

            token_dot(0)
            token_mix(0)
            ln_1(0, 1)

            with dve.Fori(0, NG) as g:
                def w(name, n):
                    dve.wait_ge(s[name], g * PER[name] + n)

                def inc(ins, name):
                    ins.then_inc(s[name], 1)

                def ln(name, src, dst, ready):
                    norm(name, src, dst, lambda b: (s[ready[0]], g * PER[ready[0]] + ready[1](b)), 1e-5, g * PER[name],
                         (s["rstd"], g * PER["rstd"] + rstd_of(name)), rs)

                for b in range(G):
                    w("proj", b + 1)
                    qk = PS[b % 2][:, 0, 0:384].rearrange("p (h d) -> p h d", d=HD)
                    hh = HD // 2
                    T(rq[:, b, :, 0:HD], qk, bc(con("cos"), 1, 24), ALU.mult).then_inc(s["rope"], 1)
                    T(sq[:, b, :, 0:hh], qk[:, :, hh:HD], bc(con("sin")[:, 0:hh], 1, 24), ALU.mult)\
                        .then_inc(s["rope"], 1)
                    T(sq[:, b, :, hh:HD], qk[:, :, 0:hh], bc(con("sin")[:, hh:HD], 1, 24), ALU.mult)\
                        .then_inc(s["rope"], 1)
                    w("rope", 4 * b + 3)
                    T(rq[:, b, :, 0:HD], rq[:, b, :, 0:HD], sq[:, b, :, :], ALU.add).then_inc(s["rope"], 1)
                for b in range(G):
                    w("usum", half(b))
                    T(osum[:, b, :], psl(PD, b, D), vug[:, b, D:2 * D], ALU.mult).then_inc(s["sdot"], 1)
                    w("sdot", 3 * b + 1)
                    nc.vector.reduce_sum(hl[:, 0, b, :], osum[:, b, :].rearrange("p (h d) -> p h d", h=H), AX.X)\
                        .then_inc(s["sdot"], 1)
                    w("sdot", 3 * b + 2)
                    T(es[:, 1, b, :], hl[:, 0, b, :], rtau[:, :], ALU.mult).then_inc(s["sdot"], 1)
                for b in range(G):
                    w("qk_sq", b + 1)
                    nc.vector.reduce_sum(nrm[:, b, :], sq[:, b, :, :], AX.X).then_inc(s["norm2"], 1)
                w("norm2", 4)
                TS(nrm[:, :, :], nrm[:, :, :], 1e-24, None, ALU.max).then_inc(s["norm2"], 1)
                w("usum", 5)
                nc.vector.reduce_max(smx[:, :], PD[0:G * H, 0, 0:128], AX.X).then_inc(s["smax"], 1)
                w("smax", 1)
                TS(smx[:, :], smx[:, :], -1.0, None, ALU.mult).then_inc(s["smax"], 1)
                for b in range(G):
                    w("qkT", b + 1)
                    nc.vector.tensor_copy(qkT[:, 1, b, :, :], PS[2 - b % 2][:, 1, 0:384].rearrange("p (j t) -> p j t", j=3))\
                        .then_inc(s["k_evac"], 1)
                w("eback", 1)
                nc.vector.tensor_copy(es[:, 0, :, :], PD[:, 0, 128:128 + G * H].rearrange("p (b h) -> p b h", b=G))\
                    .then_inc(s["es_ready"], 1)
                sig1, sigh = eg[:, :, :, 0], eg[:, :, :, 1]
                et = PD[:, 0, 192:240].rearrange("p (b h) -> p b h", b=G)
                pt = PD[:, 0, 240:288].rearrange("p (b h) -> p b h", b=G)
                al, be, gm = cf[:, 0, :, :], cf[:, 1, :, :], cf[:, 2, :, :]
                w("gexp", 1)
                inc(TS(eg[:, :, :, :], eg[:, :, :, :], 1.0, None, ALU.add), "coef")
                w("coef", 1)
                inc(nc.vector.reciprocal(eg[:, :, :, :], eg[:, :, :, :]), "coef")
                w("roots", 1)
                inc(nc.vector.reciprocal(nrm[:, :, :], nrm[:, :, :]), "norm2")
                w("norm2", 6)
                inc(nc.vector.tensor_copy(ck[:, :, :, 2], nrm[:, :, H:24]), "coef")
                w("es_ready", 1)
                inc(T(ck[:, :, :, 0], es[:, 0, :, :], nrm[:, :, H:24], ALU.mult), "coef")
                inc(T(ck[:, :, :, 1], es[:, 1, :, :], nrm[:, :, H:24], ALU.mult), "coef")
                w("coef", 2)
                inc(T(be, sig1, sigh, ALU.subtract), "coef")
                w("coef", 6)
                inc(TS(be, be, con("rt"), None, ALU.mult), "coef")
                w("cum", 1)
                inc(TS(al, et, 1e-12, None, ALU.add), "coef")
                w("coef", 8)
                inc(nc.vector.reciprocal(al, al), "coef")
                inc(T(gm, be, pt, ALU.mult), "coef")
                w("coef", 10)
                inc(T(al, al, sigh, ALU.mult), "coef")
                inc(T(gm, gm, sigh, ALU.add), "coef")
                w("coef", 12)
                inc(TS(gm, gm, con("rt"), -1.0, ALU.mult, ALU.mult), "coef")
                inc(T(cq[:, :, :, 0], al, nrm[:, :, 0:H], ALU.mult), "coef")
                inc(T(cq[:, :, :, 1], be, nrm[:, :, 0:H], ALU.mult), "coef")
                w("coef", 13)
                inc(T(cq[:, :, :, 2], gm, nrm[:, :, 0:H], ALU.mult), "coef")

                def mask(b):
                    if b >= 2:
                        w("pv", b - 1)
                    for hf in range(2):
                        w("A0", 2 * b + hf + 1)
                        T(am[:, b % 2, 2 * hf:2 * hf + 2, :, :],
                          PS[hf][:, :, 0:384].rearrange("p i (j t) -> p i j t", j=3),
                          bc(bc(con("le"), 1, 3), 1, 2), ALU.mult).then_inc(s["A_masked"], 1)

                def weigh(b):
                    w("pv", b + 1)
                    if b >= 2:
                        w("o_sum", 2 * (b - 2) + 2)
                    for c in range(C):
                        T(o3[:, b % 2, c * HC:(c + 1) * HC, :].rearrange("p h (k d) -> p (h k) d", k=3),
                          PS[2 + b % 2][:, c, 0:288].rearrange("p (x d) -> p x d", d=HD),
                          bc(cq[:, b, c * HC:(c + 1) * HC, :].rearrange("p h k -> p (h k)"), 2, HD), ALU.mult)\
                            .then_inc(s["o3"], 1)

                oh3 = [osum[:, b, :].rearrange("p (h d) -> p h d", h=H) for b in range(G)]
                on3 = [onrm[:, b, :].rearrange("p (h d) -> p h d", h=H) for b in range(G)]
                jk3 = [junk[:, b, :].rearrange("p (h d) -> p h d", h=H) for b in range(G)]

                def spread(b):
                    w("o_sum", 2 * b + 2)
                    nc.vector.reduce_sum(hl[:, 0, b, :], oh3[b], AX.X).then_inc(s["hln"], 1)
                    w("hln", 4 * b + 1)
                    STT(on3[b], bc(hl[:, 0, b, :], 2, HD), -1.0 / HD, oh3[b], ALU.mult, ALU.add).then_inc(s["hln"], 1)
                    w("hln", 4 * b + 2)
                    T(jk3[b], on3[b], on3[b], ALU.mult).then_inc(s["hln"], 1)
                    w("hln", 4 * b + 3)
                    nc.vector.reduce_sum(hl[:, 1, b, :], jk3[b], AX.X).then_inc(s["hln"], 1)

                mask(0)
                for b in range(1, G):
                    mask(b)
                    if b > 1:
                        spread(b - 2)
                    weigh(b - 1)
                spread(G - 2)
                weigh(G - 1)
                spread(G - 1)
                w("hln", 16)
                TS(hl[:, 3, :, :], hl[:, 1, :, :], HD * 1e-5, None, ALU.add).then_inc(s["hln"], 1)
                w("roots", 2)
                nc.vector.reciprocal(hl[:, 2, :, :], hl[:, 2, :, :]).then_inc(s["hln"], 1)
                w("hln", 18)
                for b in range(G):
                    STT(on3[b], on3[b], float(HD) ** 0.5, bc(hl[:, 2, b, :], 2, HD), ALU.mult, ALU.mult)\
                        .then_inc(s["hln"], 1)
                for b in range(G):
                    w("wo", half(b))
                    T(h[:, b, :], btok[:, b, :], psl(PB, b, D), ALU.add).then_inc(s["h_attn"], 1)

                ln("ln2", h, x, ("h_attn", lambda b: b + 1))
                dve.wait_ge(s["base_out"], AHEAD + g * PER["base_out"])
                w("ln2", 12)
                T(rs[:, 0, :], rs[:, 1, :], rs[:, 1, :], ALU.mult).then_inc(s["ln3"], 1)
                w("ln3", 1)
                T(g1s[:, 0, :], rs[:, 0, :], mv[:, 5, :], ALU.mult).then_inc(s["ln3"], 1)
                w("ln3", 2)
                TS(rs[:, 0, :], g1s[:, 0, :], 1.0 / D, 1e-5, ALU.mult, ALU.add).then_inc(s["ln3"], 1)
                w("rstd", rstd_of("ln3"))
                for b in range(G):
                    w("ln2", 11 + b + 1)
                    TS(xn[:, b, :], x[:, b, :], rs[:, 1, b:b + 1], None, ALU.mult).then_inc(s["ln3"], 1)
                for b in range(G):
                    w("ln3", 3 + b + 1)
                    nc.vector.tensor_tensor_reduce(
                        out=junk[:, b, :], in0=xn[:, b, :], in1=wrr, scale=1.0, scalar=0.0, op0=ALU.mult,
                        op1=ALU.add, accum_out=zz[:, 0, b:b + 1]).then_inc(s["zdot"], 1)
                fill(mT[96:97, :, :], 1.0).then_inc(s["mT_one"], 1)
                w("zexp", 1)
                TS(zz[:, 2, :], zz[:, 1, :], 1.0, None, ALU.add).then_inc(s["score"], 1)
                w("score", 1)
                nc.vector.reciprocal(zz[:, 3, :], zz[:, 2, :]).then_inc(s["score"], 1)
                w("score", 2)
                for b in range(G):
                    TS(dg[:, b, :], ident, zz[:, 3, b:b + 1], None, ALU.mult).then_inc(s["dg"], 1)
                w("ssum", 1)
                TS(ga[:, 0, :], PD[:, 1, 0:G], 1e-6, None, ALU.add).then_inc(s["wsel"], 1)
                w("wsel", 1)
                nc.vector.reciprocal(ga[:, 1, :], ga[:, 0, :]).then_inc(s["wsel"], 1)
                w("wsel", 2)
                T(pw[:, :, KSEL], zz[:, 3, :], ga[:, 1, :], ALU.mult).then_inc(s["wsel"], 1)
                T(ga[:, 2, :], PD[:, 1, 0:G], ga[:, 1, :], ALU.mult).then_inc(s["wsel"], 1)
                for b in range(G):
                    w("bc", 4)
                    STT(junk[:, b, 0:128], PD[:, 0, tok(b)], zz[:, 3, b:b + 1], con("gt"), ALU.is_lt, ALU.mult,
                        accum_out=rk[:, 0, b:b + 1]).then_inc(s["rank"], 1)
                for b in range(G):
                    STT(btok[:, b, 0:128], PD[:, 0, tok(b)], zz[:, 3, b:b + 1], con("lt"), ALU.is_le, ALU.mult,
                        accum_out=rk[:, 1, b:b + 1]).then_inc(s["rank"], 1)
                for b in range(G):
                    w("rank", 4 + b + 1)
                    T(rk[:, 2, b:b + 1], rk[:, 0, b:b + 1], rk[:, 1, b:b + 1], ALU.add).then_inc(s["rank"], 1)
                for b in range(G):
                    w("rank", 8 + b + 1)
                    TS(pw[:, b, 0:KSEL], con("iota"), rk[:, 2, b:b + 1], None, ALU.is_equal).then_inc(s["rank"], 1)
                TS(nmask[:, :], rk[:, 2, :], KSEL - 0.5, None, ALU.is_ge).then_inc(s["nmask"], 1)
                w("selT", 2)
                for c in range(C):
                    TS(ptmp[:, c, :], ga[0:CW, 2, :], b1c[:, c:c + 1], None, ALU.mult).then_inc(s["pool_fix"], 1)
                    w("pool_fix", 2 * c + 1)
                    STT(poolT[:, c, :], PA[0:CW, c, 0:G * (KSEL + 1)].rearrange("p (b k) -> p b k", b=G)[:, :, KSEL],
                        g1c[:, c:c + 1], ptmp[:, c, :], ALU.mult, ALU.add).then_inc(s["pool_fix"], 1)
                hmb = con("hm", CW)
                for c in range(C):
                    w("q_bias", c + 1)
                    T(qbd[:, c, :, :].rearrange("p b (h k) -> p b h k", h=HC), bc(qTs[:, c, :, :], 2, HC),
                      bc(bc(hmb, 2, KSEL), 1, G), ALU.mult).then_inc(s["qbd"], 1)
                for b in range(G):
                    w("lg", half(b))
                    nc.vector.reduce_max(nx[:, 0, b, :], half_of(PC, HC * KSEL, b // 2)[:, b % 2, :, :], AX.X).then_inc(s["nmax"], 1)
                    w("nmax", 2 * b + 1)
                    TS(nx[:, 1, b, :], nx[:, 0, b, :], -0.25, None, ALU.mult).then_inc(s["nmax"], 1)
                w("pool_fix", 4)
                for b in range(G):
                    w("nT", b // 2 + 1)
                    for c in range(C):
                        STT(mT[0:CW, c, tok(b)], PD[0:CW, 0, tok(b)], poolT[:, c, b:b + 1], nT[0:CW, c, tok(b)],
                            ALU.mult, ALU.add).then_inc(s["mixT"], 1)
                for b in range(G):
                    w("pexp", 2 * b + 2)
                    nc.vector.reciprocal(nx[:, 0, b, :], nx[:, 2, b, :]).then_inc(s["pnorm"], 1)
                    w("pnorm", 3 * b + 1)
                    for c in range(C):
                        TS(pr[:, b, c, :], pr[:, b, c, :], nx[:, 0, b, c:c + 1], None, ALU.mult)\
                            .then_inc(s["pnorm"], 1)
                token_rows(g + 1)
                for b in range(G):
                    w("ctx", half(b))
                    T(ctxm[:, :, b, :].rearrange("p c (h k) -> p c h k", h=HC),
                      half_of(PA, CW, b // 2, HC * KSEL)[:, b % 2, :, :].rearrange("p c (h k) -> p c h k", h=HC),
                      bc(bc(hmb, 2, KSEL), 1, C), ALU.mult).then_inc(s["ctx_m"], 1)
                    w("ctx_m", b + 1)
                    nc.vector.reduce_sum(ctxT[0:CW, :, b, :], ctxm[:, :, b, :].rearrange("p c (h k) -> p c k h", h=HC),
                                         AX.X).then_inc(s["ctxT"], 1)
                for b in range(G):
                    w("mix", half(b))
                    STT(x[:, b, :], psl(PD, b, D), nmask[:, b:b + 1], x[:, b, :], ALU.mult, ALU.add)\
                        .then_inc(s["hin"], 1)
                    w("attn", half(b))
                    w("hin", 2 * b + 1)
                    T(x[:, b, :], x[:, b, :], psl(PB, b, D), ALU.add).then_inc(s["hin"], 1)
                ln("ln4", x, xn, ("hin", lambda b: 2 * b + 2))
                token_dot(g + 1)
                for b in range(G):
                    w("down", half(b))
                    w("hb", 2 * b + 2)
                    T(h[:, b, :], hb[:, b, :], psl(PA, b, D), ALU.add).then_inc(s["h_ffn"], 1)

                ln("ln5", h, x, ("h_ffn", lambda b: b + 1))
                token_mix(g + 1)
                w("x5T", 4)
                ln_1(g + 1, g * PER["rstd"] + rstd_of("ln1"))

                def maxima(b):
                    for hf in range(2):
                        w("lg1", 2 * b + hf + 1)
                        nc.vector.reduce_max(nm1[:, b, 6 * hf:6 * hf + 6],
                                             PS[2 + hf][:, :, 0:384].rearrange("p i (j t) -> p i j t", j=3), AX.X)\
                            .then_inc(s["nm1"], 1)
                    w("nm1", 3 * b + 2)
                    TS(nm1[:, b, :], nm1[:, b, :], -0.25, None, ALU.mult).then_inc(s["nm1"], 1)

                def eT_evac(b):
                    w("e1T", 2 * b + 1)
                    if b >= 2:
                        w("pv1", b - 1)
                    nc.vector.tensor_copy(eT[:, b % 2, 0:8, :].rearrange("p (i j) t -> p i (j t)", i=2), PA[:, :, :])\
                        .then_inc(s["e1T_ev"], 1)

                def attend(b):
                    w("pv1", b + 1)
                    pv = PB[:, 1, 0:H * (HD + 1)].rearrange("p (h d) -> p h d", h=H)
                    r = r1[:, b, :]
                    at_ = att[:, b, :].rearrange("p (h d) -> p h d", h=H)
                    nc.vector.reciprocal(r, pv[:, :, HD]).then_inc(s["h_l1"], 1)
                    w("h_l1", 3 * b + 1)
                    T(at_, pv[:, :, 0:HD], bc(r, 2, HD), ALU.mult).then_inc(s["h_l1"], 1)
                    w("h_l1", 3 * b + 2)
                    T(h[:, b, :], h[:, b, :], att[:, b, :], ALU.add).then_inc(s["h_l1"], 1)

                maxima(0)
                for b in range(G):
                    if b + 1 < G:
                        maxima(b + 1)
                    eT_evac(b)
                    if b:
                        attend(b - 1)
                attend(G - 1)

                ln("ln6", h, xn, ("h_l1", lambda b: 3 * b + 3))
                w("gate", 1)
                lg = PB[:, 0, 0:G * NE].rearrange("p (b e) -> p b e", b=G)
                nc.vector.reduce_max(g1s[:, 0, :], lg, AX.X).then_inc(s["smx"], 1)
                w("smx", 1)
                T(gl[:, 0, :, :], lg, bc(g1s[:, 0, :], 2, NE), ALU.subtract).then_inc(s["smx"], 1)
                w("gexp2", 1)
                nc.vector.reduce_sum(g1s[:, 1, :], gl[:, 1, :, :], AX.X).then_inc(s["smx"], 1)
                w("smx", 3)
                nc.vector.reciprocal(g1s[:, 2, :], g1s[:, 1, :]).then_inc(s["smx"], 1)
                w("smx", 4)
                T(gl[:, 2, :, :], gl[:, 1, :, :], bc(g1s[:, 2, :], 2, NE), ALU.mult).then_inc(s["smx"], 1)
                w("smx", 5)
                inc(nc.vector.tensor_copy(g1s[:, 3, :], g1s[:, 2, :]), "topk")
                for b in range(G):
                    nc.vector.max(m8[:, b, :], gl[:, 2, b, :]).then_inc(s["topk"], 1)
                w("topk", 5)
                inc(nc.vector.tensor_copy(g1s[:, 3, :], g1s[:, 2, :]), "topk")
                for b in range(G):
                    nc.vector.max_index(i8[:, b, :], m8[:, b, :], gl[:, 2, b, :]).then_inc(s["topk"], 1)
                inc(T(g1s[:, 0, :], m8[:, :, 0], m8[:, :, 1], ALU.add), "topw")
                w("topk", 10)
                inc(nc.vector.tensor_copy(i8f[:, :, :], i8[:, :, 0:2]), "topw")
                w("topw", 1)
                inc(TS(g1s[:, 1, :], g1s[:, 0, :], 1e-9, None, ALU.add), "topw")
                w("topw", 2)
                io8 = bc(con("iota8"), 1, G)
                inc(T(ohg[:, 0, :, :], io8, bc(i8f[:, :, 0], 2, NE), ALU.is_equal), "topw")
                inc(T(ohg[:, 1, :, :], io8, bc(i8f[:, :, 1], 2, NE), ALU.is_equal), "topw")
                w("topw", 3)
                inc(nc.vector.reciprocal(g1s[:, 3, :], g1s[:, 1, :]), "topw")
                w("topw", 6)
                inc(T(tw[:, :, :], m8[:, :, 0:2], bc(g1s[:, 3, :], 2, 2), ALU.mult), "topw")
                w("topw", 7)
                inc(T(gl[:, 3, :, :], ohg[:, 0, :, :], bc(tw[:, :, 0], 2, NE), ALU.mult), "topw")
                inc(T(gl[:, 4, :, :], ohg[:, 1, :, :], bc(tw[:, :, 1], 2, NE), ALU.mult), "topw")
                w("topw", 9)
                inc(T(gl[:, 0, :, :], gl[:, 3, :, :], gl[:, 4, :, :], ALU.add), "topw")
                w("keep", AHEAD + 1)
                for b in range(G):
                    w("b2p", half(b))
                    T(xn[:, b, :], h[:, b, :], psl(PC, b, D), ALU.add).then_inc(s["out_row"], 1)

            done = [0]

            def r_step(ins):
                ins.then_inc(route, 1)
                done[0] += 1
                return done[0]

            def r_wait(n):
                dve.wait_ge(route, n)

            flat = "p b e -> p (b e)"
            dve.wait_ge(s["keep"], AHEAD + NG * PER["keep"])
            n = r_step(T(ohs, oh[:, 0, :, :], oh[:, 1, :, :], ALU.add))
            assert n == R_OHS
            r_step(nc.vector.tensor_copy(x_all[:, :, D], w12[:, :, 0]))
            r_step(nc.vector.tensor_copy(x_all[:, :, D + 1].bitcast(I32), tok_no[:, :]))
            r_step(fill(before[:, 0, :], 0.0))
            dve.wait_ge(route_p, 1)
            n = r_step(nc.vector.tensor_copy(tot.rearrange(flat), PA[:, 0, 128:256]))
            for t in range(1, B):
                r_wait(n)
                n = r_step(T(before[:, t, :], before[:, t - 1, :], tot[:, t - 1, :], ALU.add))
            r_wait(n)
            n = r_step(T(cnt[:, 0, :], before[:, B - 1, :], tot[:, B - 1, :], ALU.add))
            r_wait(n)
            n = r_step(TS(cnt_i[:, 0, :], cnt[:, 0, :], 127.0, None, ALU.add))
            r_wait(n)
            n = r_step(TS(cnt_i[:, 1, :], cnt_i[:, 0, :], 7, None, ALU.logical_shift_right))
            r_wait(n)
            n = r_step(nc.vector.tensor_copy(cnt[:, 1, :], cnt_i[:, 1, :]))
            r_wait(n)
            n = r_step(nc.vector.tensor_copy(cnt[:, 2, 0:1], cnt[:, 1, 0:1]))
            for e in range(1, NE):
                r_wait(n)
                n = r_step(T(cnt[:, 2, e:e + 1], cnt[:, 2, e - 1:e], cnt[:, 1, e:e + 1], ALU.add))
            r_wait(n)
            n = r_step(T(cnt[:, 3, :], cnt[:, 2, :], cnt[:, 1, :], ALU.subtract))
            k = r_step(T(owner, bc(con("slot"), 2, NE), bc(cnt[:, 2, :], 1, MT), ALU.is_ge))
            r_wait(n)
            n = r_step(TS(cnt[:, 3, :], cnt[:, 3, :], 128.0, None, ALU.mult))
            r_wait(k)
            k = r_step(nc.vector.reduce_sum(ownf, owner, AX.X))
            r_step(T(pos.rearrange(flat), before.rearrange(flat), PA[:, 0, 0:128], ALU.add))
            r_wait(k)
            r_step(TS(own_i[:, :], ownf, float(NE - 1), None, ALU.min))
            r_wait(n + 2)
            n = r_step(T(pos, pos, bc(cnt[:, 3, :], 1, B), ALU.add))
            r_wait(n)
            for k in range(2):
                n = r_step(T(posk[:, k, :, :], oh[:, k, :, :], pos, ALU.mult))
            r_wait(n)
            for k in range(2):
                n = r_step(nc.vector.reduce_sum(posf[:, k, :], posk[:, k, :, :], AX.X))
            r_wait(n)
            n = r_step(nc.vector.tensor_copy(pos_i[:, :, :], posf))
            assert n == R_DONE, n
            dve.wait_ge(scattered, 16 * B)
            nc.vector.tensor_copy(x_all[:, :, D], w12[:, :, 1]).then_inc(route, 1)

            def xT_evac(tile, u):
                dve.wait_ge(m_xT, tile + 1)
                since(dve, m_up, tile - 1)
                nc.vector.tensor_copy(xT[0:CW, :, tok(u % 2)], PD[0:CW, 0, 0:256].rearrange("p (c t) -> p c t", c=C))\
                    .then_inc(m_xTe, 1)

            def hT_evac(tile, u):
                dve.wait_ge(m_hT, tile + 1)
                since(dve, m_down, tile - 1)
                nc.vector.tensor_copy(hTm[:, u % 2, :, :].rearrange("p (c j) t -> p c j t", c=2),
                                      PC[:, :, 0:384].rearrange("p c (j t) -> p c j t", j=3)).then_inc(m_hTe, 1)

            def weight(tile, u):
                dve.wait_ge(m_down, tile + 1)
                since(dve, m_add, (tile - (RING - 1)) * 16)
                TS(ym[:, u, :], PD[:, 1, 0:D], xs[:, u, D:D + 1], None, ALU.mult).then_inc(m_y, 1)

            def evacuate(tile, u, turn):
                if more(tile, 2):
                    xT_evac(tile + 2, (u + 2) % RING)
                hT_evac(tile, u)
                if more(tile, -1):
                    weight(tile - 1, (u - 1) % RING)

            xT_evac(0, 0)
            xT_evac(1, 1)
            tiles(dve, evacuate)
            weight(MT - 1, (MT - 1) % RING)

        @block.tensor
        def _(pe):
            def mm(o, l, r, start=True, stop=True):
                return nc.tensor.matmul(o, l, r, start=start, stop=stop)

            def tr(o, i, k):
                return nc.tensor.transpose(o, i, ident[0:k, 0:k])

            pe.wait_ge(ld_const, 48)
            pe.wait_ge(ld_l1, 112)
            mm(PA[0:HD, 0, 0:HD], mu_mv[:, 0, 0:HD], mu_mv[:, 1, 0:HD]).then_inc(setup_p, 1)
            pe.wait_ge(setup_v, V_MQK)
            for hh in range(H):
                i = mm(PB[0:97, 0, hh * HD:(hh + 1) * HD], u_fold[:, hh, :], mqk)
            i.then_inc(setup_p, 1)
            pe.wait_ge(setup_v, V_UM)
            for w_, (dst, lo) in enumerate(((PC, 0), (PC, D), (PD, 0))):
                for c in range(C):
                    i = mm(dst[0:KC[c], c, lo:lo + D], v_fold[:, w_, c, 0:KC[c]], um[:, w_, :])
            i.then_inc(setup_p, 1)
            pe.wait_ge(setup_v, V_SETUP)
            pe.wait_ge(ld_l0, 128)
            pe.wait_ge(ld_tok, 208)
            pe.wait_ge(ld_ffn, 192)


            def word_vectors(turn, mixed=None):
                pe.wait_ge(s["gathered"], turn * 128 + 128)
                for b in range(G):
                    tr(PA[0:WV, 0, tok(b)], wvg[:, b, :], 128).then_inc(s["wvT"], 1)
                for b in range(G):
                    pe.wait_ge(s["gT"], turn + 1)
                    if mixed is not None:
                        pe.wait_ge(s["hin"], mixed)
                    mm(psl(PD, b, D), gT[:, b, :], w_g2b[:, :]).then_inc(s["g_ready"], 1)

            word_vectors(0)
            pe.wait_ge(s["g_diff"], 4)
            with pe.Fori(0, NG) as g:
                def w(name, n):
                    pe.wait_ge(s[name], g * PER[name] + n)

                def inc(ins, name):
                    ins.then_inc(s[name], 1)

                def both(o, l, r, rows=(CW, CW), extra=None):
                    mm(o, l(0)[0:rows[0]], r(0)[0:rows[0]], True, False)
                    return mm(o, l(1)[0:rows[1]], r(1)[0:rows[1]], False, True)

                for b in range(G):
                    w("ln1", 11 + b + 1)
                    for c in range(C):
                        i = tr(part_of(PD, CW, b, c), x[:, b, c * CW:(c + 1) * CW], 128)
                    inc(i, "x1T")
                for b in range(G):
                    w("xT", b // 2 + 1)
                    if b >= 2:
                        w("vug", b - 1)
                        w("rope", 4 * (b - 2) + 3)
                    for k, (lo, hi) in enumerate(((0, 384), (384, 804))):
                        i = both(PS[b % 2][:, k, 0:hi - lo], lambda c: xT[:, c, tok(b)], lambda c: w_l0[:, c, lo:hi])
                    inc(i, "proj")
                for b in range(G):
                    w("vug", b + 1)
                    mm(psl(PD, b, D), con("le"), vug[:, b, D:2 * D], True, False)
                    inc(mm(psl(PD, b, D), con("ones")[0:1, :], taumu[:, :], False, True), "usum")
                for b in range(G):
                    w("rope", 4 * b + 4)
                    if b == 0:
                        w("xT", 2)
                    elif b == 1:
                        w("rope", 16)
                        w("vug", 4)
                    else:
                        w("q_evac", b - 1)
                        w("k_evac", b - 1)
                    for k in range(2):
                        for j in range(3):
                            i = tr(PS[2 - b % 2][:, k, j * 128:(j + 1) * 128],
                                   rq[:, b, 12 * k + 4 * j:12 * k + 4 * j + 4, :].rearrange("p h d -> p (h d)"), 128)
                    inc(i, "qkT")
                    if b == 1:
                        w("sdot", 12)
                        inc(mm(PD[0:G * H, 0, 0:128], es[:, 1, :, :].rearrange("p b h -> p (b h)"), ident), "usum")
                w("s_exp", 1)
                inc(mm(PD[:, 0, 128:128 + G * H], eTs[:, :], ident[0:G * H, 0:G * H]), "eback")
                w("es_ready", 1)
                inc(mm(PD[:, 0, 192:288], con("le"), es[:, :, :, :].rearrange("p k b h -> p (k b h)")), "cum")

                def kq(b):
                    for hf in range(2):
                        if b:
                            w("A_masked", 2 * (b - 1) + hf + 1)
                        elif hf == 0:
                            w("q_evac", 4)
                            w("k_evac", 4)
                        for j in range(3):
                            for i_ in (2 * hf, 2 * hf + 1):
                                r = slice(32 * i_, 32 * i_ + HD)
                                i = mm(PS[hf][:, i_ % 2, j * 128:(j + 1) * 128], qkT[r, 1, b, j, :], qkT[r, 0, b, j, :])
                        inc(i, "A0")

                def av(b):
                    w("A_masked", 2 * b + 2)
                    w("vk", b + 1)
                    if b >= 2:
                        w("o3", 2 * (b - 2) + 2)
                    elif b == 1:
                        w("coef", 16)
                    for hh in range(H):
                        i = mm(PS[2 + b % 2][:, hh // HC, (hh % HC) * 48:(hh % HC) * 48 + 48],
                               am[:, b % 2, hh % 4, hh // 4, :], vk[:, b, hh, :])
                    inc(i, "pv")

                for b in range(G):
                    kq(b)
                    if b:
                        av(b - 1)
                av(G - 1)
                for b in range(G):
                    w("hln", 18 + b + 1)
                    for c in range(C):
                        i = tr(part_of(PA, CW, b, c), onrm[:, b, c * CW:(c + 1) * CW], 128)
                    inc(i, "onT")
                for b in range(G):
                    w("oT", b // 2 + 1)
                    inc(both(psl(PB, b, D), lambda c: nT[:, c, tok(b)], lambda c: w_l0o[:, c, :]), "wo")

                for b in range(G):
                    w("ln3", 3 + b + 1)
                    for c in range(C):
                        i = tr(part_of(PC, CW, b, c), xn[:, b, c * CW:(c + 1) * CW], 128)
                    inc(i, "n3T")
                w("score", 2)
                inc(mm(PD[:, 1, 0:G], con("ones"), zz[:, 3, :]), "ssum")
                for b in range(G):
                    w("dg", b + 1)
                    inc(mm(PD[:, 0, tok(b)], con("ones"), dg[:, b, :]), "bc")
                w("nT", 2)
                for c in range(C):
                    i = both(PC[0:CW, c, :], lambda k: w_fk[:, k, c * CW:(c + 1) * CW], lambda k: nT[:, k, :])
                inc(i, "kT")
                w("h_attn", 4)
                for b in range(G):
                    inc(both(psl(PB, b, D), lambda c: nT[:, c, tok(b)], lambda c: w_fv[:, c, :], KC), "v2p")
                w("wsel", 4)
                for b in range(G):
                    w("rank", 12 + b + 1)
                    lo = b * (KSEL + 1)
                    for c in range(C):
                        i = mm(PA[0:CW, c, lo:lo + KSEL + 1], xn[:, b, c * CW:(c + 1) * CW], pw[:, b, :])
                    inc(i, "sel")
                w("selT", 2)
                for c in range(C):
                    i = both(PD[0:CW, 1, 64 + c * 80:64 + c * 80 + G * KSEL], lambda k: w_fq[:, k, c * CW:(c + 1) * CW],
                             lambda k: sT[:, k, :, 0:KSEL])
                inc(i, "qT")
                w("pool_fix", 4)
                for b in range(G):
                    inc(tr(PA[0:KSEL, 0, tok(b)], pw[:, b, 0:KSEL], 128), "pselT_p")
                w("kT_evac", 2)
                w("qbd", 2)
                for b in range(G):
                    for c in range(C):
                        i = mm(part_of(PC, HC * KSEL, b, c), qbd[:, c, b, :], k2T[:, c, tok(b)])
                    inc(i, "lg")
                w("mT_one", 1)
                w("mixT", 8)
                for b in range(G):
                    inc(both(psl(PD, b, D), lambda c: mT[:, c, tok(b)], lambda c: w_fm[:, c, :], KC), "mix")
                w("v2", 2)
                for b in range(G):
                    w("pnorm", 3 * b + 3)
                    for c in range(C):
                        i = tr(part_of(PB, 128, b, c, HC * KSEL), pr[:, b, c, :], HC * KSEL)
                    inc(i, "pT_p")
                w("pselT", 1)
                for b in range(G):
                    w("pT", b // 2 + 1)
                    for c in range(C):
                        i = mm(part_of(PA, CW, b, c, HC * KSEL), v2[:, b, c * CW:(c + 1) * CW], pT[:, c, b, :])
                    inc(i, "ctx")
                for b in range(G):
                    w("ctxT", b + 1)
                    inc(both(psl(PC, b, D)[0:KSEL, :], lambda c: ctxT[:, c, b, :], lambda c: w_fo[:, c, :], KC), "asel_p")
                for b in range(G):
                    w("asel", b // 2 + 1)
                    inc(mm(psl(PB, b, D), pselT[:, b, :], aselb[:, b, :]), "attn")
                word_vectors(g + 1, g * PER["hin"] + 7)
                for b in range(G):
                    w("ln4", 11 + b + 1)
                    for c in range(C):
                        i = tr(part_of(PA, CW, b, c), xn[:, b, c * CW:(c + 1) * CW], 128)
                    inc(i, "n4T")
                w("n2T", 2)
                for j in range(FJ):
                    if j == 4:
                        pe.wait_ge(s["g_diff"], g * G + 2 * G)
                    inc(both(PS[1 + j // 2][:, j % 2, :], lambda k: w_up[:, k, j * 128:(j + 1) * 128], lambda k: nT[:, k, :]),
                        "up")
                for b in range(G):
                    w("gelu", FJ)
                    for j in range(FJ):
                        i = mm(psl(PA, b, D), hid[:, j, tok(b)], w_down[:, j, :], j == 0, j == FJ - 1)
                    inc(i, "down")

                for b in range(G):
                    w("ln5", 11 + b + 1)
                    for c in range(C):
                        i = tr(part_of(PB, CW, b, c), x[:, b, c * CW:(c + 1) * CW], 128)
                    inc(i, "x5T")
                w("x5T_e", 2)
                for n in range(6):
                    j, wt = n // 2, (w_1q, w_1k)[n % 2]
                    inc(both((PC, PD, PA)[j][:, n % 2, :],
                             lambda k: wt[:, k, 4 * j:4 * j + 4, :].rearrange("p h d -> p (h d)"),
                             lambda k: xT[:, k, :], KC), "qk1")
                def logits(b):
                    for hf in range(2):
                        if b:
                            w("e1", 2 * (b - 1) + hf + 1)
                        elif hf == 0:
                            w("qk1_e", 6)
                        for j in range(3):
                            for i_ in (2 * hf, 2 * hf + 1):
                                r = slice(32 * i_, 32 * i_ + HD)
                                i = mm(PS[2 + hf][:, i_ % 2, j * 128:(j + 1) * 128], q1k1[r, 0, j, tok(b)],
                                       q1k1[r, 1, j, tok(b)])
                        inc(i, "lg1")

                def eT_(b):
                    w("e1", 2 * b + 1)
                    if b:
                        w("e1T_ev", b)
                    for k in range(H):
                        if k == 6:
                            w("e1", 2 * b + 2)
                        if k == 8:
                            if b:
                                w("e1T_e", b)
                            else:
                                w("v1", 2)
                        i = tr((PA, PB)[k // 8][:, (k % 8) // 4, (k % 4) * 128:(k % 4) * 128 + 128], e1[:, b % 2, k, :], 128)
                        if k in (7, 11):
                            inc(i, "e1T")

                def av1(b):
                    w("e1T_e", b + 1)
                    w("e1T_ev", b + 1)
                    if b:
                        w("h_l1", 3 * (b - 1) + 2)
                    for hh in range(H):
                        i = mm(PB[:, 1, hh * (HD + 1):(hh + 1) * (HD + 1)], eT[:, b % 2, (hh % 4) * 3 + hh // 4, :],
                               v1[:, b, hh * (HD + 1):(hh + 1) * (HD + 1)])
                    inc(i, "pv1")

                logits(0)
                for b in range(G):
                    inc(both(psl(PB, b, H * (HD + 1)), lambda c: xT[:, c, tok(b)],
                             lambda c: w_1v[:, c, :, :].rearrange("p h d -> p (h d)"), KC), "v1p")
                for b in range(G):
                    if b + 1 < G:
                        logits(b + 1)
                    eT_(b)
                    if b:
                        av1(b - 1)
                av1(G - 1)

                for b in range(G):
                    w("ln6", 11 + b + 1)
                    for c in range(C):
                        i = tr(part_of(PA, CW, b, c), xn[:, b, c * CW:(c + 1) * CW], 128)
                    inc(i, "x6T")
                for b in range(G):
                    w("x6T_e", b // 2 + 1)
                    i = both(PB[:, 0, b * NE:(b + 1) * NE], lambda c: xT[:, c, tok(b)], lambda c: w_gate[:, c, :])
                inc(i, "gate")
                w("topw", 10)
                for b in range(G):
                    inc(tr(PB[0:NE, 1, tok(b)], gl[:, 0, b, :], 128), "gatesT_p")
                for b in range(G):
                    w("gatesT", 1)
                    inc(mm(psl(PC, b, D), gatT[:, b, :], w_b2[:, :]), "b2p")

            pe.wait_ge(route, R_OHS)
            pe.wait_ge(s["out_row"], AHEAD + NG * PER["out_row"])
            mm(PA[:, 0, 0:128], con("gt"), ohs.rearrange("p b e -> p (b e)"))
            mm(PA[:, 0, 128:256], con("ones"), ohs.rearrange("p b e -> p (b e)")).then_inc(route_p, 1)
            pe.wait_ge(route, R_DONE)
            pe.wait_ge(ld_w1, 16 * (NE + 2))

            def x_T(tile, u, loads):
                pe.wait_ge(slot_in[u], loads * 16)
                since(pe, m_xTe, tile)
                for c in range(C):
                    i = tr(PD[0:CW, 0, c * 128:(c + 1) * 128], xs[:, u, c * CW:(c + 1) * CW], 128)
                i.then_inc(m_xT, 1)

            def up(tile, u):
                expert = pe.value_load(own_i[0:1, bass.ds(tile, 1)], min_val=0, max_val=NE - 1)
                pe.wait_ge(m_xTe, tile + 1)
                since(pe, m_gelu, tile - 1)
                for hf in range(2):
                    for c in range(C):
                        i = mm(PS[u % 2][:, hf, 0:384], xT[0:KC[c], c, tok(u % 2)],
                               w_e1[0:KC[c], bass.ds(expert, 1), c, hf * 384:(hf + 1) * 384].rearrange("p a n -> p (a n)"),
                               c == 0, c == C - 1)
                i.then_inc(m_up, 1)

            def hidden_T(tile, u):
                pe.wait_ge(m_gelu, tile + 1)
                since(pe, m_hTe, tile)
                for j in range(FJ):
                    i = tr(PC[:, j // 3, (j % 3) * 128:(j % 3) * 128 + 128], hm_[:, u % 2, j * 128:(j + 1) * 128], 128)
                i.then_inc(m_hT, 1)

            def down(tile, u):
                expert = pe.value_load(own_i[0:1, bass.ds(tile, 1)], min_val=0, max_val=NE - 1)
                pe.wait_ge(m_hTe, tile + 1)
                since(pe, m_y, tile)
                for j in range(FJ):
                    i = mm(PD[:, 1, 0:D], hTm[:, u % 2, j, :],
                           w_e2[:, bass.ds(expert, 1), j, :].rearrange("p a n -> p (a n)"), j == 0, j == FJ - 1)
                i.then_inc(m_down, 1)

            def work(tile, u, turn):
                if more(tile, 1):
                    up(tile + 1, u + 1)
                if more(tile, 2):
                    x_T(tile + 2, (u + 2) % RING, turn + (u + 2) // RING + 1)
                hidden_T(tile, u)
                if more(tile, -1):
                    if isinstance(tile, int) and tile == 1:
                        pe.wait_ge(ld_w2, 16 * NE)
                    down(tile - 1, (u - 1) % RING)

            x_T(0, 0, 1)
            x_T(1, 1, 1)
            up(0, 0)
            tiles(pe, work)
            down(MT - 1, (MT - 1) % RING)


def _constants():
    p = np.arange(128)[:, None]
    f = np.arange(128)[None, :]
    inv = (1.0 / 10000.0 ** (np.arange(0, HD, 2, dtype=np.float32) / np.float32(HD))).astype(np.float32)
    ang = np.arange(S, dtype=np.float32)[:, None] * inv[None, :]
    sin = np.repeat(np.sin(ang), 2, axis=-1)
    sin[:, 0:HD // 2] *= -1
    parts = dict(
        ident=p == f, le=p <= f, lt=f < p, gt=f > p, ones=np.ones((128, 128)), iota=np.tile(np.arange(KSEL), (128, 1)),
        iota8=np.tile(np.arange(NE), (128, 1)), hm=(p // HD == np.arange(HC)[None, :]),
        cos=np.repeat(np.cos(ang), 2, axis=-1), sin=sin, rt=np.float32(1) / (p + 1).astype(np.float32), t=p + 1,
        slot=np.tile(np.arange(MT), (128, 1)))
    return np.concatenate([np.asarray(parts[n], np.float32) for n in _C], axis=1)


def _layout(i):
    n = {k: np.asarray(v) for k, v in i.items()}

    def col(name, c=C):
        return n[name].reshape(c, -1).T

    d = {"consts": _constants()}
    d["ids"] = np.stack([n["x"].T, n["itok_BS_2_399970"].T], axis=1)
    d["tok_no"] = (np.arange(B)[None, :] * S + np.arange(S)[:, None]).astype(np.int32)
    t = "L0_tok_"
    d["word_emb"], d["wvec"], d["pos"], d["type"] = (n[t + k] for k in ("word_emb", "wvec", "pos_emb", "type_emb"))
    d["gamma"], d["beta"], d["gate_w"] = (n[t + k].reshape(D) for k in ("ln_gamma", "ln_beta", "gate_w"))
    d["gate_b"] = n[t + "gate_b"].reshape(1)
    d["g2b_w"] = n[t + "g2b_w"].T
    d["g2b_b"] = n[t + "g2b_b"].reshape(1, D)
    for k in ("Wq", "Wk", "Wv", "Wu", "Wg", "Wo"):
        d[k] = n["L0_attn_" + k].T
    d["log_tau"] = n["L0_attn_prior_log_tau"].reshape(H)
    d["mu"] = n["L0_attn_prior_mu"].reshape(1, D)
    f = "L0_ffn_"
    d["Wr"], d["bf2"], d["g1"], d["b1"] = (n[f + k] for k in ("Wr", "bf2", "g1", "b1"))
    d["br"] = n[f + "br"].reshape(1)
    d["cols"] = np.stack([col(f + k) for k in ("g1", "b1", "g2", "b2", "bq", "bk")], axis=1)
    d["bf1"] = col(f + "bf1", FJ)
    for k in ("Wq", "Wk", "Wv", "Wo", "Wm"):
        d["f" + k] = n[f + k]
    d["W1"], d["W2"] = n[f + "W1"], n[f + "W2"]
    for k in ("bv", "bo", "bm"):
        d[k] = n[f + k].reshape(1, D)
    l = "L1_attn_"
    d["M_UT"], d["M_V"] = n[l + "M_U"].T, n[l + "M_V"]
    u = [np.concatenate([n[l + "U_" + k], n[l + "bias_" + k.lower()].reshape(1, D)]) for k in "QKV"]
    d["U_fold"] = u[0].reshape(97, H, HD).transpose(2, 1, 0)
    d["U_rows"] = np.stack(u[1:], axis=1)
    v_fold = np.zeros((97, 3, C, 97), np.float32)
    v_fold[96, :, 0, 96] = 1
    for w, k in enumerate("QKV"):
        v_fold[0:96, w, :, 0:96] = n[l + "V_" + k].reshape(C, CW, 96).transpose(2, 0, 1)
    d["V_fold"] = v_fold
    e = "L1_ffn_"
    d["gate"] = n[e + "gate_w"].T
    d["w1"], d["eb1"], d["w2"], d["b2"] = (n[e + k] for k in ("w1", "b1", "w2", "b2"))
    return {k: np.ascontiguousarray(v) for k, v in d.items()}


def kernel(**inputs):
    import concourse.bacc as bacc
    from concourse.bass_utils import run_bass_kernel_spmd

    nc = bacc.Bacc("TRN2", target_bir_lowering=False, num_devices=1)
    arrays, aps = {}, {}
    for name, v in _layout(inputs).items():
        arrays[f"in_{name}"] = v
        aps[name] = nc.dram_tensor(f"in_{name}", v.shape, mybir.dt.from_np(v.dtype), kind="ExternalInput").ap()
    out = nc.dram_tensor("out_0", (B, S, D), F32, kind="ExternalOutput").ap()
    build(nc, aps, out)
    r = run_bass_kernel_spmd(nc, [arrays], core_ids=[0])
    return r.results[0]["out_0"]
```
